# Optimizing a Trainium2 kernel written in Bass

```python
import numpy as np
import jax
import jax.numpy as jnp

def _softmax(x, axis=-1):
    return jax.nn.softmax(x, axis=axis)

def _gelu(x):
    return jax.nn.gelu(x, approximate=True)

def _silu(x):
    return jax.nn.silu(x)

def _sigmoid(x):
    return jax.nn.sigmoid(x)

def _layernorm(x, axis=-1, eps=1e-05):
    m = jnp.mean(x, axis=axis, keepdims=True)
    v = jnp.var(x, axis=axis, keepdims=True)
    return (x - m) / jnp.sqrt(v + eps)

def _scatter_add(tgt, idx, src, axis=0):
    return tgt.at[idx].add(src)

def _segment_sum(src, seg, n):
    return jax.ops.segment_sum(src, seg, n)
kernel_name = 'mk_lm_tower_d2_tok_ids256_r4_9b1fdd'

def setup_inputs(seed: int=0):
    np.random.seed(seed)
    _w = jnp.asarray

    def _rec_inputs():
        import jax
        import jax.numpy as jnp
        _rk = jax.random.key(seed)
        x = jax.random.randint(jax.random.fold_in(_rk, 1), (1, 2048), 0, 127998, jnp.int32)
        return x
    x = _rec_inputs()

    def _L0_tok_setup():
        import jax, jax.numpy as jnp
        import numpy as np
        VOCAB = 32000
        HIDDEN = 512
        BATCH, SEQ = (4, 1024)
        key = jax.random.key(seed)
        k_ids, k_tab = jax.random.split(key)
        input_ids = jax.random.randint(k_ids, (BATCH, SEQ), 0, VOCAB, dtype=jnp.int32)
        ple_table = jax.random.normal(k_tab, (VOCAB, HIDDEN), dtype=jnp.float32)
        return {'input_ids': input_ids, 'ple_table': ple_table, 'layer_idx': 3, 'ple_dim': 64}
    _L0_tok_all = _L0_tok_setup()
    _L0_tok_in = {k: v for k, v in _L0_tok_all.items() if k in ('ple_table',)}
    del _L0_tok_all

    def _L0_attn_setup():
        import jax, jax.numpy as jnp
        from jax import lax
        import numpy as np
        B, L, DIM = (4, 512, 64)
        D_STATE, D_CONV, EXPAND = (16, 4, 2)
        D_INNER = EXPAND * DIM
        DT_RANK = (DIM + 15) // 16
        LN_EPS = 1e-05

        def _layer_norm(x, g, b):
            mu = jnp.mean(x, axis=-1, keepdims=True)
            var = jnp.mean(jnp.square(x - mu), axis=-1, keepdims=True)
            return (x - mu) * lax.rsqrt(var + LN_EPS) * g + b

        def _mamba(x_norm, in_proj_w, conv_w, conv_b, x_proj_w, dt_proj_w, dt_proj_b, A_log, D, out_proj_w):
            xz = jnp.einsum('bld,ed->ble', x_norm, in_proj_w)
            x_in, z = (xz[..., :D_INNER], xz[..., D_INNER:])
            xc = jnp.transpose(x_in, (0, 2, 1))
            xc = lax.conv_general_dilated(xc, conv_w, (1,), [(D_CONV - 1, 0)], feature_group_count=D_INNER)
            xc = xc + conv_b[None, :, None]
            u = jax.nn.silu(jnp.transpose(xc, (0, 2, 1)))
            x_dbl = jnp.einsum('bld,ed->ble', u, x_proj_w)
            dt = x_dbl[..., :DT_RANK]
            Bm = x_dbl[..., DT_RANK:DT_RANK + D_STATE]
            Cm = x_dbl[..., DT_RANK + D_STATE:]
            delta = jax.nn.softplus(jnp.einsum('blr,dr->bld', dt, dt_proj_w) + dt_proj_b)
            A = -jnp.exp(A_log)

            def step(h, inp):
                d_t, B_t, C_t, u_t = inp
                dA = jnp.exp(d_t[:, :, None] * A)
                dBu = d_t[:, :, None] * B_t[:, None, :] * u_t[:, :, None]
                h = dA * h + dBu
                y_t = jnp.einsum('bds,bs->bd', h, C_t)
                return (h, y_t)
            xs = (jnp.swapaxes(delta, 0, 1), jnp.swapaxes(Bm, 0, 1), jnp.swapaxes(Cm, 0, 1), jnp.swapaxes(u, 0, 1))
            h0 = jnp.zeros((x_norm.shape[0], D_INNER, D_STATE), x_norm.dtype)
            _, ys = lax.scan(step, h0, xs)
            y = jnp.swapaxes(ys, 0, 1) + D * u
            y = y * jax.nn.silu(z)
            return jnp.einsum('bld,ed->ble', y, out_proj_w)
        key = jax.random.key(seed)
        ks = jax.random.split(key, 10)
        rn = lambda k, s, sc: jax.random.normal(k, s, jnp.float32) * sc
        return {'x': rn(ks[0], (B, L, DIM), 1.0), 'ln_gamma': jnp.ones((DIM,), jnp.float32), 'ln_beta': jnp.zeros((DIM,), jnp.float32), 'in_proj_w': rn(ks[1], (2 * D_INNER, DIM), DIM ** (-0.5)), 'conv_w': rn(ks[2], (D_INNER, 1, D_CONV), D_CONV ** (-0.5)), 'conv_b': jnp.zeros((D_INNER,), jnp.float32), 'x_proj_w': rn(ks[3], (DT_RANK + 2 * D_STATE, D_INNER), D_INNER ** (-0.5)), 'dt_proj_w': rn(ks[4], (D_INNER, DT_RANK), DT_RANK ** (-0.5)), 'dt_proj_b': jnp.full((D_INNER,), -4.0, jnp.float32), 'A_log': jnp.log(jnp.broadcast_to(jnp.arange(1, D_STATE + 1, dtype=jnp.float32), (D_INNER, D_STATE))), 'D': jnp.ones((D_INNER,), jnp.float32), 'out_proj_w': rn(ks[5], (DIM, D_INNER), D_INNER ** (-0.5)), 'gate_w': rn(ks[6], (DIM, DIM), DIM ** (-0.5)), 'gate_b': jnp.zeros((DIM,), jnp.float32)}
    _L0_attn_all = _L0_attn_setup()
    _L0_attn_in = {k: v for k, v in _L0_attn_all.items() if k in ('ln_gamma', 'ln_beta', 'in_proj_w', 'conv_w', 'conv_b', 'x_proj_w', 'dt_proj_w', 'dt_proj_b', 'A_log', 'D', 'out_proj_w', 'gate_w', 'gate_b')}
    del _L0_attn_all

    def _L0_ffn_setup():
        import jax, jax.numpy as jnp
        import numpy as np
        INPUT_WIDTH = 64
        DEPTH = 7
        OUTPUT_WIDTH = 64
        N_NODES = 2 ** (DEPTH + 1) - 1
        key = jax.random.key(seed)
        k_x, k_w1, k_w2 = jax.random.split(key, 3)
        init1 = 1.0 / np.sqrt(INPUT_WIDTH)
        x = jax.random.normal(k_x, (2, 256, INPUT_WIDTH), dtype=jnp.float32)
        w1s = jax.random.uniform(k_w1, (N_NODES, INPUT_WIDTH), jnp.float32, -init1, init1)
        b1s = jnp.zeros((N_NODES,), jnp.float32)
        w2s = jax.random.uniform(k_w2, (N_NODES, INPUT_WIDTH, OUTPUT_WIDTH), jnp.float32, -init1, init1)
        b2s = jnp.zeros((N_NODES, OUTPUT_WIDTH), jnp.float32)
        return {'x': x, 'w1s': w1s, 'b1s': b1s, 'w2s': w2s, 'b2s': b2s}
    _L0_ffn_all = _L0_ffn_setup()
    _L0_ffn_in = {k: v for k, v in _L0_ffn_all.items() if k in ('w1s', 'b1s', 'w2s', 'b2s')}
    del _L0_ffn_all

    def _L1_attn_setup():
        import jax, jax.numpy as jnp
        import numpy as np
        key = jax.random.key(seed)
        ks = jax.random.split(key, 5)
        b, t, e, h = (8, 256, 64, 8)
        w = lambda k, shape: jax.random.normal(k, shape, dtype=jnp.float32) * 0.02
        return {'x': jax.random.normal(ks[0], (b, t, e), dtype=jnp.float32), 'Wq': w(ks[1], (e, e * h)), 'bq': jnp.zeros((e * h,), jnp.float32), 'Wk': w(ks[2], (e, e * h)), 'bk': jnp.zeros((e * h,), jnp.float32), 'Wv': w(ks[3], (e, e * h)), 'bv': jnp.zeros((e * h,), jnp.float32), 'Wu': w(ks[4], (e * h, e)), 'bu': jnp.zeros((e,), jnp.float32)}
    _L1_attn_all = _L1_attn_setup()
    _L1_attn_in = {k: v for k, v in _L1_attn_all.items() if k in ('Wq', 'bq', 'Wk', 'bk', 'Wv', 'bv', 'Wu', 'bu')}
    del _L1_attn_all

    def _L1_ffn_setup():
        import jax, jax.numpy as jnp
        import numpy as np
        B, S, H, F, E, K = (8, 1024, 64, 128, 16, 2)
        EPS = 1e-05
        key = jax.random.key(seed)
        ks = jax.random.split(key, 9)
        sc = 0.02
        return {'x': jax.random.normal(ks[0], (B, S, H), dtype=jnp.float32), 'gate_w': jax.random.normal(ks[1], (H, E), dtype=jnp.float32) * sc, 'gate_b': jnp.zeros((E,), dtype=jnp.float32), 'w1': jax.random.normal(ks[2], (E, H, F), dtype=jnp.float32) * sc, 'b1': jnp.zeros((E, F), dtype=jnp.float32), 'w2': jax.random.normal(ks[3], (E, F, H), dtype=jnp.float32) * sc, 'b2': jnp.zeros((E, H), dtype=jnp.float32), 'gamma': jnp.ones((H,), dtype=jnp.float32), 'beta': jnp.zeros((H,), dtype=jnp.float32)}
    _L1_ffn_all = _L1_ffn_setup()
    _L1_ffn_in = {k: v for k, v in _L1_ffn_all.items() if k in ('gate_w', 'gate_b', 'w1', 'b1', 'w2', 'b2', 'gamma', 'beta')}
    del _L1_ffn_all
    return {'x': x, 'L0_tok_ple_table': _L0_tok_in['ple_table'], 'L0_attn_ln_gamma': _L0_attn_in['ln_gamma'], 'L0_attn_ln_beta': _L0_attn_in['ln_beta'], 'L0_attn_in_proj_w': _L0_attn_in['in_proj_w'], 'L0_attn_conv_w': _L0_attn_in['conv_w'], 'L0_attn_conv_b': _L0_attn_in['conv_b'], 'L0_attn_x_proj_w': _L0_attn_in['x_proj_w'], 'L0_attn_dt_proj_w': _L0_attn_in['dt_proj_w'], 'L0_attn_dt_proj_b': _L0_attn_in['dt_proj_b'], 'L0_attn_A_log': _L0_attn_in['A_log'], 'L0_attn_D': _L0_attn_in['D'], 'L0_attn_out_proj_w': _L0_attn_in['out_proj_w'], 'L0_attn_gate_w': _L0_attn_in['gate_w'], 'L0_attn_gate_b': _L0_attn_in['gate_b'], 'L0_ffn_w1s': _L0_ffn_in['w1s'], 'L0_ffn_b1s': _L0_ffn_in['b1s'], 'L0_ffn_w2s': _L0_ffn_in['w2s'], 'L0_ffn_b2s': _L0_ffn_in['b2s'], 'L1_attn_Wq': _L1_attn_in['Wq'], 'L1_attn_bq': _L1_attn_in['bq'], 'L1_attn_Wk': _L1_attn_in['Wk'], 'L1_attn_bk': _L1_attn_in['bk'], 'L1_attn_Wv': _L1_attn_in['Wv'], 'L1_attn_bv': _L1_attn_in['bv'], 'L1_attn_Wu': _L1_attn_in['Wu'], 'L1_attn_bu': _L1_attn_in['bu'], 'L1_ffn_gate_w': _L1_ffn_in['gate_w'], 'L1_ffn_gate_b': _L1_ffn_in['gate_b'], 'L1_ffn_w1': _L1_ffn_in['w1'], 'L1_ffn_b1': _L1_ffn_in['b1'], 'L1_ffn_w2': _L1_ffn_in['w2'], 'L1_ffn_b2': _L1_ffn_in['b2'], 'L1_ffn_gamma': _L1_ffn_in['gamma'], 'L1_ffn_beta': _L1_ffn_in['beta']}

def reference(x, L0_tok_ple_table, L0_attn_ln_gamma, L0_attn_ln_beta, L0_attn_in_proj_w, L0_attn_conv_w, L0_attn_conv_b, L0_attn_x_proj_w, L0_attn_dt_proj_w, L0_attn_dt_proj_b, L0_attn_A_log, L0_attn_D, L0_attn_out_proj_w, L0_attn_gate_w, L0_attn_gate_b, L0_ffn_w1s, L0_ffn_b1s, L0_ffn_w2s, L0_ffn_b2s, L1_attn_Wq, L1_attn_bq, L1_attn_Wk, L1_attn_bk, L1_attn_Wv, L1_attn_bv, L1_attn_Wu, L1_attn_bu, L1_ffn_gate_w, L1_ffn_gate_b, L1_ffn_w1, L1_ffn_b1, L1_ffn_w2, L1_ffn_b2, L1_ffn_gamma, L1_ffn_beta):
    import jax
    import jax.numpy as jnp

    def _L0_tok_ref(input_ids, ple_table, layer_idx, ple_dim):
        import jax, jax.numpy as jnp
        import numpy as np
        VOCAB = 32000
        HIDDEN = 512
        BATCH, SEQ = (4, 1024)
        start = layer_idx * ple_dim
        layer_slice = jax.lax.dynamic_slice_in_dim(ple_table, start, ple_dim, axis=1)
        return layer_slice[input_ids].astype(jnp.float32)

    def _L0_attn_ref(x, ln_gamma, ln_beta, in_proj_w, conv_w, conv_b, x_proj_w, dt_proj_w, dt_proj_b, A_log, D, out_proj_w, gate_w, gate_b):
        import jax, jax.numpy as jnp
        from jax import lax
        import numpy as np
        B, L, DIM = (4, 512, 64)
        D_STATE, D_CONV, EXPAND = (16, 4, 2)
        D_INNER = EXPAND * DIM
        DT_RANK = (DIM + 15) // 16
        LN_EPS = 1e-05

        def _layer_norm(x, g, b):
            mu = jnp.mean(x, axis=-1, keepdims=True)
            var = jnp.mean(jnp.square(x - mu), axis=-1, keepdims=True)
            return (x - mu) * lax.rsqrt(var + LN_EPS) * g + b

        def _mamba(x_norm, in_proj_w, conv_w, conv_b, x_proj_w, dt_proj_w, dt_proj_b, A_log, D, out_proj_w):
            xz = jnp.einsum('bld,ed->ble', x_norm, in_proj_w)
            x_in, z = (xz[..., :D_INNER], xz[..., D_INNER:])
            xc = jnp.transpose(x_in, (0, 2, 1))
            xc = lax.conv_general_dilated(xc, conv_w, (1,), [(D_CONV - 1, 0)], feature_group_count=D_INNER)
            xc = xc + conv_b[None, :, None]
            u = jax.nn.silu(jnp.transpose(xc, (0, 2, 1)))
            x_dbl = jnp.einsum('bld,ed->ble', u, x_proj_w)
            dt = x_dbl[..., :DT_RANK]
            Bm = x_dbl[..., DT_RANK:DT_RANK + D_STATE]
            Cm = x_dbl[..., DT_RANK + D_STATE:]
            delta = jax.nn.softplus(jnp.einsum('blr,dr->bld', dt, dt_proj_w) + dt_proj_b)
            A = -jnp.exp(A_log)

            def step(h, inp):
                d_t, B_t, C_t, u_t = inp
                dA = jnp.exp(d_t[:, :, None] * A)
                dBu = d_t[:, :, None] * B_t[:, None, :] * u_t[:, :, None]
                h = dA * h + dBu
                y_t = jnp.einsum('bds,bs->bd', h, C_t)
                return (h, y_t)
            xs = (jnp.swapaxes(delta, 0, 1), jnp.swapaxes(Bm, 0, 1), jnp.swapaxes(Cm, 0, 1), jnp.swapaxes(u, 0, 1))
            h0 = jnp.zeros((x_norm.shape[0], D_INNER, D_STATE), x_norm.dtype)
            _, ys = lax.scan(step, h0, xs)
            y = jnp.swapaxes(ys, 0, 1) + D * u
            y = y * jax.nn.silu(z)
            return jnp.einsum('bld,ed->ble', y, out_proj_w)
        x_norm = _layer_norm(x, ln_gamma, ln_beta)
        mamba_out = _mamba(x_norm, in_proj_w, conv_w, conv_b, x_proj_w, dt_proj_w, dt_proj_b, A_log, D, out_proj_w)
        gate = jax.nn.sigmoid(jnp.einsum('bld,ed->ble', x_norm, gate_w) + gate_b)
        return x + mamba_out * gate

    def _L0_ffn_ref(x, w1s, b1s, w2s, b2s):
        import jax, jax.numpy as jnp
        import numpy as np
        INPUT_WIDTH = 64
        DEPTH = 7
        OUTPUT_WIDTH = 64
        N_NODES = 2 ** (DEPTH + 1) - 1
        B, S, D = x.shape
        flat_x = x.reshape(B * S, D)
        T = flat_x.shape[0]
        current = jnp.zeros((T,), dtype=jnp.int32)
        all_nodes = []
        all_logits = []
        for _ in range(DEPTH + 1):
            all_nodes.append(current)
            score = jnp.einsum('td,td->t', flat_x, w1s[current]) + b1s[current]
            all_logits.append(score)
            choice = ((jnp.sign(score) + 1.0) / 2.0).astype(jnp.int32)
            current = current * 2 + choice + 1
        logits = jnp.stack(all_logits, axis=1)
        path_weights = jax.nn.gelu(jnp.abs(logits), approximate=False)
        out = jnp.zeros((T, OUTPUT_WIDTH), dtype=x.dtype)
        for i in range(DEPTH + 1):
            nodes_i = all_nodes[i]
            t_i = jnp.einsum('td,tdo->to', flat_x, w2s[nodes_i]) + b2s[nodes_i]
            out = out + t_i * path_weights[:, i][:, None]
        return out.reshape(B, S, OUTPUT_WIDTH)

    def _L1_attn_ref(x, Wq, bq, Wk, bk, Wv, bv, Wu, bu):
        import jax, jax.numpy as jnp
        import numpy as np
        b, t, e = x.shape
        h = Wq.shape[1] // e
        q = (x @ Wq + bq).reshape(b, t, h, e)
        k = (x @ Wk + bk).reshape(b, t, h, e)
        v = (x @ Wv + bv).reshape(b, t, h, e)
        scores = jnp.einsum('bihe,bjhe->bhij', q, k) / jnp.sqrt(jnp.asarray(e, jnp.float32))
        i = jnp.arange(t)[:, None]
        j = jnp.arange(t)[None, :]
        scores = jnp.where(j >= i, -jnp.inf, scores)
        scores = jnp.where(i == 0, 0.0, scores)
        att = jax.nn.softmax(scores, axis=-1)
        att = jnp.where(i == 0, 0.0, att)
        out = jnp.einsum('bhij,bjhe->bihe', att, v).reshape(b, t, h * e)
        return out @ Wu + bu

    def _L1_ffn_ref(x, gate_w, gate_b, w1, b1, w2, b2, gamma, beta):
        import jax, jax.numpy as jnp
        import numpy as np
        B, S, H, F, E, K = (8, 1024, 64, 128, 16, 2)
        EPS = 1e-05
        gate_logits = x @ gate_w + gate_b
        topk_vals, topk_idx = jax.lax.top_k(gate_logits, K)
        topk_w = jax.nn.softmax(topk_vals, axis=-1)
        h = jax.nn.relu(jnp.einsum('bsh,ehf->bsef', x, w1) + b1)
        expert_out = jnp.einsum('bsef,efh->bseh', h, w2) + b2
        sel = jnp.take_along_axis(expert_out, topk_idx[:, :, :, None], axis=2)
        moe = jnp.sum(topk_w[..., None] * sel, axis=2)
        y = x + moe
        mu = jnp.mean(y, axis=-1, keepdims=True)
        var = jnp.var(y, axis=-1, keepdims=True)
        return (y - mu) / jnp.sqrt(var + EPS) * gamma + beta
    h = _L0_tok_ref(x, L0_tok_ple_table, 3, 64)
    h = h + _L0_attn_ref(_layernorm(h, axis=-1), L0_attn_ln_gamma, L0_attn_ln_beta, L0_attn_in_proj_w, L0_attn_conv_w, L0_attn_conv_b, L0_attn_x_proj_w, L0_attn_dt_proj_w, L0_attn_dt_proj_b, L0_attn_A_log, L0_attn_D, L0_attn_out_proj_w, L0_attn_gate_w, L0_attn_gate_b)
    h = h + _L0_ffn_ref(_layernorm(h, axis=-1), L0_ffn_w1s, L0_ffn_b1s, L0_ffn_w2s, L0_ffn_b2s)
    h = h + _L1_attn_ref(_layernorm(h, axis=-1), L1_attn_Wq, L1_attn_bq, L1_attn_Wk, L1_attn_bk, L1_attn_Wv, L1_attn_bv, L1_attn_Wu, L1_attn_bu)
    h = h + _L1_ffn_ref(_layernorm(h, axis=-1), L1_ffn_gate_w, L1_ffn_gate_b, L1_ffn_w1, L1_ffn_b1, L1_ffn_w2, L1_ffn_b2, L1_ffn_gamma, L1_ffn_beta)
    return h

_drawn_inputs = setup_inputs


def setup_inputs(seed=0):
    import zlib

    import numpy as np

    out = dict(_drawn_inputs(seed))
    spreads = {'L0_attn_ln_gamma': (1.0, 0.2),
     'L0_attn_ln_beta': (0.0, 0.1),
     'L0_attn_conv_b': (0.0, 0.1),
     'L0_attn_dt_proj_b': (-4.0, 0.58),
     'L0_attn_D': (1.0, 0.2),
     'L0_attn_gate_b': (0.0, 0.496),
     'L0_ffn_b1s': (0.0, 0.1),
     'L0_ffn_b2s': (0.0, 0.1),
     'L1_attn_bq': (0.0, 2.0),
     'L1_attn_bk': (0.0, 2.0),
     'L1_attn_bv': (0.0, 0.389),
     'L1_attn_bu': (0.0, 0.1),
     'L1_ffn_gate_b': (0.0, 0.413),
     'L1_ffn_b1': (0.0, 0.8),
     'L1_ffn_b2': (0.0, 0.342),
     'L1_ffn_gamma': (1.0, 0.2),
     'L1_ffn_beta': (0.0, 0.1)}
    factors = {'L1_attn_Wq': 25.055,
     'L1_attn_Wk': 23.017,
     'L1_ffn_gate_w': 3.393,
     'L1_ffn_w1': 8.0,
     'L1_ffn_w2': 8.0}
    for name, (base, spread) in spreads.items():
        noise = np.random.default_rng([zlib.crc32(name.encode()), seed]).standard_normal(out[name].shape)
        drawn = base * np.exp(spread * noise) if base else spread * noise
        out[name] = jnp.asarray(drawn.astype(out[name].dtype))
    for name, factor in factors.items():
        out[name] = (out[name] * factor).astype(out[name].dtype)
    return out
```

```python
from contextlib import ExitStack

import concourse.bass as bass
from concourse import mybir

F32 = mybir.dt.float32
BF16 = mybir.dt.bfloat16
I32 = mybir.dt.int32
U32 = mybir.dt.uint32
ALU = mybir.AluOpType
ACT = mybir.ActivationFunctionType
AX_X = mybir.AxisListType.X

P = 128
SEED = 1
BANK = 512
NEG = -1.0e30


class Steps:

    def __init__(self, eng, sem):
        self.eng, self.sem, self.n = eng, sem, 0

    def did(self, ins):
        ins.then_inc(self.sem, 1)
        self.n += 1
        return self.n

    def after(self, n=None):
        self.eng.wait_ge(self.sem, self.n if n is None else n)


def tower_kernel(nc, a, out):
    T = a["x"].shape[1]
    V, HID = a["L0_tok_ple_table"].shape
    E = a["L0_attn_gate_w"].shape[0]
    LAYER = 3
    NT = T // P
    NCH = T // BANK
    TPC = BANK // P
    DI = a["L0_attn_D"].shape[0]
    DS = a["L0_attn_A_log"].shape[1]
    KC = a["L0_attn_conv_w"].shape[2]
    RK = a["L0_attn_dt_proj_w"].shape[1]
    NH = a["L1_attn_Wq"].shape[1] // E
    NP = NH // 2
    NE = a["L1_ffn_gate_w"].shape[1]
    FF = a["L1_ffn_w1"].shape[2]
    ND = a["L0_ffn_w1s"].shape[0]
    NDP = ND + 1
    DL = NDP.bit_length() - 1
    NG = NDP // 32
    EPS = 1e-5

    with ExitStack() as ctx:
        def sb(name, shape, dt=F32):
            return ctx.enter_context(nc.sbuf_tensor(name, shape, dt))

        def sem(name):
            return ctx.enter_context(nc.semaphore(name))

        ps = ctx.enter_context(nc.psum_tensor("ps", [P, 8, BANK], F32))
        arena = sb("arena", [P, 26 * 1024])
        taken = {"mamba": 0, "tree": 0, "attention": 0, "moe": 0}

        def part(stage, shape, dt=F32):
            n = 1
            for d in shape[1:]:
                n *= d
            words = n * mybir.dt.size(dt) // 4
            v = arena[0:shape[0], taken[stage]:taken[stage] + words]
            taken[stage] += words
            if dt != F32:
                v = v.bitcast(dt)
            if len(shape) == 2:
                return v
            names = "abcd"[:len(shape) - 1]
            return v.rearrange(f"p ({' '.join(names)}) -> p {' '.join(names)}", **dict(zip(names[1:], shape[2:])))

        ident = sb("ident", [P, P])
        nident = sb("nident", [P, P])
        identb = sb("identb", [P, P], BF16)
        mask_q = sb("mask_q", [P, P], BF16)
        mask_k = sb("mask_k", [P, P], BF16)
        sel = sb("sel", [96, 32, P], BF16)
        iota_e = sb("iota_e", [P, NE])

        h0 = sb("h0", [P, NT, E])
        h1 = sb("h1", [P, NT, E])
        h3 = sb("h3", [P, NT, E])
        cen = sb("cen", [P, NT, E])
        sq = sb("sq", [P, NT, E])
        xn = sb("xn", [P, NT, E])
        stat = sb("stat", [P, 8, NT])
        xt = sb("xt", [P, T])

        ids = sb("ids", [NT, P], I32)
        idr = sb("idr", [NT, P])
        idf = sb("idf", [P, 2, NT])
        rows = sb("rows", [P, NT], U32)

        win = sb("win", [P, 2, E])
        convw = sb("convw", [DI, KC])
        convb = sb("convb", [DI, 1])
        xpw = sb("xpw", [RK + 2 * DS, DI])
        dtw = sb("dtw", [DI, RK])
        dtb = sb("dtb", [DI, 1])
        alog = sb("alog", [DI, DS])
        neg_a = sb("neg_a", [DI, DS])
        dskip = sb("dskip", [DI, 1])
        outw = sb("outw", [E, DI])
        gatew = sb("gatew", [E, E])
        gateb = sb("gateb", [E, 1])
        gam = sb("gam", [E, 1])
        bet = sb("bet", [E, 1])
        wtap = sb("wtap", [DI, KC, E])
        wconv = sb("wconv", [P, 2, DI])
        wz = sb("wz", [P, DI])
        wg = sb("wg", [P, E])
        wbc = sb("wbc", [DI, 2 * DS])
        dtwT = sb("dtwT", [RK, DI])
        wdelta = sb("wdelta", [DI, DI])
        woT = sb("woT", [DI, E])
        x2 = part("mamba", [P, T + 8])
        u = part("mamba", [DI, T])
        sz = part("mamba", [DI, T])
        gsig = part("mamba", [E, T])
        delta = part("mamba", [DI, T])
        du = part("mamba", [DI, T])
        spl = part("mamba", [DI, 2, BANK])
        bc = sb("bc", [96, T], BF16)
        res1 = sb("res1", [32, BANK])
        mid = sb("mid", [32, BANK], BF16)
        res2 = sb("res2", [32, BANK])
        dA = part("mamba", [DI, 2, BANK])
        dbu = part("mamba", [DI, 2, BANK])
        hs = part("mamba", [DI, DS, BANK + 1])
        dcur = spl[:, 0, :]
        hc = part("mamba", [DI, 2, BANK])
        yb = part("mamba", [DI, 2, BANK])
        mo = part("mamba", [E, BANK])

        step_v = sem("vector_step")
        step_s = sem("scalar_step")
        step_g = sem("gpsimd_step")
        step_t = sem("tensor_step")
        s_ids = sem("ids_loaded")
        s_idr = sem("ids_as_floats")
        s_idt = sem("ids_turned")
        s_ident = sem("identity_ready")
        s_rows = sem("rows_ready")
        s_emb = sem("embeddings_loaded")
        s_const = sem("constants_ready")
        s_wm = sem("mamba_weights_loaded")
        s_wa = sem("attn_weights_loaded")
        s_we = sem("moe_weights_loaded")
        s_wtap = sem("taps_scaled")
        s_wps = sem("mamba_weights_turned")
        s_wsb = sem("mamba_weights_in_sbuf")
        s_wdp = sem("wdelta_product")
        s_wds = sem("wdelta_in_sbuf")
        s_var = sem("ln_variance")
        s_std = sem("ln_std")
        s_xn = sem("normalised_tokens")
        s_xtp = sem("turned_in_psum")
        s_xt = sem("turned_in_sbuf")
        s_wpad = sem("weight_pads_zeroed")
        s_pad = sem("mamba_pads_zeroed")
        s_apad = sem("attn_pads_set")
        s_in = sem("in_projected")
        s_u = sem("u_ready")
        s_zg = sem("z_gate_ready")
        s_bcp = sem("bc_projected")
        s_bch = sem("bc_parts")
        s_dlp = sem("delta_projected")
        s_abs = sem("delta_abs")
        s_ln1 = sem("delta_log")
        s_dl = sem("delta_ready")
        s_bb = sem("b_broadcast")
        s_cb = sem("c_broadcast")
        s_dcur = sem("chunk_delta_ready")
        s_da = sem("decay_ready")
        s_scan = sem("scan_done")
        s_dbu = sem("dbu_done")
        s_hc = sem("hc_ready")
        s_yac = sem("hc_accumulated")
        s_y = sem("y_gated")
        s_op = sem("out_projected")
        s_mo = sem("gated_out")
        s_mt = sem("out_turned")
        s_h1 = sem("h1_ready")

        w1n = part("tree", [P, 2, E])
        w1T = part("tree", [P, NDP])
        b2n = part("tree", [P, 2, E])
        w2n = part("tree", [P, NDP // 2, E])
        sel2 = part("tree", [96, 16, 2, E], BF16)
        ls = part("tree", [P, NT, DL])
        pw = part("tree", [P, NT, DL])
        pmT = part("tree", [P, 2, T])
        zz = part("tree", [P, 4, BANK])
        bcg = part("tree", [96, 2, T], BF16)
        tw0 = taken["tree"]
        sc = part("tree", [P, NT, NDP])
        taken["tree"] = tw0
        parts = part("tree", [P, 2, 3, T], BF16)
        taken["tree"] = tw0 + NT * NDP
        mk = part("tree", [P, NT, NDP])
        taken["tree"] = tw0 + 2 * 3 * T // 2
        rem = part("tree", [P, T])
        s_tpad = sem("tree_pads_zeroed")
        s_wt = sem("tree_weights_loaded")
        s_w2n = sem("tree_w2_loaded")
        s_w1p = sem("tree_w1_turned")
        s_w1T = sem("tree_w1_in_sbuf")
        s_sc = sem("tree_scores")
        s_sce = sem("tree_scores_in_sbuf")
        s_ls = sem("tree_path_scores")
        s_pw = sem("tree_path_weights")
        s_pm = sem("tree_node_weights")
        s_pmp = sem("tree_node_weights_turned")
        s_pmT = sem("tree_node_weights_in_sbuf")
        s_parts = sem("tree_parts")
        s_bg = sem("tree_group_loaded_even")
        s_bg1 = sem("tree_group_loaded_odd")
        s_zb = sem("tree_weight_broadcast")
        s_z = sem("tree_z_ready")
        s_zu = sem("tree_z_used")
        s_sum = sem("tree_summed")
        s_h2 = sem("h2_ready")
        s_xr = sem("xt_pads_restored")

        wqk = sb("wqk", [P, 2, NH * E])
        wv = sb("wv", [P, NH * E])
        wu = sb("wu", [E + 1, NH, E + 1])
        bub = sb("bub", [P, E])
        wpair = sb("wpair", [P, 2, P])
        wupair = sb("wupair", [E + 1, 2, E + 1])
        qa = part("attention", [P, 2, T])
        ka = part("attention", [P, 2, T])
        va = part("attention", [P, NT, 2, E + 1])
        mx = sb("mx", [P, 2, TPC, NCH])
        mx4 = sb("mx4", [P, 2, TPC])
        pt = part("attention", [P, 4, BANK])
        ot = sb("ot", [E + 1, BANK])
        rden = sb("rden", [P, 2, TPC])
        on = sb("on", [P, TPC, E])
        s_qs = sem("pair_weights_copied")
        s_qkp = sem("qk_projected")
        s_vp = sem("v_projected")
        s_qe = sem("q_in_sbuf")
        s_ke = sem("kv_in_sbuf")
        s_sm = sem("scores_for_max")
        s_mxd = sem("scores_max_taken")
        s_mx4 = sem("row_max_ready")
        s_mrp = sem("row_max_turned")
        s_mr = sem("row_max_in_q")
        s_st = sem("scores_turned")
        s_ex = sem("exp_done")
        s_av = sem("av_step")
        s_ot = sem("av_in_sbuf")
        s_pj = sem("head_projected")
        s_hd = sem("head_added")

        gw = sb("gw", [P, NE])
        w1 = sb("w1", [P, NE, FF])
        w2 = sb("w2", [FF, NE, E])
        b2 = sb("b2", [P, E])
        gamb = sb("gamb", [P, E])
        betb = sb("betb", [P, E])
        lg = sb("lg", [P, NT, NE])
        top = sb("top", [P, NT, 8])
        topi = sb("topi", [P, NT, 8], U32)
        topf = sb("topf", [P, NT, 2])
        tw = sb("tw", [P, 3, NT])
        ge = sb("ge", [P, NT, NE])
        ge2 = sb("ge2", [P, NT, NE])
        gT = part("moe", [P, T])
        hr = part("moe", [FF, 2, BANK])
        hg = part("moe", [FF, 2, BANK])
        yt = part("moe", [E, BANK])
        s_lg = sem("gate_logits")
        s_d = sem("top2_difference")
        s_e = sem("top2_exp")
        s_g = sem("gates_ready")
        s_gt = sem("gates_turned")
        s_gp = sem("gate_parts")
        s_m1 = sem("expert_up")
        s_gb = sem("gate_broadcast")
        s_rl = sem("expert_relu")
        s_hg = sem("expert_gated")
        s_m2 = sem("expert_down")
        s_mm = sem("moe_summed")
        s_yt = sem("moe_in_sbuf")
        s_ytp = sem("moe_turned")
        s_ya = sem("moe_added")
        s_fin = sem("result_ready")
        s_out = sem("result_stored")

        UNITS = [(h, ic) for ic in range(NCH) for h in range(2)]
        NSTEP = sum(4 * (ic + 1) for _, ic in UNITS)
        FIRST = [sum(4 * (ic + 1) for _, ic in UNITS[:n]) for n in range(len(UNITS) + 1)]

        block = ctx.enter_context(nc.Block())

        @block.sync
        def _(sp):
            def load(dst, src, s):
                sp.dma_start(dst, src).then_inc(s, 16)

            load(ids[:, :], a["x"].rearrange("b (c p) -> (b c) p", p=P), s_ids)
            col = lambda ap: ap.rearrange("(p o) -> p o", o=1)
            m = "L0_attn_"
            for dst, src in (
                (win[:, :, :], a[m + "in_proj_w"].rearrange("(k p) d -> p k d", p=P)),
                (convw[:, :], a[m + "conv_w"].rearrange("d o k -> d (o k)")),
                (convb[:, :], col(a[m + "conv_b"])), (xpw[:, :], a[m + "x_proj_w"]),
                (dtw[:, :], a[m + "dt_proj_w"]), (dtb[:, :], col(a[m + "dt_proj_b"])),
                (alog[:, :], a[m + "A_log"]), (dskip[:, :], col(a[m + "D"])),
                (outw[:, :], a[m + "out_proj_w"]), (gatew[:, :], a[m + "gate_w"]),
                (gateb[:, :], col(a[m + "gate_b"])),
                (gam[:, :], col(a[m + "ln_gamma"])), (bet[:, :], col(a[m + "ln_beta"])),
            ):
                load(dst, src, s_wm)
            sp.wait_ge(s_wpad, 1)
            row = lambda ap: ap.rearrange("(o n) -> o n", o=1)
            m = "L1_attn_"
            for dst, src in (
                (wqk[0:E, 0, :], a[m + "Wq"]), (wqk[0:E, 1, :], a[m + "Wk"]), (wv[0:E, :], a[m + "Wv"]),
                (wqk[E:E + 1, 0, :], row(a[m + "bq"])), (wqk[E:E + 1, 1, :], row(a[m + "bk"])),
                (wv[E:E + 1, :], row(a[m + "bv"])),
                (wu[0:E, :, 0:E], a[m + "Wu"].rearrange("(h e) n -> e h n", e=E)),
                (bub[:, :], a[m + "bu"].partition_broadcast(P)),
            ):
                load(dst, src, s_wa)
            m = "L1_ffn_"
            for dst, src in (
                (gw[0:E, :], a[m + "gate_w"]), (gw[E:E + 1, :], row(a[m + "gate_b"])),
                (w1[0:E, :, :], a[m + "w1"].rearrange("e d f -> d e f")),
                (w1[E:E + 1, :, :], a[m + "b1"].rearrange("(o e) f -> o e f", o=1)),
                (w2[:, :, :], a[m + "w2"].rearrange("e f d -> f e d")), (b2[0:NE, :], a[m + "b2"]),
                (gamb[:, :], a[m + "gamma"].partition_broadcast(P)),
                (betb[:, :], a[m + "beta"].partition_broadcast(P)),
            ):
                load(dst, src, s_we)
            sp.wait_ge(s_tpad, 1)
            m = "L0_ffn_"
            for dst, src in (
                (w1n[:, 0, :], a[m + "w1s"][0:P, :]), (w1n[0:ND - P, 1, :], a[m + "w1s"][P:ND, :]),
                (w1T[E:E + 1, 0:ND], row(a[m + "b1s"])),
                (b2n[:, 0, :], a[m + "b2s"][0:P, :]), (b2n[0:ND - P, 1, :], a[m + "b2s"][P:ND, :]),
            ):
                load(dst, src, s_wt)
            pairs = a[m + "w2s"][0:ND - 1].rearrange("(q h) d o -> h d q o", h=2)
            for q0 in range(0, NDP // 2, 32):
                q1 = min(q0 + 32, ND // 2)
                for h in range(2):
                    load(w2n[h * E:(h + 1) * E, q0:q1, :], pairs[h, :, q0:q1, :], s_w2n)
            load(w2n[0:E, ND // 2, :], a[m + "w2s"][ND - 1], s_w2n)
            sp.wait_ge(s_parts, 2)
            for g in range(NG):
                if g >= 2:
                    sp.wait_ge(s_zu, (g - 1) * 16 * NCH + SEED)
                r = 32 * (g % 4)
                for k in range(3):
                    load(bcg[32 * k:32 * k + 32, g % 2, :], parts[r:r + 32, g // 4, k, :], (s_bg, s_bg1)[g % 2])
            sp.wait_ge(s_fin, 1)
            sp.dma_start(out.rearrange("b (c p) d -> p (b c) d", p=P), xn[:, :, :]).then_inc(s_out, 16)
            sp.wait_ge(s_out, 16)

        N_WM, N_WA, N_WE, N_WT, N_W2 = 13 * 16, 8 * 16, 8 * 16, 5 * 16, 9 * 16

        @block.gpsimd
        def _(pool):
            st = Steps(pool, step_g)
            st.did(pool.memset(ident[:, :], 0.0))
            st.after()
            pool.affine_select(out=ident[:, :], in_=ident[:, :], compare_op=ALU.not_equal, fill=1.0,
                               base=0, pattern=[[-1, P]], channel_multiplier=1).then_inc(s_ident, 1)
            pool.wait_ge(s_ident, 1)
            for t in (wqk[E:P], wv[E:P], gw[E:P], w1[E:P], b2[:, :]):
                st.did(pool.memset(t, 0.0))
                st.after()
            st.after()
            st.did(pool.memset(wu[:, :, :], 0.0))
            st.after()
            st.did(pool.memset(wu[E:E + 1, :, E:E + 1], 1.0))
            st.after()
            pool.sem_inc(s_wpad, 1)
            for t in (identb, mask_q, mask_k, nident):
                st.did(pool.memset(t[:, :], 0.0))
            st.did(pool.memset(sel[:, :, :], 0.0))
            st.did(pool.iota(iota_e[:, :], [[1, NE]], base=0, channel_multiplier=0,
                             allow_small_or_imprecise_dtypes=True))
            pool.wait_ge(s_rows, 1)
            st.after()
            for c in range(NT):
                pool.indirect_dma_start(
                    out=h0[:, c, :], out_offset=None,
                    in_=a["L0_tok_ple_table"].rearrange("v (k e) -> (v k) e", e=E),
                    in_offset=bass.IndirectOffsetOnAxis(ap=rows[:, c:c + 1], axis=0),
                ).then_inc(s_emb, 16)
            for t, fill in ((identb, 1.0), (nident, -1.0)):
                st.did(pool.affine_select(out=t[:, :], in_=t[:, :], compare_op=ALU.not_equal, fill=fill,
                                          base=0, pattern=[[-1, P]], channel_multiplier=1))
            st.did(pool.affine_select(out=mask_q[:, :], in_=mask_q[:, :], compare_op=ALU.is_gt, fill=NEG,
                                      base=0, pattern=[[-1, P]], channel_multiplier=1))
            st.did(pool.affine_select(out=mask_k[:, :], in_=mask_k[:, :], compare_op=ALU.is_gt, fill=NEG,
                                      base=0, pattern=[[1, P]], channel_multiplier=-1))
            for part in range(3):
                st.after()
                st.did(pool.affine_select(out=sel[:, :, :], in_=sel[:, :, :], compare_op=ALU.not_equal,
                                          fill=1.0, base=-32 * part, pattern=[[-1, 32], [0, P]],
                                          channel_multiplier=1))
            st.after()
            pool.sem_inc(s_const, 1)
            pool.wait_ge(s_h1, 2 * NCH + SEED)
            for t in (w1T[:, :], b2n[:, :, :], w1n[:, 1, :], w2n[E:P, ND // 2, :]):
                st.did(pool.memset(t, 0.0))
                st.after()
            pool.sem_inc(s_tpad, 1)
            st.did(pool.memset(sel2[:, :, :, :], 0.0))
            for part in range(3):
                st.after()
                st.did(pool.affine_select(out=sel2[:, :, :, :], in_=sel2[:, :, :, :], compare_op=ALU.not_equal,
                                          fill=1.0, base=-32 * part, pattern=[[-2, 16], [-1, 2], [0, E]],
                                          channel_multiplier=1))
            st.after()
            pool.sem_inc(s_tpad, 1)
            pool.wait_ge(s_h2, 1)
            st.did(pool.memset(qa[E:P, :, :], 0.0))
            st.did(pool.memset(ka[E:P, :, :], 0.0))
            st.after()
            st.did(pool.memset(va[:, :, :, E:E + 1], 1.0))
            st.after()
            pool.memset(ka[E:E + 1, :, :], 1.0).then_inc(s_apad, 1)
            pool.wait_ge(s_apad, 1)
            pool.wait_ge(s_wa, N_WA)
            with pool.Fori(0, NP) as p:
                pool.wait_ge(s_hd, p * len(UNITS) + SEED)
                pool.tensor_copy(wpair[:, :, :], wqk[:, :, bass.ds(p * P, P)]).then_inc(s_qs, 1)
                pool.tensor_copy(wupair[:, :, :], wu[:, bass.ds(p * 2, 2), :]).then_inc(s_qs, 1)

        @block.tensor
        def _(pe):
            for s in (s_yac, s_op, s_mt, s_av, s_pj, s_zu, s_m2, s_ytp):
                pe.sem_inc(s, SEED)
            def turn_tokens(k):
                pe.wait_ge(s_xn, k + 1)
                for c in range(NT):
                    last = pe.transpose(ps[0:E, c // TPC, (c % TPC) * P:(c % TPC + 1) * P], xn[:, c, :], ident[:, :])
                    if c % TPC == TPC - 1:
                        last.then_inc(s_xtp, 1)

            pe.wait_ge(s_ident, 1)
            pe.wait_ge(s_idr, 1)
            pe.transpose(ps[:, 7, 0:NT], idr[:, :], ident[0:NT, 0:NT]).then_inc(s_idt, 1)
            pe.wait_ge(s_wm, N_WM)
            pe.wait_ge(s_wtap, 1)
            for k in range(2):
                pe.transpose(ps[:, 4, k * P:(k + 1) * P], wtap[:, 2 * k:2 * k + 2, :], ident[:, :])
            pe.transpose(ps[0:E, 4, 2 * P:3 * P], win[:, 1, :], ident[:, :])
            pe.transpose(ps[0:E, 4, 3 * P:3 * P + E], gatew[:, :], ident[0:E, 0:E])
            pe.transpose(ps[:, 5, 0:RK + 2 * DS], xpw[:, :], ident[0:RK + 2 * DS, 0:RK + 2 * DS])
            pe.transpose(ps[0:RK, 5, P:2 * P], dtw[:, :], ident[:, :])
            pe.transpose(ps[:, 5, 2 * P:2 * P + E], outw[:, :], ident[0:E, 0:E]).then_inc(s_wps, 1)
            pe.wait_ge(s_wsb, 1)
            pe.matmul(ps[:, 6, 0:DI], xpw[0:RK, :], dtwT[:, :], start=True, stop=True).then_inc(s_wdp, 1)

            turn_tokens(0)
            pe.wait_ge(s_wds, 1)
            for c in range(NCH):
                pe.wait_ge(s_xt, c + 1)
                if c == 0:
                    pe.wait_ge(s_pad, 1)
                if c >= 1:
                    pe.wait_ge(s_zg, c)
                b = 4
                for k in range(2):
                    pe.matmul(ps[:, b, :], wconv[:, k, :], x2[:, c * BANK + 3 - 2 * k:c * BANK + 3 - 2 * k + BANK],
                              start=(k == 0), stop=(k == 1))
                pe.matmul(ps[:, b + 1, :], wz[:, :], x2[:, c * BANK + 3:c * BANK + 3 + BANK], start=True, stop=True)
                pe.matmul(ps[0:E, b + 2, :], wg[:, :], x2[:, c * BANK + 3:c * BANK + 3 + BANK],
                          start=True, stop=True).then_inc(s_in, 1)
            pe.wait_ge(s_zg, NCH)
            for c in range(NCH):
                us = u[:, c * BANK:(c + 1) * BANK]
                if c >= 2:
                    pe.wait_ge(s_abs, c - 1)
                    pe.wait_ge(s_dl, c - 1)
                    pe.wait_ge(s_bch, c - 1)
                pe.matmul(ps[:, 6 + c % 2, :], wdelta[:, :], us, start=True, stop=True).then_inc(s_dlp, 1)
                pe.matmul(ps[0:2 * DS, c % 2, :], wbc[:, :], us, start=True, stop=True).then_inc(s_bcp, 1)

            pe.wait_ge(s_const, 1)
            pe.wait_ge(s_dl, NCH)
            pe.wait_ge(s_bch, NCH)
            with pe.Fori(0, NCH) as c:
                for s in range(DS + 1):
                    if s < DS:
                        if s >= 2:
                            pe.wait_ge(s_dbu, c * DS + s - 1 + SEED)
                            pe.wait_ge(s_hc, c * DS + s - 1 + SEED)
                        else:
                            pe.wait_ge(s_dbu, c * DS + SEED)
                            pe.wait_ge(s_hc, c * DS + SEED)
                        mv = bc[:, bass.ds(c * BANK, BANK)]
                        pe.matmul(ps[:, s % 2, :], sel[:, s, :], mv, start=True, stop=True).then_inc(s_bb, 1)
                        pe.matmul(ps[:, 2 + s % 2, :], sel[:, DS + s, :], mv, start=True, stop=True).then_inc(s_cb, 1)
                    if s >= 1:
                        if s == 1:
                            pe.wait_ge(s_y, c + SEED)
                        pe.wait_ge(s_hc, c * DS + s + SEED)
                        pe.matmul(ps[:, 4, :], ident[:, :], hc[:, (s - 1) % 2, :], start=(s == 1), stop=(s == DS))\
                          .then_inc(s_yac, 1)
                pe.wait_ge(s_y, c + 1 + SEED)
                pe.matmul(ps[0:E, 5, :], woT[:, :], yb[:, 1, :], start=True, stop=True).then_inc(s_op, 1)
                pe.wait_ge(s_mo, c + 1 + SEED)
                for r in range(TPC):
                    last = pe.matmul(ps[:, 6, r * E:(r + 1) * E], mo[:, r * P:(r + 1) * P], ident[0:E, 0:E],
                                     start=True, stop=True)
                last.then_inc(s_mt, 1)

            turn_tokens(1)
            pe.wait_ge(s_wt, N_WT)
            for k in range(2):
                m = pe.transpose(ps[0:E, 7, k * P:(k + 1) * P], w1n[:, k, :], ident[:, :])
            m.then_inc(s_w1p, 1)
            pe.wait_ge(s_w1T, 1)
            pe.wait_ge(s_xt, 2 * NCH)
            for c in range(NT):
                pe.matmul(ps[:, (4 + c // 2) % 8, (c % 2) * NDP:(c % 2) * NDP + ND], xt[:, c * P:(c + 1) * P],
                          w1T[:, 0:ND], start=True, stop=True).then_inc(s_sc, 1)
            pe.wait_ge(s_sce, NT // 2)
            pe.wait_ge(s_pm, 1)
            for k in range(2):
                for c in range(NT):
                    m = pe.transpose(ps[:, 4 * k + c // TPC, (c % TPC) * P:(c % TPC + 1) * P],
                                     sc[:, c, k * P:(k + 1) * P], ident[:, :])
                    if c % TPC == TPC - 1:
                        m.then_inc(s_pmp, 1)
            pe.wait_ge(s_pmT, 8)
            for c in range(NT):
                pe.matmul(ps[:, 4 + c // 8, (c % 8) * E:(c % 8 + 1) * E], pmT[:, 0, c * P:(c + 1) * P],
                          b2n[:, 0, :], start=(c % 8 == 0), stop=False)
            pe.wait_ge(s_w2n, N_W2)
            pe.wait_ge(s_tpad, 2)
            NU = 16 * NCH
            with pe.Fori(0, NG // 2) as g2:
                for gi in range(2):
                    pe.wait_ge((s_bg, s_bg1)[gi], g2 * 48 + 48)
                    for v in range(NU + 2):
                        if v < NU:
                            q, c = divmod(v, NCH)
                            pe.wait_ge(s_z, (g2 * 2 * NU + gi * NU + v - 3 if gi or v >= 4 else g2 * 2 * NU) + SEED)
                            pe.matmul(ps[:, v % 4, :], sel2[:, q, :, :].rearrange("p h e -> p (h e)"),
                                      bcg[:, gi, c * BANK:(c + 1) * BANK], start=True, stop=True).then_inc(s_zb, 1)
                        if v >= 2:
                            q, c = divmod(v - 2, NCH)
                            pe.wait_ge(s_z, g2 * 2 * NU + gi * NU + v - 1 + SEED)
                            for r in range(TPC):
                                i = c * TPC + r
                                m = pe.matmul(ps[:, 4 + i // 8, (i % 8) * E:(i % 8 + 1) * E],
                                              zz[:, (v - 2) % 4, r * P:(r + 1) * P],
                                              w2n[:, bass.ds(g2 * 32 + (gi * 16 + q), 1), :].rearrange("p o e -> p (o e)"),
                                              start=False, stop=False)
                            m.then_inc(s_zu, 1)
            for c in range(NT):
                m = pe.matmul(ps[:, 4 + c // 8, (c % 8) * E:(c % 8 + 1) * E], pmT[:, 1, c * P:(c + 1) * P],
                              b2n[:, 1, :], start=False, stop=(c % 8 == 7))
            m.then_inc(s_sum, 1)

            turn_tokens(2)
            pe.wait_ge(s_xt, 3 * NCH)
            pe.wait_ge(s_xr, 1)
            pe.wait_ge(s_wa, N_WA)

            def scores_max(p, n, k):
                h, ic = UNITS[n]
                g = FIRST[n] + k
                r, jc = divmod(k, ic + 1)
                w = BANK if jc < ic else (r + 1) * P
                q0 = ic * BANK + r * P
                pe.wait_ge(s_mxd, (p * NSTEP + g - 1 if g >= 2 else p * NSTEP) + SEED)
                m = pe.matmul(ps[:, g % 2, 0:w], qa[:, h, q0:q0 + P], ka[:, h, jc * BANK:jc * BANK + w],
                              start=True, stop=jc < ic)
                if jc == ic:
                    m = pe.matmul(ps[:, g % 2, r * P:(r + 1) * P], identb[:, :], mask_q[:, :], start=False, stop=True)
                m.then_inc(s_sm, 1)

            def scores_turned(p, n, k):
                h, ic = UNITS[n]
                g = FIRST[n] + k
                lo = max(0, k - 4 * ic) * P
                bank = 2 + g % 4
                pe.wait_ge(s_ex, (p * NSTEP + g - 3 if g >= 4 else p * NSTEP) + SEED)
                m = pe.matmul(ps[:, bank, lo:BANK], ka[:, h, k * P:(k + 1) * P],
                              qa[:, h, ic * BANK + lo:(ic + 1) * BANK], start=True, stop=k < 4 * ic)
                if k >= 4 * ic:
                    m = pe.matmul(ps[:, bank, lo:lo + P], identb[:, :], mask_k[:, :], start=False, stop=True)
                m.then_inc(s_st, 1)

            def values(p, n, k):
                h, ic = UNITS[n]
                g = FIRST[n] + k
                lo = max(0, k - 4 * ic) * P
                if k == 0:
                    pe.wait_ge(s_ot, p * len(UNITS) + n + SEED)
                pe.wait_ge(s_ex, p * NSTEP + g + 1 + SEED)
                m = pe.matmul(ps[0:E + 1, 6, lo:BANK], va[:, k, h, :], pt[:, g % 4, lo:BANK],
                              start=(k == 0), stop=(k == 4 * ic + 3))
                m.then_inc(s_av, 1)

            def project(p, n):
                pe.wait_ge(s_ot, p * len(UNITS) + n + 1 + SEED)
                pe.wait_ge(s_hd, p * len(UNITS) + n + SEED)
                for r in range(TPC):
                    m = pe.matmul(ps[:, 7, r * (E + 1):(r + 1) * (E + 1)], ot[:, r * P:(r + 1) * P],
                                  wupair[:, UNITS[n][0], :], start=True, stop=True)
                m.then_inc(s_pj, 1)

            with pe.Fori(0, NP) as p:
                pe.wait_ge(s_qs, p * 2 + 2)
                pe.wait_ge(s_hd, p * len(UNITS) + SEED)
                for t in range(2):
                    for c in range(NCH):
                        pe.matmul(ps[:, t * 4 + c, :], wpair[:, t, :], xt[:, c * BANK:(c + 1) * BANK],
                                  start=True, stop=True).then_inc(s_qkp, 1)
                for c in range(NCH):
                    pe.wait_ge(s_qe, p * NCH + c + 1)
                    for r in range(TPC):
                        m = pe.matmul(ps[:, c, r * P:(r + 1) * P], xt[:, (c * TPC + r) * P:(c * TPC + r + 1) * P],
                                      wv[:, bass.ds(p * P, P)], start=True, stop=True)
                    m.then_inc(s_vp, 1)
                pe.wait_ge(s_ke, p * (2 * NCH + 1) + 2 * NCH + 1 + SEED)
                for k in range(4 * (UNITS[0][1] + 1)):
                    scores_max(p, 0, k)
                for n, (h, ic) in enumerate(UNITS):
                    pe.wait_ge(s_mx4, p * len(UNITS) + n + 1 + SEED)
                    if n >= 1:
                        pe.wait_ge(s_hd, p * len(UNITS) + n - 1 + SEED)
                    for r in range(TPC):
                        m = pe.matmul(ps[0:1, 7, r * P:(r + 1) * P], mx4[:, n % 2, r:r + 1], nident[:, :],
                                      start=True, stop=True)
                    m.then_inc(s_mrp, 1)
                    ns = 4 * (UNITS[n + 1][1] + 1) if n + 1 < len(UNITS) else 0
                    nt = 4 * (ic + 1)
                    for k in range(max(ns, nt + 4)):
                        if k < ns:
                            scores_max(p, n + 1, k)
                        if k == 1:
                            pe.wait_ge(s_mr, p * len(UNITS) + n + 1 + SEED)
                        if k == 3 and n >= 1:
                            project(p, n - 1)
                        if 1 <= k <= nt:
                            scores_turned(p, n, k - 1)
                        if 3 <= k < nt + 3:
                            values(p, n, k - 3)
                project(p, len(UNITS) - 1)

            turn_tokens(3)
            pe.wait_ge(s_xt, 4 * NCH)
            pe.wait_ge(s_we, N_WE)
            for c in range(NT):
                m = pe.matmul(ps[:, 4, c * NE:(c + 1) * NE], xt[:, c * P:(c + 1) * P], gw[:, :], start=True, stop=True)
            m.then_inc(s_lg, 1)
            pe.wait_ge(s_g, 1)
            for c in range(NT):
                m = pe.transpose(ps[0:NE, c // TPC, (c % TPC) * P:(c % TPC + 1) * P], ge[:, c, :], ident[:, :])
                if c % TPC == TPC - 1:
                    m.then_inc(s_gt, 1)
            pe.wait_ge(s_gp, NCH)
            with pe.Fori(0, NCH) as c:
                for e in range(NE + 1):
                    if e < NE:
                        pe.wait_ge(s_hg, (c * NE + e - 1 if e >= 2 else c * NE) + SEED)
                        pe.matmul(ps[:, e % 2, :], w1[:, e, :], xt[:, bass.ds(c * BANK, BANK)],
                                  start=True, stop=True).then_inc(s_m1, 1)
                        pe.matmul(ps[:, 2 + e % 2, :], sel[:, e, :], bc[:, bass.ds(c * BANK, BANK)],
                                  start=True, stop=True).then_inc(s_gb, 1)
                    if e == 0:
                        pe.wait_ge(s_yt, c + SEED)
                        pe.matmul(ps[0:E, 4, :], b2[:, :], gT[:, bass.ds(c * BANK, BANK)], start=True, stop=False)
                    else:
                        pe.wait_ge(s_hg, c * NE + e + SEED)
                        pe.matmul(ps[0:E, 4, :], w2[:, e - 1, :], hg[:, (e - 1) % 2, :],
                                  start=False, stop=(e == NE)).then_inc(s_m2, 1)
                pe.wait_ge(s_yt, c + 1 + SEED)
                pe.wait_ge(s_ya, c + SEED)
                for r in range(TPC):
                    m = pe.matmul(ps[:, 5, r * E:(r + 1) * E], yt[:, r * P:(r + 1) * P], ident[0:E, 0:E],
                                  start=True, stop=True)
                m.then_inc(s_ytp, 1)

        @block.scalar
        def _(act):
            for s in (s_ex, s_ot, s_yt):
                act.sem_inc(s, SEED)
            def ln_std(k):
                act.wait_ge(s_var, k + 1)
                act.activation(stat[:, 3, :], stat[:, 2, :], ACT.Sqrt).then_inc(s_std, 1)

            def turned(k):
                for c in range(NCH):
                    act.wait_ge(s_xtp, k * NCH + c + 1)
                    act.activation(xt[0:E, c * BANK:(c + 1) * BANK], ps[0:E, c, :], ACT.Copy).then_inc(s_xt, 1)

            act.wait_ge(s_wm, N_WM)
            act.activation(neg_a[:, :], alog[:, :], ACT.Exp).then_inc(step_s, 1)
            act.wait_ge(step_s, 1)
            act.mul(neg_a[:, :], neg_a[:, :], -1.0).then_inc(step_s, 1)
            act.wait_ge(s_pad, 1)
            act.wait_ge(s_wps, 1)
            for dst, src in (
                (dtwT[:, :], ps[0:RK, 5, P:2 * P]),
                (wconv[:, :, :], ps[:, 4, 0:2 * P].rearrange("p (k n) -> p k n", k=2)),
                (wz[0:E, :], ps[0:E, 4, 2 * P:3 * P]), (wg[0:E, :], ps[0:E, 4, 3 * P:3 * P + E]),
                (wbc[:, :], ps[:, 5, RK:RK + 2 * DS]), (woT[:, :], ps[:, 5, 2 * P:2 * P + E]),
            ):
                last = act.activation(dst, src, ACT.Copy)
            last.then_inc(s_wsb, 1)
            act.wait_ge(s_wdp, 1)
            act.activation(wdelta[:, :], ps[:, 6, 0:DI], ACT.Copy).then_inc(s_wds, 1)
            ln_std(0)
            ln_std(1)
            for c in range(NCH):
                act.wait_ge(s_xtp, c + 1)
                act.activation(x2[0:E, 3 + c * BANK:3 + (c + 1) * BANK], ps[0:E, c, :], ACT.Identity,
                               bias=bet[:, :], scale=gam[:, :])
                act.activation(x2[E:P, 4 + c * BANK:4 + (c + 1) * BANK], ps[0:E, c, :], ACT.Identity,
                               bias=bet[:, :], scale=gam[:, :]).then_inc(s_xt, 1)
            for c in range(NCH):
                cs = slice(c * BANK, (c + 1) * BANK)
                act.wait_ge(s_in, c + 1)
                act.activation(u[:, cs], ps[:, 4, :], ACT.Silu, bias=convb[:, :]).then_inc(s_u, 1)
                act.activation(sz[:, cs], ps[:, 5, :], ACT.Silu)
                act.activation(gsig[:, cs], ps[0:E, 6, :], ACT.Identity, bias=gateb[:, :]).then_inc(s_zg, 1)
            act.wait_ge(s_zg, NCH)
            act.activation(gsig[:, :], gsig[:, :], ACT.Sigmoid).then_inc(s_zg, 1)
            for c in range(NCH):
                act.wait_ge(s_dlp, c + 1)
                if c >= 2:
                    act.wait_ge(s_dl, c - 1)
                b = spl[:, c % 2, :]
                act.activation(b, ps[:, 6 + c % 2, :], ACT.Abs, bias=dtb[:, :]).then_inc(s_abs, 1)
                act.wait_ge(s_abs, c + 1)
                act.activation(b, b, ACT.Exp, scale=-1.0).then_inc(step_s, 1)
                act.wait_ge(step_s, 3 + c)
                act.activation(b, b, ACT.Ln, bias=1.0).then_inc(s_ln1, 1)
            with act.Fori(0, NCH) as c:
                for s in range(DS):
                    if s == 0:
                        act.wait_ge(s_dcur, c + 1)
                    act.wait_ge(s_scan, (c * DS + s - 1 if s >= 2 else c * DS) + SEED)
                    act.activation(dA[:, s % 2, :], dcur[:, :], ACT.Exp,
                                   scale=neg_a[:, s:s + 1]).then_inc(s_da, 1)

            ln_std(2)
            act.wait_ge(s_w1p, 1)
            act.activation(w1T[0:E, 0:ND], ps[0:E, 7, 0:ND], ACT.Copy).then_inc(s_w1T, 1)
            turned(1)
            for b in range(NT // 2):
                act.wait_ge(s_sc, 2 * b + 2)
                act.activation(sc[:, 2 * b:2 * b + 2, 0:ND],
                               ps[:, (4 + b) % 8, :].rearrange("p (c n) -> p c n", n=NDP)[:, :, 0:ND], ACT.Copy)\
                   .then_inc(s_sce, 1)
            act.wait_ge(s_ls, 1)
            act.activation(ls[:, :, :], ls[:, :, :], ACT.Abs).then_inc(s_pw, 1)
            act.wait_ge(s_pw, 1)
            act.activation(pw[:, :, :], ls[:, :, :], ACT.Gelu).then_inc(s_pw, 1)
            for b in range(8):
                act.wait_ge(s_pmp, b + 1)
                act.activation(pmT[:, b // 4, (b % 4) * BANK:(b % 4 + 1) * BANK], ps[:, b, :], ACT.Copy)\
                   .then_inc(s_pmT, 1)

            ln_std(3)
            turned(2)
            with act.Fori(0, NP) as p:
                for c in range(NCH):
                    act.wait_ge(s_qkp, p * 2 * NCH + c + 1)
                    act.activation(qa[0:E, 0, c * BANK:(c + 1) * BANK], ps[0:E, c, :], ACT.Copy, scale=float(E) ** -0.5)
                    act.activation(qa[0:E, 1, c * BANK:(c + 1) * BANK], ps[E:P, c, :], ACT.Copy,
                                   scale=float(E) ** -0.5).then_inc(s_qe, 1)
                for n, (h, ic) in enumerate(UNITS):
                    for k in range(4 * (ic + 1)):
                        g = FIRST[n] + k
                        lo = max(0, k - 4 * ic) * P
                        act.wait_ge(s_st, p * NSTEP + g + 1)
                        act.wait_ge(s_av, (p * NSTEP + g - 3 if g >= 4 else p * NSTEP) + SEED)
                        act.activation(pt[:, g % 4, lo:BANK], ps[:, 2 + g % 4, lo:BANK], ACT.Exp).then_inc(s_ex, 1)
                    act.wait_ge(s_av, p * NSTEP + FIRST[n + 1] + SEED)
                    if n >= 1:
                        act.wait_ge(s_pj, p * len(UNITS) + n + SEED)
                    else:
                        act.wait_ge(s_pj, p * len(UNITS) + SEED)
                    act.activation(ot[:, :], ps[0:E + 1, 6, :], ACT.Copy).then_inc(s_ot, 1)

            ln_std(4)
            turned(3)
            act.wait_ge(s_d, 1)
            act.activation(tw[:, 1, :], tw[:, 0, :], ACT.Exp).then_inc(s_e, 1)
            with act.Fori(0, NCH) as c:
                for e in range(NE):
                    act.wait_ge(s_m1, c * NE + e + 1)
                    act.wait_ge(s_hg, (c * NE + e - 1 if e >= 2 else c * NE) + SEED)
                    act.activation(hr[:, e % 2, :], ps[:, e % 2, :], ACT.Relu).then_inc(s_rl, 1)
                act.wait_ge(s_m2, c * NE + NE + SEED)
                act.wait_ge(s_ytp, c + SEED)
                act.activation(yt[:, :], ps[0:E, 4, :], ACT.Copy).then_inc(s_yt, 1)
            ln_std(5)

        @block.vector
        def _(dve):
            st = Steps(dve, step_v)
            for s in (s_dbu, s_hc, s_y, s_h1, s_mxd, s_mx4, s_hd,
                      s_z, s_hg, s_ya, s_scan, s_mr, s_mo, s_ke):
                dve.sem_inc(s, SEED)

            def wide(col):
                return col.unsqueeze(2).to_broadcast([P, NT, E])

            def layernorm(src, dst, k):
                st.after()
                st.did(dve.tensor_reduce(stat[:, 0, :], src, AX_X, ALU.add))
                st.after()
                st.did(dve.tensor_scalar(stat[:, 0, :], stat[:, 0, :], -1.0 / E, None, ALU.mult))
                st.after()
                st.did(dve.tensor_tensor(cen[:, :, :], src, wide(stat[:, 0, :]), ALU.add))
                st.after()
                st.did(dve.tensor_tensor(sq[:, :, :], cen[:, :, :], cen[:, :, :], ALU.mult))
                st.after()
                st.did(dve.tensor_reduce(stat[:, 1, :], sq[:, :, :], AX_X, ALU.add))
                st.after()
                dve.tensor_scalar(stat[:, 2, :], stat[:, 1, :], 1.0 / E, EPS, ALU.mult, ALU.add).then_inc(s_var, 1)
                dve.wait_ge(s_std, k + 1)
                st.did(dve.reciprocal(stat[:, 4, :], stat[:, 3, :]))
                st.after()
                st.did(dve.tensor_tensor(dst, cen[:, :, :], wide(stat[:, 4, :]), ALU.mult))

            dve.wait_ge(s_ids, 16)
            dve.tensor_copy(idr[:, :], ids[:, :]).then_inc(s_idr, 1)
            dve.wait_ge(s_idt, 1)
            st.did(dve.tensor_copy(idf[:, 0, :], ps[:, 7, 0:NT]))
            st.after()
            st.did(dve.tensor_scalar(idf[:, 1, :], idf[:, 0, :], 0.0, float(V), ALU.is_lt, ALU.mult))
            st.after()
            st.did(dve.tensor_tensor(idf[:, 0, :], idf[:, 0, :], idf[:, 1, :], ALU.add))
            st.after()
            st.did(dve.tensor_scalar(idf[:, 0, :], idf[:, 0, :], 0.0, float(V - 1), ALU.max, ALU.min))
            st.after()
            dve.tensor_scalar(rows[:, :], idf[:, 0, :], float(HID // E), float(LAYER), ALU.mult, ALU.add)\
               .then_inc(s_rows, 1)
            for t in (x2[:, 0:4], wz[E:P, :], wg[E:P, :], hs[:, :, 0:1], xt[E:P, :]):
                st.did(dve.memset(t, 0.0))
            st.after()
            st.did(dve.memset(xt[E:E + 1, :], 1.0))
            st.after()
            dve.sem_inc(s_pad, 1)
            dve.wait_ge(s_wm, N_WM)
            for k in range(KC):
                st.did(dve.tensor_scalar(wtap[:, k, :], win[:, 0, :], convw[:, KC - 1 - k:KC - k], None, ALU.mult))
            st.after()
            dve.sem_inc(s_wtap, 1)

            dve.wait_ge(s_emb, NT * 16)
            layernorm(h0[:, :, :], xn[:, :, :], 0)
            st.after()
            st.did(dve.tensor_tensor(h1[:, :, :], h0[:, :, :], xn[:, :, :], ALU.add))
            layernorm(xn[:, :, :], xn[:, :, :], 1)
            st.after()
            dve.sem_inc(s_xn, 1)
            for c in range(NCH):
                cs = slice(c * BANK, (c + 1) * BANK)
                dve.wait_ge(s_abs, c + 1)
                st.did(dve.tensor_scalar(delta[:, cs], ps[:, 6 + c % 2, :], dtb[:, :], 0.0, ALU.add, ALU.max))
                dve.wait_ge(s_bcp, c + 1)
                st.did(dve.tensor_copy(bc[0:32, cs], ps[0:32, c % 2, :]))
                st.after()
                st.did(dve.tensor_tensor(res1[:, :], ps[0:32, c % 2, :], bc[0:32, cs], ALU.subtract))
                st.after()
                st.did(dve.tensor_copy(mid[:, :], res1[:, :]))
                st.after()
                st.did(dve.tensor_tensor(res2[:, :], res1[:, :], mid[:, :], ALU.subtract))
                st.did(dve.tensor_copy(bc[32:64, cs], mid[:, :]))
                st.after()
                dve.tensor_copy(bc[64:96, cs], res2[:, :]).then_inc(s_bch, 1)
                dve.wait_ge(s_ln1, c + 1)
                st.did(dve.tensor_tensor(delta[:, cs], delta[:, cs], spl[:, c % 2, :], ALU.add))
                st.after()
                dve.wait_ge(s_u, c + 1)
                dve.tensor_tensor(du[:, cs], delta[:, cs], u[:, cs], ALU.mult).then_inc(s_dl, 1)
            dve.wait_ge(s_dl, NCH)
            dve.wait_ge(s_zg, NCH + 1)
            n0 = st.n
            with dve.Fori(0, NCH) as c:
                cd = bass.ds(c * BANK, BANK)
                dve.tensor_copy(dcur[:, :], delta[:, cd]).then_inc(s_dcur, 1)
                for s in range(DS + 1):
                    if s < DS:
                        dve.wait_ge(s_bb, c * DS + s + 1)
                        dve.tensor_tensor(dbu[:, s % 2, :], du[:, cd], ps[:, s % 2, :], ALU.mult).then_inc(s_dbu, 1)
                    if s >= 1:
                        dve.wait_ge(s_cb, c * DS + s)
                        dve.wait_ge(s_scan, c * DS + s + SEED)
                        dve.wait_ge(s_yac, (c * DS + s - 2 if s >= 3 else c * DS) + SEED)
                        dve.tensor_tensor(hc[:, (s - 1) % 2, :], hs[:, s - 1, 1:BANK + 1], ps[:, 2 + (s - 1) % 2, :],
                                          ALU.mult).then_inc(s_hc, 1)
                    if s < DS:
                        dve.wait_ge(s_da, c * DS + s + 1)
                        dve.wait_ge(s_dbu, c * DS + s + 1 + SEED)
                        if s == 0:
                            dve.wait_ge(s_h1, c * 2 + SEED)
                        dve.tensor_tensor_scan(hs[:, s, 1:BANK + 1], dA[:, s % 2, :], dbu[:, s % 2, :],
                                               hs[:, s, 0:1], ALU.mult, ALU.add).then_inc(s_scan, 1)
                dve.wait_ge(s_hc, c * DS + DS + SEED)
                dve.tensor_copy(hs[:, :, 0:1], hs[:, :, BANK:BANK + 1]).then_inc(s_h1, 1)
                dve.wait_ge(s_yac, c * DS + DS + SEED)
                dve.scalar_tensor_tensor(yb[:, 0, :], u[:, cd], dskip[:, :], ps[:, 4, :], ALU.mult, ALU.add)\
                   .then_inc(step_v, 1)
                dve.wait_ge(step_v, n0 + c * 1 + 1)
                dve.wait_ge(s_op, c + SEED)
                dve.tensor_tensor(yb[:, 1, :], yb[:, 0, :], sz[:, cd], ALU.mult).then_inc(s_y, 1)
                dve.wait_ge(s_op, c + 1 + SEED)
                dve.wait_ge(s_mt, c + SEED)
                dve.tensor_tensor(mo[:, :], ps[0:E, 5, :], gsig[:, cd], ALU.mult).then_inc(s_mo, 1)
                dve.wait_ge(s_mt, c + 1 + SEED)
                hv = h1[:, bass.ds(c * TPC, TPC), :]
                dve.tensor_tensor(hv, hv, ps[:, 6, 0:TPC * E].rearrange("p (r e) -> p r e", e=E), ALU.add)\
                   .then_inc(s_h1, 1)
            st.n = n0 + NCH
            dve.wait_ge(s_h1, 2 * NCH + SEED)

            layernorm(h1[:, :, :], xn[:, :, :], 2)
            st.after()
            dve.sem_inc(s_xn, 1)
            st.did(dve.memset(mk[:, :, 0:1], 1.0))
            st.did(dve.memset(mk[:, :, ND:NDP], 0.0))
            dve.wait_ge(s_sce, NT // 2)
            st.did(dve.memset(sc[:, :, ND:NDP], 0.0))
            for i in range(DL - 1):
                lo, n = 2 ** i - 1, 2 ** i
                kids = mk[:, :, 2 * lo + 1:2 * lo + 1 + 2 * n].rearrange("p c (n h) -> p c n h", h=2)
                left, right = kids[:, :, :, 0], kids[:, :, :, 1]
                st.after()
                st.did(dve.scalar_tensor_tensor(right, sc[:, :, lo:lo + n], 0.0, mk[:, :, lo:lo + n],
                                                ALU.is_gt, ALU.mult))
                st.after()
                st.did(dve.tensor_tensor(left, mk[:, :, lo:lo + n], right, ALU.subtract))
            st.after()
            st.did(dve.tensor_tensor(sc[:, :, :], sc[:, :, :], mk[:, :, :], ALU.mult))
            st.after()
            for i in range(DL):
                lo, n = 2 ** i - 1, 2 ** i
                st.did(dve.tensor_reduce(ls[:, :, i:i + 1].rearrange("p c o -> p (c o)"), sc[:, :, lo:lo + n],
                                         AX_X, ALU.add))
            st.after()
            dve.sem_inc(s_ls, 1)
            dve.wait_ge(s_pw, 2)
            for i in range(DL):
                lo, n = 2 ** i - 1, 2 ** i
                st.did(dve.tensor_tensor(sc[:, :, lo:lo + n], mk[:, :, lo:lo + n],
                                         pw[:, :, i:i + 1].to_broadcast([P, NT, n]), ALU.mult))
            st.after()
            dve.sem_inc(s_pm, 1)
            for c in range(NCH):
                st.did(dve.tensor_copy(xt[E:P, c * BANK:(c + 1) * BANK], xt[0:E, c * BANK:(c + 1) * BANK]))
            for k in range(2):
                dve.wait_ge(s_pmT, 8)
                st.did(dve.tensor_copy(parts[:, k, 0, :], pmT[:, k, :]))
                st.after()
                st.did(dve.tensor_tensor(rem[:, :], pmT[:, k, :], parts[:, k, 0, :], ALU.subtract))
                st.after()
                st.did(dve.tensor_copy(parts[:, k, 1, :], rem[:, :]))
                st.after()
                st.did(dve.tensor_tensor(rem[:, :], rem[:, :], parts[:, k, 1, :], ALU.subtract))
                st.after()
                st.did(dve.tensor_copy(parts[:, k, 2, :], rem[:, :]))
                st.after()
                dve.sem_inc(s_parts, 1)
            NU = 16 * NCH
            with dve.Fori(0, NG // 2) as g2:
                for v in range(2 * NU):
                    c = v % NCH
                    dve.wait_ge(s_zb, g2 * 2 * NU + v + 1)
                    dve.wait_ge(s_zu, (g2 * 2 * NU + v - 3 if v >= 4 else g2 * 2 * NU) + SEED)
                    dve.tensor_tensor(zz[:, v % 4, :], xt[:, c * BANK:(c + 1) * BANK], ps[:, v % 4, :], ALU.mult)\
                       .then_inc(s_z, 1)
            dve.wait_ge(s_sum, 1)
            hv = h1[:, :, :]
            for k in range(2):
                hv = h1[:, 8 * k:8 * k + 8, :]
                st.did(dve.tensor_tensor(hv, hv, ps[:, 4 + k, :].rearrange("p (r e) -> p r e", e=E), ALU.add))
            st.did(dve.memset(xt[E:P, :], 0.0))
            st.after()
            dve.sem_inc(s_h2, 1)
            dve.memset(xt[E:E + 1, :], 1.0).then_inc(s_xr, 1)

            layernorm(h1[:, :, :], xn[:, :, :], 3)
            st.after()
            dve.sem_inc(s_xn, 1)
            dve.wait_ge(s_wa, N_WA)
            st.did(dve.tensor_tensor(h3[:, :, :], h1[:, :, :], bub[:, :].unsqueeze(1).to_broadcast([P, NT, E]), ALU.add))
            st.after()

            def take_max(p, n, between=None):
                h, ic = UNITS[n]
                for k in range(4 * (ic + 1)):
                    if k == 4 and between:
                        between()
                    g = FIRST[n] + k
                    r, jc = divmod(k, ic + 1)
                    w = BANK if jc < ic else (r + 1) * P
                    dve.wait_ge(s_sm, p * NSTEP + g + 1)
                    if k == 0:
                        dve.wait_ge(s_mx4, p * len(UNITS) + n + SEED)
                    dve.tensor_reduce(mx[:, n % 2, r, jc:jc + 1], ps[:, g % 2, 0:w], AX_X, ALU.max).then_inc(s_mxd, 1)
                dve.wait_ge(s_mxd, p * NSTEP + FIRST[n + 1] + SEED)
                if ic == 0 and between:
                    between()
                dve.tensor_reduce(mx4[:, n % 2, :], mx[:, n % 2, :, 0:ic + 1], AX_X, ALU.max).then_inc(s_mx4, 1)

            def max_row(p, n):
                h, ic = UNITS[n]
                dve.wait_ge(s_mrp, p * len(UNITS) + n + 1)
                dve.tensor_copy(qa[E:E + 1, h, ic * BANK:(ic + 1) * BANK], ps[0:1, 7, :]).then_inc(s_mr, 1)

            def add_head(p, n, m0):
                h, ic = UNITS[n]
                dve.wait_ge(s_pj, p * len(UNITS) + n + 1 + SEED)
                v = ps[:, 7, 0:TPC * (E + 1)].rearrange("p (r e) -> p r e", e=E + 1)
                m = m0 + p * (2 * len(UNITS) + 2)
                k = 2 * n + (n > 0) + (n > 1)
                dve.reciprocal(rden[:, 0, :], v[:, :, E:E + 1].rearrange("p r o -> p (r o)")).then_inc(step_v, 1)
                k += 1
                dve.wait_ge(step_v, m + k)
                if ic == 0:
                    dve.memset(rden[0:1, 0, 0:1], 0.0).then_inc(step_v, 1)
                    k += 1
                    dve.wait_ge(step_v, m + k)
                dve.tensor_tensor(on[:, :, :], v[:, :, 0:E], rden[:, 0, :].unsqueeze(2).to_broadcast([P, TPC, E]),
                                  ALU.mult).then_inc(step_v, 1)
                k += 1
                dve.wait_ge(step_v, m + k)
                hv = h3[:, ic * TPC:(ic + 1) * TPC, :]
                dve.tensor_tensor(hv, hv, on[:, :, :], ALU.add).then_inc(s_hd, 1)

            n0 = st.n
            with dve.Fori(0, NP) as p:
                for c in range(NCH):
                    dve.wait_ge(s_qkp, p * 2 * NCH + NCH + c + 1)
                    dve.tensor_copy(ka[0:E, 0, c * BANK:(c + 1) * BANK], ps[0:E, 4 + c, :])
                    dve.tensor_copy(ka[0:E, 1, c * BANK:(c + 1) * BANK], ps[E:P, 4 + c, :]).then_inc(s_ke, 1)
                dve.wait_ge(s_apad, 1)
                dve.memset(qa[E:E + 1, :, :], 0.0).then_inc(s_ke, 1)
                for c in range(NCH):
                    dve.wait_ge(s_vp, p * NCH + c + 1)
                    dve.tensor_copy(va[:, c * TPC:(c + 1) * TPC, :, 0:E],
                                    ps[:, c, :].rearrange("p (r h e) -> p r h e", h=2, e=E)).then_inc(s_ke, 1)
                take_max(p, 0)
                for n in range(len(UNITS)):
                    max_row(p, n)
                    add = (lambda: add_head(p, n - 1, n0)) if n >= 1 else None
                    if n + 1 < len(UNITS):
                        take_max(p, n + 1, add)
                    else:
                        add()
                add_head(p, len(UNITS) - 1, n0)
            st.n = n0 + NP * (2 * len(UNITS) + 2)
            dve.wait_ge(s_hd, NP * len(UNITS) + SEED)

            layernorm(h3[:, :, :], xn[:, :, :], 4)
            st.after()
            dve.sem_inc(s_xn, 1)
            dve.wait_ge(s_lg, 1)
            st.did(dve.tensor_copy(lg[:, :, :], ps[:, 4, 0:NT * NE].rearrange("p (c e) -> p c e", e=NE)))
            st.after()
            for c in range(NT):
                st.did(dve.max(out=top[:, c, :], in_=lg[:, c, :]))
            st.after()
            for c in range(NT):
                st.did(dve.max_index(out=topi[:, c, :], in_max=top[:, c, :], in_values=lg[:, c, :]))
            dve.tensor_tensor(tw[:, 0, :], top[:, :, 1:2].rearrange("p c o -> p (c o)"),
                              top[:, :, 0:1].rearrange("p c o -> p (c o)"), ALU.subtract).then_inc(s_d, 1)
            st.after()
            st.did(dve.tensor_copy(topf[:, :, :], topi[:, :, 0:2]))
            dve.wait_ge(s_e, 1)
            st.did(dve.tensor_scalar(tw[:, 2, :], tw[:, 1, :], 1.0, None, ALU.add))
            st.after()
            st.did(dve.reciprocal(tw[:, 0, :], tw[:, 2, :]))
            st.after()
            st.did(dve.tensor_tensor(tw[:, 1, :], tw[:, 1, :], tw[:, 0, :], ALU.mult))
            io = iota_e[:, :].unsqueeze(1).to_broadcast([P, NT, NE])
            dve.wait_ge(s_const, 1)
            for j, dst in ((0, ge), (1, ge2)):
                st.after()
                st.did(dve.tensor_tensor(dst[:, :, :], io, topf[:, :, j:j + 1].to_broadcast([P, NT, NE]), ALU.is_equal))
                st.after()
                st.did(dve.tensor_tensor(dst[:, :, :], dst[:, :, :], tw[:, j, :].unsqueeze(2).to_broadcast([P, NT, NE]),
                                         ALU.mult))
            st.after()
            dve.tensor_tensor(ge[:, :, :], ge[:, :, :], ge2[:, :, :], ALU.add).then_inc(s_g, 1)
            st.did(dve.memset(bc[:, :], 0.0))
            st.did(dve.memset(gT[:, :], 0.0))
            st.after()
            for c in range(NCH):
                cs = slice(c * BANK, (c + 1) * BANK)
                dve.wait_ge(s_gt, c + 1)
                st.did(dve.tensor_copy(gT[0:NE, cs], ps[0:NE, c, :]))
                st.after()
                st.did(dve.tensor_copy(bc[0:NE, cs], gT[0:NE, cs]))
                st.after()
                st.did(dve.tensor_tensor(res1[0:NE, :], gT[0:NE, cs], bc[0:NE, cs], ALU.subtract))
                st.after()
                st.did(dve.tensor_copy(mid[0:NE, :], res1[0:NE, :]))
                st.after()
                st.did(dve.tensor_tensor(res2[0:NE, :], res1[0:NE, :], mid[0:NE, :], ALU.subtract))
                st.did(dve.tensor_copy(bc[32:32 + NE, cs], mid[0:NE, :]))
                st.after()
                dve.tensor_copy(bc[64:64 + NE, cs], res2[0:NE, :]).then_inc(s_gp, 1)
                dve.wait_ge(s_gp, c + 1)
            with dve.Fori(0, NCH) as c:
                for e in range(NE):
                    dve.wait_ge(s_gb, c * NE + e + 1)
                    dve.wait_ge(s_rl, c * NE + e + 1)
                    dve.wait_ge(s_m2, (c * NE + e - 1 if e >= 2 else c * NE) + SEED)
                    dve.tensor_tensor(hg[:, e % 2, :], hr[:, e % 2, :], ps[:, 2 + e % 2, :], ALU.mult).then_inc(s_hg, 1)
                dve.wait_ge(s_ytp, c + 1 + SEED)
                xv = xn[:, bass.ds(c * TPC, TPC), :]
                dve.tensor_tensor(xv, xv, ps[:, 5, 0:TPC * E].rearrange("p (r e) -> p r e", e=E), ALU.add)\
                   .then_inc(s_ya, 1)
            dve.wait_ge(s_ya, NCH + SEED)
            layernorm(xn[:, :, :], xn[:, :, :], 5)
            dve.wait_ge(s_we, N_WE)
            st.after()
            st.did(dve.tensor_tensor(xn[:, :, :], xn[:, :, :], gamb[:, :].unsqueeze(1).to_broadcast([P, NT, E]), ALU.mult))
            st.did(dve.tensor_tensor(h3[:, :, :], h3[:, :, :], betb[:, :].unsqueeze(1).to_broadcast([P, NT, E]), ALU.add))
            st.after()
            dve.tensor_tensor(xn[:, :, :], xn[:, :, :], h3[:, :, :], ALU.add).then_inc(s_fin, 1)


_INS = ['x', 'L0_tok_ple_table', 'L0_attn_ln_gamma', 'L0_attn_ln_beta', 'L0_attn_in_proj_w', 'L0_attn_conv_w',
        'L0_attn_conv_b', 'L0_attn_x_proj_w', 'L0_attn_dt_proj_w', 'L0_attn_dt_proj_b', 'L0_attn_A_log', 'L0_attn_D',
        'L0_attn_out_proj_w', 'L0_attn_gate_w', 'L0_attn_gate_b', 'L0_ffn_w1s', 'L0_ffn_b1s', 'L0_ffn_w2s',
        'L0_ffn_b2s', 'L1_attn_Wq', 'L1_attn_bq', 'L1_attn_Wk', 'L1_attn_bk', 'L1_attn_Wv', 'L1_attn_bv',
        'L1_attn_Wu', 'L1_attn_bu', 'L1_ffn_gate_w', 'L1_ffn_gate_b', 'L1_ffn_w1', 'L1_ffn_b1', 'L1_ffn_w2',
        'L1_ffn_b2', 'L1_ffn_gamma', 'L1_ffn_beta']


def kernel(**inputs):
    import numpy as _np
    import concourse.bacc as _bacc
    from concourse import mybir as _mybir
    from concourse.bass_utils import run_bass_kernel_spmd as _run

    nc = _bacc.Bacc("TRN2", target_bir_lowering=False, num_devices=1)
    arrays, args = {}, {}
    for name in _INS:
        v = _np.ascontiguousarray(inputs[name])
        arrays[f"in_{name}"] = v
        args[name] = nc.dram_tensor(f"in_{name}", v.shape, _mybir.dt.from_np(v.dtype), kind="ExternalInput").ap()
    t = inputs["x"].shape[1]
    d = inputs["L0_attn_gate_w"].shape[0]
    out = nc.dram_tensor("out_h", (1, t, d), _mybir.dt.float32, kind="ExternalOutput").ap()
    tower_kernel(nc, args, out)
    r = _run(nc, [arrays], core_ids=[0])
    return r.results[0]["out_h"]
```

```python
from contextlib import ExitStack

import concourse.bass as bass
from concourse import mybir

F32 = mybir.dt.float32
BF16 = mybir.dt.bfloat16
I32 = mybir.dt.int32
U32 = mybir.dt.uint32
ALU = mybir.AluOpType
ACT = mybir.ActivationFunctionType
AX_X = mybir.AxisListType.X

P = 128
SEED = 1
BANK = 512
NEG = -1.0e30


class Steps:

    def __init__(self, eng, sem):
        self.eng, self.sem, self.n = eng, sem, 0

    def did(self, ins):
        ins.then_inc(self.sem, 1)
        self.n += 1
        return self.n

    def after(self, n=None):
        self.eng.wait_ge(self.sem, self.n if n is None else n)


def tower_kernel(nc, a, out):
    T = a["x"].shape[1]
    V, HID = a["L0_tok_ple_table"].shape
    E = a["L0_attn_gate_w"].shape[0]
    LAYER = 3
    NT = T // P
    NCH = T // BANK
    TPC = BANK // P
    DI = a["L0_attn_D"].shape[0]
    DS = a["L0_attn_A_log"].shape[1]
    KC = a["L0_attn_conv_w"].shape[2]
    RK = a["L0_attn_dt_proj_w"].shape[1]
    NH = a["L1_attn_Wq"].shape[1] // E
    NP = NH // 2
    NE = a["L1_ffn_gate_w"].shape[1]
    FF = a["L1_ffn_w1"].shape[2]
    ND = a["L0_ffn_w1s"].shape[0]
    NDP = ND + 1
    DL = NDP.bit_length() - 1
    NL = 2 ** (DL - 1)
    BLK = 32
    TS = -(-(T // BLK + NL) // (P // BLK * 8)) * 8
    NB = TS * (P // BLK)
    SH = BLK.bit_length() - 1
    QN = [NL >> (2 * q) for q in range(DL // 2)]
    PL = E + DL
    EPS = 1e-5

    with ExitStack() as ctx:
        def sb(name, shape, dt=F32):
            return ctx.enter_context(nc.sbuf_tensor(name, shape, dt))

        def sem(name):
            return ctx.enter_context(nc.semaphore(name))

        ps = ctx.enter_context(nc.psum_tensor("ps", [P, 8, BANK], F32))
        arena = sb("arena", [P, 26 * 1024])
        taken = {"mamba": 0, "tree": 0, "attention": 0, "moe": 0}

        def part(stage, shape, dt=F32):
            n = 1
            for d in shape[1:]:
                n *= d
            words = n * mybir.dt.size(dt) // 4
            v = arena[0:shape[0], taken[stage]:taken[stage] + words]
            taken[stage] += words
            if dt != F32:
                v = v.bitcast(dt)
            if len(shape) == 2:
                return v
            names = "abcd"[:len(shape) - 1]
            return v.rearrange(f"p ({' '.join(names)}) -> p {' '.join(names)}", **dict(zip(names[1:], shape[2:])))

        ident = sb("ident", [P, P])
        nident = sb("nident", [P, P])
        identb = sb("identb", [P, P], BF16)
        mask_q = sb("mask_q", [P, P], BF16)
        mask_k = sb("mask_k", [P, P], BF16)
        sel = sb("sel", [96, 32, P], BF16)
        iota_e = sb("iota_e", [P, NE])
        iota_b = sb("iota_b", [P, 2])
        onesb = sb("onesb", [P, P], BF16)
        before = sb("before", [P, P], BF16)

        h0 = sb("h0", [P, NT, E])
        h1 = sb("h1", [P, NT, E])
        h3 = sb("h3", [P, NT, E])
        cen = sb("cen", [P, NT, E])
        sq = sb("sq", [P, NT, E])
        xn = sb("xn", [P, NT, E])
        stat = sb("stat", [P, 8, NT])
        xt = sb("xt", [P, T])

        ids = sb("ids", [NT, P], I32)
        idr = sb("idr", [NT, P])
        idf = sb("idf", [P, 2, NT])
        rows = sb("rows", [P, NT], U32)

        win = sb("win", [P, 2, E])
        convw = sb("convw", [DI, KC])
        convb = sb("convb", [DI, 1])
        xpw = sb("xpw", [RK + 2 * DS, DI])
        dtw = sb("dtw", [DI, RK])
        dtb = sb("dtb", [DI, 1])
        alog = sb("alog", [DI, DS])
        neg_a = sb("neg_a", [DI, DS])
        dskip = sb("dskip", [DI, 1])
        outw = sb("outw", [E, DI])
        gatew = sb("gatew", [E, E])
        gateb = sb("gateb", [E, 1])
        gam = sb("gam", [E, 1])
        bet = sb("bet", [E, 1])
        wtap = sb("wtap", [DI, KC, E])
        wconv = sb("wconv", [P, 2, DI])
        wz = sb("wz", [P, DI])
        wg = sb("wg", [P, E])
        wbc = sb("wbc", [DI, 2 * DS])
        dtwT = sb("dtwT", [RK, DI])
        wdelta = sb("wdelta", [DI, DI])
        woT = sb("woT", [DI, E])
        x2 = part("mamba", [P, T + 8])
        u = part("mamba", [DI, T])
        sz = part("mamba", [DI, T])
        gsig = part("mamba", [E, T])
        delta = part("mamba", [DI, T])
        du = part("mamba", [DI, T])
        spl = part("mamba", [DI, 2, BANK])
        bc = sb("bc", [96, T], BF16)
        res1 = sb("res1", [32, BANK])
        mid = sb("mid", [32, BANK], BF16)
        res2 = sb("res2", [32, BANK])
        dA = part("mamba", [DI, 2, BANK])
        dbu = part("mamba", [DI, 2, BANK])
        hs = part("mamba", [DI, DS, BANK + 1])
        dcur = spl[:, 0, :]
        hc = part("mamba", [DI, 2, BANK])
        yb = part("mamba", [DI, 2, BANK])
        mo = part("mamba", [E, BANK])

        step_v = sem("vector_step")
        step_s = sem("scalar_step")
        step_g = sem("gpsimd_step")
        step_t = sem("tensor_step")
        s_ids = sem("ids_loaded")
        s_idr = sem("ids_as_floats")
        s_idt = sem("ids_turned")
        s_ident = sem("identity_ready")
        s_rows = sem("rows_ready")
        s_emb = sem("embeddings_loaded")
        s_const = sem("constants_ready")
        s_wm = sem("mamba_weights_loaded")
        s_wa = sem("attn_weights_loaded")
        s_we = sem("moe_weights_loaded")
        s_wtap = sem("taps_scaled")
        s_wps = sem("mamba_weights_turned")
        s_wsb = sem("mamba_weights_in_sbuf")
        s_wdp = sem("wdelta_product")
        s_wds = sem("wdelta_in_sbuf")
        s_var = sem("ln_variance")
        s_std = sem("ln_std")
        s_xn = sem("normalised_tokens")
        s_xtp = sem("turned_in_psum")
        s_xt = sem("turned_in_sbuf")
        s_wpad = sem("weight_pads_zeroed")
        s_pad = sem("mamba_pads_zeroed")
        s_apad = sem("attn_pads_set")
        s_in = sem("in_projected")
        s_u = sem("u_ready")
        s_zg = sem("z_gate_ready")
        s_bcp = sem("bc_projected")
        s_bch = sem("bc_parts")
        s_dlp = sem("delta_projected")
        s_abs = sem("delta_abs")
        s_ln1 = sem("delta_log")
        s_dl = sem("delta_ready")
        s_bb = sem("b_broadcast")
        s_cb = sem("c_broadcast")
        s_dcur = sem("chunk_delta_ready")
        s_da = sem("decay_ready")
        s_scan = sem("scan_done")
        s_dbu = sem("dbu_done")
        s_hc = sem("hc_ready")
        s_yac = sem("hc_accumulated")
        s_y = sem("y_gated")
        s_op = sem("out_projected")
        s_mo = sem("gated_out")
        s_mt = sem("out_turned")
        s_h1 = sem("h1_ready")

        w1n = part("tree", [P, 2, E])
        w1T = part("tree", [P, NDP])
        b2n = part("tree", [P, 2, E])
        w2q = [part("tree", [P, n * E]) for n in QN]
        ls = part("tree", [P, NT, DL])
        pw = part("tree", [P, NT, DL])
        pay = part("tree", [P, NT, PL])
        offs = part("tree", [1, NB * len(QN)], I32)
        cnt = part("tree", [P, NL], I32)
        nbf, cumend, base, onesf = [sq[:, k * NL // E:(k + 1) * NL // E, :].rearrange("p c e -> p (c e)")
                                    for k in range(4)]
        slot = part("tree", [P, NT])
        idf2 = part("tree", [P, 2, NT])
        cnt_row = part("tree", [1, NB], I32)
        slot_i = part("tree", [P, 3, NT], I32)
        tw0 = taken["tree"]
        sc = part("tree", [P, NT, NDP])
        mk = part("tree", [P, NT, NDP])
        tw1 = taken["tree"]
        pmT = part("tree", [P, 2, T])
        taken["tree"] = tw1
        ohb = part("tree", [P, NT, NL], BF16)
        pre = part("tree", [P, NT, NL], BF16)
        rank = part("tree", [P, NT, NL])
        taken["tree"] = tw0
        ob = part("tree", [P, TS, E])
        taken["tree"] = tw0 + NT * NDP
        xsb = part("tree", [P, TS, PL])
        taken["tree"] = tw1
        zz = part("tree", [P, 2, DL, E])
        zt = part("tree", [P, 2, DL // 2, P])
        res = cen
        slots_x = nc.dram_tensor("slots_x", (P * TS, PL), F32, kind="Internal").ap()
        slots_y = nc.dram_tensor("slots_y", (P * TS, E), F32, kind="Internal").ap()
        s_tpad = sem("tree_pads_zeroed")
        s_wt = sem("tree_weights_loaded")
        s_w2n = sem("tree_w2_loaded")
        s_w1p = sem("tree_w1_turned")
        s_w1T = sem("tree_w1_in_sbuf")
        s_sc = sem("tree_scores")
        s_sce = sem("tree_scores_in_sbuf")
        s_ls = sem("tree_path_scores")
        s_pw = sem("tree_path_weights")
        s_pm = sem("tree_node_weights")
        s_pmp = sem("tree_node_weights_turned")
        s_pmT = sem("tree_node_weights_in_sbuf")
        s_zero = sem("zeros_ready")
        zeros = dA[:, :, :].rearrange("p a b -> p (a b)")[:, 0:TS // 4 * PL]
        s_zf = sem("slots_zeroed")
        s_cnt = sem("leaf_counts")
        s_oh = sem("leaves_marked")
        s_rkp = sem("ranks_in_psum")
        s_slot = sem("slots_ready")
        s_lc = sem("leaf_of_block")
        s_lr = sem("leaf_of_block_turned")
        s_offs = sem("block_offsets_ready")
        s_pay = sem("payload_ready")
        s_scat = sem("payload_scattered")
        s_xs = sem("sorted_tokens_loaded")
        s_z = sem("z_ready")
        s_tz = sem("z_turned")
        s_zt = sem("turned_z_in_sbuf")
        s_blk = sem("tile_of_blocks_done")
        s_ob = sem("results_in_sbuf")
        s_obs = sem("results_stored")
        s_res = sem("results_gathered")
        s_sum = sem("tree_summed")
        s_h2 = sem("h2_ready")

        wqk = sb("wqk", [P, 2, NH * E])
        wv = sb("wv", [P, NH * E])
        wu = sb("wu", [E + 1, NH, E + 1])
        bub = sb("bub", [P, E])
        wpair = sb("wpair", [P, 2, P])
        wupair = sb("wupair", [E + 1, 2, E + 1])
        qa = part("attention", [P, 2, T])
        ka = part("attention", [P, 2, T])
        va = part("attention", [P, NT, 2, E + 1])
        mx = sb("mx", [P, 2, TPC, NCH])
        mx4 = sb("mx4", [P, 2, TPC])
        pt = part("attention", [P, 4, BANK])
        ot = sb("ot", [E + 1, BANK])
        rden = sb("rden", [P, 2, TPC])
        on = sb("on", [P, TPC, E])
        s_qs = sem("pair_weights_copied")
        s_qkp = sem("qk_projected")
        s_vp = sem("v_projected")
        s_qe = sem("q_in_sbuf")
        s_ke = sem("kv_in_sbuf")
        s_sm = sem("scores_for_max")
        s_mxd = sem("scores_max_taken")
        s_mx4 = sem("row_max_ready")
        s_mrp = sem("row_max_turned")
        s_mr = sem("row_max_in_q")
        s_st = sem("scores_turned")
        s_ex = sem("exp_done")
        s_av = sem("av_step")
        s_ot = sem("av_in_sbuf")
        s_pj = sem("head_projected")
        s_hd = sem("head_added")

        gw = sb("gw", [P, NE])
        w1 = sb("w1", [P, NE, FF])
        w2 = sb("w2", [FF, NE, E])
        b2 = sb("b2", [P, E])
        gamb = sb("gamb", [P, E])
        betb = sb("betb", [P, E])
        lg = sb("lg", [P, NT, NE])
        top = sb("top", [P, NT, 8])
        topi = sb("topi", [P, NT, 8], U32)
        topf = sb("topf", [P, NT, 2])
        tw = sb("tw", [P, 3, NT])
        ge = sb("ge", [P, NT, NE])
        ge2 = sb("ge2", [P, NT, NE])
        gT = part("moe", [P, T])
        hr = part("moe", [FF, 2, BANK])
        hg = part("moe", [FF, 2, BANK])
        yt = part("moe", [E, BANK])
        s_lg = sem("gate_logits")
        s_d = sem("top2_difference")
        s_e = sem("top2_exp")
        s_g = sem("gates_ready")
        s_gt = sem("gates_turned")
        s_gp = sem("gate_parts")
        s_m1 = sem("expert_up")
        s_gb = sem("gate_broadcast")
        s_rl = sem("expert_relu")
        s_hg = sem("expert_gated")
        s_m2 = sem("expert_down")
        s_mm = sem("moe_summed")
        s_yt = sem("moe_in_sbuf")
        s_ytp = sem("moe_turned")
        s_ya = sem("moe_added")
        s_fin = sem("result_ready")
        s_out = sem("result_stored")

        UNITS = [(h, ic) for ic in range(NCH) for h in range(2)]
        NSTEP = sum(4 * (ic + 1) for _, ic in UNITS)
        FIRST = [sum(4 * (ic + 1) for _, ic in UNITS[:n]) for n in range(len(UNITS) + 1)]

        block = ctx.enter_context(nc.Block())

        @block.sync
        def _(sp):
            def load(dst, src, s):
                sp.dma_start(dst, src).then_inc(s, 16)

            load(ids[:, :], a["x"].rearrange("b (c p) -> (b c) p", p=P), s_ids)
            col = lambda ap: ap.rearrange("(p o) -> p o", o=1)
            m = "L0_attn_"
            for dst, src in (
                (win[:, :, :], a[m + "in_proj_w"].rearrange("(k p) d -> p k d", p=P)),
                (convw[:, :], a[m + "conv_w"].rearrange("d o k -> d (o k)")),
                (convb[:, :], col(a[m + "conv_b"])), (xpw[:, :], a[m + "x_proj_w"]),
                (dtw[:, :], a[m + "dt_proj_w"]), (dtb[:, :], col(a[m + "dt_proj_b"])),
                (alog[:, :], a[m + "A_log"]), (dskip[:, :], col(a[m + "D"])),
                (outw[:, :], a[m + "out_proj_w"]), (gatew[:, :], a[m + "gate_w"]),
                (gateb[:, :], col(a[m + "gate_b"])),
                (gam[:, :], col(a[m + "ln_gamma"])), (bet[:, :], col(a[m + "ln_beta"])),
            ):
                load(dst, src, s_wm)
            sp.wait_ge(s_zero, 1)
            for t0 in range(0, TS, TS // 4):
                load(slots_x.rearrange("(p t) d -> p t d", t=TS)[:, t0:t0 + TS // 4, :],
                     zeros[:, :].rearrange("p (t d) -> p t d", d=PL), s_zf)
            sp.wait_ge(s_wpad, 1)
            row = lambda ap: ap.rearrange("(o n) -> o n", o=1)
            m = "L1_attn_"
            for dst, src in (
                (wqk[0:E, 0, :], a[m + "Wq"]), (wqk[0:E, 1, :], a[m + "Wk"]), (wv[0:E, :], a[m + "Wv"]),
                (wqk[E:E + 1, 0, :], row(a[m + "bq"])), (wqk[E:E + 1, 1, :], row(a[m + "bk"])),
                (wv[E:E + 1, :], row(a[m + "bv"])),
                (wu[0:E, :, 0:E], a[m + "Wu"].rearrange("(h e) n -> e h n", e=E)),
                (bub[:, :], a[m + "bu"].partition_broadcast(P)),
            ):
                load(dst, src, s_wa)
            m = "L1_ffn_"
            for dst, src in (
                (gw[0:E, :], a[m + "gate_w"]), (gw[E:E + 1, :], row(a[m + "gate_b"])),
                (w1[0:E, :, :], a[m + "w1"].rearrange("e d f -> d e f")),
                (w1[E:E + 1, :, :], a[m + "b1"].rearrange("(o e) f -> o e f", o=1)),
                (w2[:, :, :], a[m + "w2"].rearrange("e f d -> f e d")), (b2[0:NE, :], a[m + "b2"]),
                (gamb[:, :], a[m + "gamma"].partition_broadcast(P)),
                (betb[:, :], a[m + "beta"].partition_broadcast(P)),
            ):
                load(dst, src, s_we)
            sp.wait_ge(s_tpad, 1)
            m = "L0_ffn_"
            for dst, src in (
                (w1n[:, 0, :], a[m + "w1s"][0:P, :]), (w1n[0:ND - P, 1, :], a[m + "w1s"][P:ND, :]),
                (w1T[E:E + 1, 0:ND], row(a[m + "b1s"])),
                (b2n[:, 0, :], a[m + "b2s"][0:P, :]), (b2n[0:ND - P, 1, :], a[m + "b2s"][P:ND, :]),
            ):
                load(dst, src, s_wt)
            for q, n in enumerate(QN):
                load(w2q[q][0:E, :].rearrange("p (n o) -> p n o", o=E),
                     a[m + "w2s"][n - 1:2 * n - 1].rearrange("n d o -> d n o"), s_w2n)
                for h in range(2):
                    load(w2q[q][E:P, :].rearrange("p (n h o) -> p n h o", h=2, o=E)[:, :, h, :],
                         a[m + "w2s"][n // 2 - 1:n - 1].rearrange("n d o -> d n o"), s_w2n)
            sp.wait_ge(s_scat, NT * 16)
            load(xsb[:, :, :], slots_x.rearrange("(p t) d -> p t d", t=TS), s_xs)
            sp.wait_ge(s_ob, TS // 2 + SEED)
            load(slots_y.rearrange("(p t) d -> p t d", t=TS), ob[:, :, :], s_obs)
            sp.wait_ge(s_fin, 1)
            sp.dma_start(out.rearrange("b (c p) d -> p (b c) d", p=P), xn[:, :, :]).then_inc(s_out, 16)
            sp.wait_ge(s_out, 16)

        N_WM, N_WA, N_WE, N_WT, N_W2 = 13 * 16, 8 * 16, 8 * 16, 5 * 16, 3 * (DL // 2) * 16

        @block.gpsimd
        def _(pool):
            st = Steps(pool, step_g)
            st.did(pool.memset(ident[:, :], 0.0))
            st.after()
            pool.affine_select(out=ident[:, :], in_=ident[:, :], compare_op=ALU.not_equal, fill=1.0,
                               base=0, pattern=[[-1, P]], channel_multiplier=1).then_inc(s_ident, 1)
            pool.wait_ge(s_ident, 1)
            for t in (wqk[E:P], wv[E:P], gw[E:P], w1[E:P], b2[:, :]):
                st.did(pool.memset(t, 0.0))
                st.after()
            st.after()
            st.did(pool.memset(wu[:, :, :], 0.0))
            st.after()
            st.did(pool.memset(wu[E:E + 1, :, E:E + 1], 1.0))
            st.after()
            pool.sem_inc(s_wpad, 1)
            for t in (identb, mask_q, mask_k, nident):
                st.did(pool.memset(t[:, :], 0.0))
            st.did(pool.memset(sel[:, :, :], 0.0))
            st.did(pool.iota(iota_e[:, :], [[1, NE]], base=0, channel_multiplier=0,
                             allow_small_or_imprecise_dtypes=True))
            pool.wait_ge(s_rows, 1)
            st.after()
            for c in range(NT):
                pool.indirect_dma_start(
                    out=h0[:, c, :], out_offset=None,
                    in_=a["L0_tok_ple_table"].rearrange("v (k e) -> (v k) e", e=E),
                    in_offset=bass.IndirectOffsetOnAxis(ap=rows[:, c:c + 1], axis=0),
                ).then_inc(s_emb, 16)
            pool.memset(zeros, 0.0).then_inc(s_zero, 1)
            st.did(pool.memset(onesb[:, :], 1.0))
            st.did(pool.iota(iota_b[:, :], [[P, 2]], base=0, channel_multiplier=1,
                             allow_small_or_imprecise_dtypes=True))
            st.did(pool.memset(before[:, :], 1.0))
            st.after()
            st.did(pool.affine_select(out=before[:, :], in_=before[:, :], compare_op=ALU.is_gt, fill=0.0,
                                      base=0, pattern=[[1, P]], channel_multiplier=-1))
            for t, fill in ((identb, 1.0), (nident, -1.0)):
                st.did(pool.affine_select(out=t[:, :], in_=t[:, :], compare_op=ALU.not_equal, fill=fill,
                                          base=0, pattern=[[-1, P]], channel_multiplier=1))
            st.did(pool.affine_select(out=mask_q[:, :], in_=mask_q[:, :], compare_op=ALU.is_gt, fill=NEG,
                                      base=0, pattern=[[-1, P]], channel_multiplier=1))
            st.did(pool.affine_select(out=mask_k[:, :], in_=mask_k[:, :], compare_op=ALU.is_gt, fill=NEG,
                                      base=0, pattern=[[1, P]], channel_multiplier=-1))
            for part in range(3):
                st.after()
                st.did(pool.affine_select(out=sel[:, :, :], in_=sel[:, :, :], compare_op=ALU.not_equal,
                                          fill=1.0, base=-32 * part, pattern=[[-1, 32], [0, P]],
                                          channel_multiplier=1))
            st.after()
            pool.sem_inc(s_const, 1)
            pool.wait_ge(s_h1, 2 * NCH + SEED)
            for t in (w1T[:, :], b2n[:, :, :], w1n[:, 1, :]):
                st.did(pool.memset(t, 0.0))
                st.after()
            pool.sem_inc(s_tpad, 1)
            pool.wait_ge(s_zf, 4 * 16)
            pool.wait_ge(s_pay, 1)
            for c in range(NT):
                pool.indirect_dma_start(
                    out=slots_x, out_offset=bass.IndirectOffsetOnAxis(ap=rows[:, c:c + 1], axis=0),
                    in_=pay[:, c, :], in_offset=None).then_inc(s_scat, 16)
            pool.wait_ge(s_obs, 16)
            for c in range(NT):
                pool.indirect_dma_start(
                    out=res[:, c, :], out_offset=None, in_=slots_y,
                    in_offset=bass.IndirectOffsetOnAxis(ap=rows[:, c:c + 1], axis=0)).then_inc(s_res, 16)
            pool.wait_ge(s_h2, 1)
            st.did(pool.memset(qa[E:P, :, :], 0.0))
            st.did(pool.memset(ka[E:P, :, :], 0.0))
            st.after()
            st.did(pool.memset(va[:, :, :, E:E + 1], 1.0))
            st.after()
            pool.memset(ka[E:E + 1, :, :], 1.0).then_inc(s_apad, 1)
            pool.wait_ge(s_apad, 1)
            pool.wait_ge(s_wa, N_WA)
            with pool.Fori(0, NP) as p:
                pool.wait_ge(s_hd, p * len(UNITS) + SEED)
                pool.tensor_copy(wpair[:, :, :], wqk[:, :, bass.ds(p * P, P)]).then_inc(s_qs, 1)
                pool.tensor_copy(wupair[:, :, :], wu[:, bass.ds(p * 2, 2), :]).then_inc(s_qs, 1)

        @block.tensor
        def _(pe):
            for s in (s_yac, s_op, s_mt, s_av, s_pj, s_blk, s_tz, s_m2, s_ytp):
                pe.sem_inc(s, SEED)
            def turn_tokens(k):
                pe.wait_ge(s_xn, k + 1)
                for c in range(NT):
                    last = pe.transpose(ps[0:E, c // TPC, (c % TPC) * P:(c % TPC + 1) * P], xn[:, c, :], ident[:, :])
                    if c % TPC == TPC - 1:
                        last.then_inc(s_xtp, 1)

            pe.wait_ge(s_ident, 1)
            pe.wait_ge(s_idr, 1)
            pe.transpose(ps[:, 7, 0:NT], idr[:, :], ident[0:NT, 0:NT]).then_inc(s_idt, 1)
            pe.wait_ge(s_wm, N_WM)
            pe.wait_ge(s_wtap, 1)
            for k in range(2):
                pe.transpose(ps[:, 4, k * P:(k + 1) * P], wtap[:, 2 * k:2 * k + 2, :], ident[:, :])
            pe.transpose(ps[0:E, 4, 2 * P:3 * P], win[:, 1, :], ident[:, :])
            pe.transpose(ps[0:E, 4, 3 * P:3 * P + E], gatew[:, :], ident[0:E, 0:E])
            pe.transpose(ps[:, 5, 0:RK + 2 * DS], xpw[:, :], ident[0:RK + 2 * DS, 0:RK + 2 * DS])
            pe.transpose(ps[0:RK, 5, P:2 * P], dtw[:, :], ident[:, :])
            pe.transpose(ps[:, 5, 2 * P:2 * P + E], outw[:, :], ident[0:E, 0:E]).then_inc(s_wps, 1)
            pe.wait_ge(s_wsb, 1)
            pe.matmul(ps[:, 6, 0:DI], xpw[0:RK, :], dtwT[:, :], start=True, stop=True).then_inc(s_wdp, 1)

            turn_tokens(0)
            pe.wait_ge(s_wds, 1)
            for c in range(NCH):
                pe.wait_ge(s_xt, c + 1)
                if c == 0:
                    pe.wait_ge(s_pad, 1)
                if c >= 1:
                    pe.wait_ge(s_zg, c)
                b = 4
                for k in range(2):
                    pe.matmul(ps[:, b, :], wconv[:, k, :], x2[:, c * BANK + 3 - 2 * k:c * BANK + 3 - 2 * k + BANK],
                              start=(k == 0), stop=(k == 1))
                pe.matmul(ps[:, b + 1, :], wz[:, :], x2[:, c * BANK + 3:c * BANK + 3 + BANK], start=True, stop=True)
                pe.matmul(ps[0:E, b + 2, :], wg[:, :], x2[:, c * BANK + 3:c * BANK + 3 + BANK],
                          start=True, stop=True).then_inc(s_in, 1)
            pe.wait_ge(s_zg, NCH)
            for c in range(NCH):
                us = u[:, c * BANK:(c + 1) * BANK]
                if c >= 2:
                    pe.wait_ge(s_abs, c - 1)
                    pe.wait_ge(s_dl, c - 1)
                    pe.wait_ge(s_bch, c - 1)
                pe.matmul(ps[:, 6 + c % 2, :], wdelta[:, :], us, start=True, stop=True).then_inc(s_dlp, 1)
                pe.matmul(ps[0:2 * DS, c % 2, :], wbc[:, :], us, start=True, stop=True).then_inc(s_bcp, 1)

            pe.wait_ge(s_const, 1)
            pe.wait_ge(s_dl, NCH)
            pe.wait_ge(s_bch, NCH)
            with pe.Fori(0, NCH) as c:
                for s in range(DS + 1):
                    if s < DS:
                        if s >= 2:
                            pe.wait_ge(s_dbu, c * DS + s - 1 + SEED)
                            pe.wait_ge(s_hc, c * DS + s - 1 + SEED)
                        else:
                            pe.wait_ge(s_dbu, c * DS + SEED)
                            pe.wait_ge(s_hc, c * DS + SEED)
                        mv = bc[:, bass.ds(c * BANK, BANK)]
                        pe.matmul(ps[:, s % 2, :], sel[:, s, :], mv, start=True, stop=True).then_inc(s_bb, 1)
                        pe.matmul(ps[:, 2 + s % 2, :], sel[:, DS + s, :], mv, start=True, stop=True).then_inc(s_cb, 1)
                    if s >= 1:
                        if s == 1:
                            pe.wait_ge(s_y, c + SEED)
                        pe.wait_ge(s_hc, c * DS + s + SEED)
                        pe.matmul(ps[:, 4, :], ident[:, :], hc[:, (s - 1) % 2, :], start=(s == 1), stop=(s == DS))\
                          .then_inc(s_yac, 1)
                pe.wait_ge(s_y, c + 1 + SEED)
                pe.matmul(ps[0:E, 5, :], woT[:, :], yb[:, 1, :], start=True, stop=True).then_inc(s_op, 1)
                pe.wait_ge(s_mo, c + 1 + SEED)
                for r in range(TPC):
                    last = pe.matmul(ps[:, 6, r * E:(r + 1) * E], mo[:, r * P:(r + 1) * P], ident[0:E, 0:E],
                                     start=True, stop=True)
                last.then_inc(s_mt, 1)

            turn_tokens(1)
            pe.wait_ge(s_wt, N_WT)
            for k in range(2):
                m = pe.transpose(ps[0:E, 7, k * P:(k + 1) * P], w1n[:, k, :], ident[:, :])
            m.then_inc(s_w1p, 1)
            pe.wait_ge(s_w1T, 1)
            pe.wait_ge(s_xt, 2 * NCH)
            for c in range(NT):
                pe.matmul(ps[:, (4 + c // 2) % 8, (c % 2) * NDP:(c % 2) * NDP + ND], xt[:, c * P:(c + 1) * P],
                          w1T[:, 0:ND], start=True, stop=True).then_inc(s_sc, 1)
            pe.wait_ge(s_oh, 1)
            pe.wait_ge(s_sce, NT // 2)
            pe.matmul(ps[:, 6, 0:NL], onesb[:, :], pre[:, NT - 1, :], start=True, stop=True).then_inc(s_cnt, 1)
            for c in range(NT):
                dst = ps[:, c // TPC, (c % TPC) * NL:(c % TPC + 1) * NL]
                m = pe.matmul(dst, before[:, :], ohb[:, c, :], start=True, stop=c == 0)
                if c:
                    m = pe.matmul(dst, onesb[:, :], pre[:, c - 1, :], start=False, stop=True)
            m.then_inc(s_rkp, 1)
            pe.wait_ge(s_lc, 1)
            for k in range(2):
                m = pe.matmul(ps[0:1, 7, k * P:(k + 1) * P], nbf[:, k:k + 1], ident[:, :], start=True, stop=True)
            m.then_inc(s_lr, 1)
            pe.wait_ge(s_offs, 1)
            pe.wait_ge(s_slot, 1)
            pe.wait_ge(s_sce, NT // 2)
            pe.wait_ge(s_pm, 1)
            for k in range(2):
                for c in range(NT):
                    m = pe.transpose(ps[:, 4 * k + c // TPC, (c % TPC) * P:(c % TPC + 1) * P],
                                     sc[:, c, k * P:(k + 1) * P], ident[:, :])
                    if c % TPC == TPC - 1:
                        m.then_inc(s_pmp, 1)
            pe.wait_ge(s_pmT, 8)
            for c in range(NT):
                for k in range(2):
                    m = pe.matmul(ps[:, 4 + c // 8, (c % 8) * E:(c % 8 + 1) * E], pmT[:, k, c * P:(c + 1) * P],
                                  b2n[:, k, :], start=(k == 0), stop=(k == 1))
            m.then_inc(s_sum, 1)
            pe.wait_ge(s_w2n, N_W2)
            BT, NQ = P // BLK, len(QN)
            place = [pe.alloc_register(f"place{i}") for i in range(BT * NQ)]
            with pe.Fori(0, TS // 8) as it:
                for v in range(9):
                    if v < 8:
                        pe.wait_ge(s_zt, (it * 8 + v - 1 if v >= 2 else it * 8) + SEED)
                        pe.wait_ge(s_z, it * 8 + v + 1)
                        for q in range(NQ):
                            m = pe.matmul(ps[:, v % 2, q * P:(q + 1) * P],
                                          zz[:, v % 2, 2 * q:2 * q + 2, :].rearrange("p k e -> p (k e)"),
                                          ident[:, :], start=True, stop=True)
                        m.then_inc(s_tz, 1)
                    if v >= 1:
                        w = v - 1
                        pe.load(place, offs[0:1, bass.ds(it * (8 * BT * NQ) + w * BT * NQ, BT * NQ)])
                        if w % 2 == 0:
                            pe.wait_ge(s_ob, (it * 4 + w // 2 - 1 if w >= 4 else it * 4) + SEED)
                        pe.wait_ge(s_zt, it * 8 + w + 1 + SEED)
                        for b in range(BT):
                            for q in range(NQ):
                                o = pe.snap(place[b * NQ + q], min_val=0, max_val=(QN[q] - 1) * E)
                                m = pe.matmul(ps[0:BLK, 2 + (w // 2) % 2, ((w % 2) * BT + b) * E:((w % 2) * BT + b + 1) * E],
                                              zt[:, w % 2, q, b * BLK:(b + 1) * BLK], w2q[q][:, bass.ds(o, E)],
                                              start=(q == 0), stop=(q == NQ - 1))
                        m.then_inc(s_blk, 1)

            turn_tokens(2)
            pe.wait_ge(s_xt, 3 * NCH)
            pe.wait_ge(s_wa, N_WA)

            def scores_max(p, n, k):
                h, ic = UNITS[n]
                g = FIRST[n] + k
                r, jc = divmod(k, ic + 1)
                w = BANK if jc < ic else (r + 1) * P
                q0 = ic * BANK + r * P
                pe.wait_ge(s_mxd, (p * NSTEP + g - 1 if g >= 2 else p * NSTEP) + SEED)
                m = pe.matmul(ps[:, g % 2, 0:w], qa[:, h, q0:q0 + P], ka[:, h, jc * BANK:jc * BANK + w],
                              start=True, stop=jc < ic)
                if jc == ic:
                    m = pe.matmul(ps[:, g % 2, r * P:(r + 1) * P], identb[:, :], mask_q[:, :], start=False, stop=True)
                m.then_inc(s_sm, 1)

            def scores_turned(p, n, k):
                h, ic = UNITS[n]
                g = FIRST[n] + k
                lo = max(0, k - 4 * ic) * P
                bank = 2 + g % 4
                pe.wait_ge(s_ex, (p * NSTEP + g - 3 if g >= 4 else p * NSTEP) + SEED)
                m = pe.matmul(ps[:, bank, lo:BANK], ka[:, h, k * P:(k + 1) * P],
                              qa[:, h, ic * BANK + lo:(ic + 1) * BANK], start=True, stop=k < 4 * ic)
                if k >= 4 * ic:
                    m = pe.matmul(ps[:, bank, lo:lo + P], identb[:, :], mask_k[:, :], start=False, stop=True)
                m.then_inc(s_st, 1)

            def values(p, n, k):
                h, ic = UNITS[n]
                g = FIRST[n] + k
                lo = max(0, k - 4 * ic) * P
                if k == 0:
                    pe.wait_ge(s_ot, p * len(UNITS) + n + SEED)
                pe.wait_ge(s_ex, p * NSTEP + g + 1 + SEED)
                m = pe.matmul(ps[0:E + 1, 6, lo:BANK], va[:, k, h, :], pt[:, g % 4, lo:BANK],
                              start=(k == 0), stop=(k == 4 * ic + 3))
                m.then_inc(s_av, 1)

            def project(p, n):
                pe.wait_ge(s_ot, p * len(UNITS) + n + 1 + SEED)
                pe.wait_ge(s_hd, p * len(UNITS) + n + SEED)
                for r in range(TPC):
                    m = pe.matmul(ps[:, 7, r * (E + 1):(r + 1) * (E + 1)], ot[:, r * P:(r + 1) * P],
                                  wupair[:, UNITS[n][0], :], start=True, stop=True)
                m.then_inc(s_pj, 1)

            with pe.Fori(0, NP) as p:
                pe.wait_ge(s_qs, p * 2 + 2)
                pe.wait_ge(s_hd, p * len(UNITS) + SEED)
                for t in range(2):
                    for c in range(NCH):
                        pe.matmul(ps[:, t * 4 + c, :], wpair[:, t, :], xt[:, c * BANK:(c + 1) * BANK],
                                  start=True, stop=True).then_inc(s_qkp, 1)
                for c in range(NCH):
                    pe.wait_ge(s_qe, p * NCH + c + 1)
                    for r in range(TPC):
                        m = pe.matmul(ps[:, c, r * P:(r + 1) * P], xt[:, (c * TPC + r) * P:(c * TPC + r + 1) * P],
                                      wv[:, bass.ds(p * P, P)], start=True, stop=True)
                    m.then_inc(s_vp, 1)
                pe.wait_ge(s_ke, p * (2 * NCH + 1) + 2 * NCH + 1 + SEED)
                for k in range(4 * (UNITS[0][1] + 1)):
                    scores_max(p, 0, k)
                for n, (h, ic) in enumerate(UNITS):
                    pe.wait_ge(s_mx4, p * len(UNITS) + n + 1 + SEED)
                    if n >= 1:
                        pe.wait_ge(s_hd, p * len(UNITS) + n - 1 + SEED)
                    for r in range(TPC):
                        m = pe.matmul(ps[0:1, 7, r * P:(r + 1) * P], mx4[:, n % 2, r:r + 1], nident[:, :],
                                      start=True, stop=True)
                    m.then_inc(s_mrp, 1)
                    ns = 4 * (UNITS[n + 1][1] + 1) if n + 1 < len(UNITS) else 0
                    nt = 4 * (ic + 1)
                    for k in range(max(ns, nt + 4)):
                        if k < ns:
                            scores_max(p, n + 1, k)
                        if k == 1:
                            pe.wait_ge(s_mr, p * len(UNITS) + n + 1 + SEED)
                        if k == 3 and n >= 1:
                            project(p, n - 1)
                        if 1 <= k <= nt:
                            scores_turned(p, n, k - 1)
                        if 3 <= k < nt + 3:
                            values(p, n, k - 3)
                project(p, len(UNITS) - 1)

            turn_tokens(3)
            pe.wait_ge(s_xt, 4 * NCH)
            pe.wait_ge(s_we, N_WE)
            for c in range(NT):
                m = pe.matmul(ps[:, 4, c * NE:(c + 1) * NE], xt[:, c * P:(c + 1) * P], gw[:, :], start=True, stop=True)
            m.then_inc(s_lg, 1)
            pe.wait_ge(s_g, 1)
            for c in range(NT):
                m = pe.transpose(ps[0:NE, c // TPC, (c % TPC) * P:(c % TPC + 1) * P], ge[:, c, :], ident[:, :])
                if c % TPC == TPC - 1:
                    m.then_inc(s_gt, 1)
            pe.wait_ge(s_gp, NCH)
            with pe.Fori(0, NCH) as c:
                for e in range(NE + 1):
                    if e < NE:
                        pe.wait_ge(s_hg, (c * NE + e - 1 if e >= 2 else c * NE) + SEED)
                        pe.matmul(ps[:, e % 2, :], w1[:, e, :], xt[:, bass.ds(c * BANK, BANK)],
                                  start=True, stop=True).then_inc(s_m1, 1)
                        pe.matmul(ps[:, 2 + e % 2, :], sel[:, e, :], bc[:, bass.ds(c * BANK, BANK)],
                                  start=True, stop=True).then_inc(s_gb, 1)
                    if e == 0:
                        pe.wait_ge(s_yt, c + SEED)
                        pe.matmul(ps[0:E, 4, :], b2[:, :], gT[:, bass.ds(c * BANK, BANK)], start=True, stop=False)
                    else:
                        pe.wait_ge(s_hg, c * NE + e + SEED)
                        pe.matmul(ps[0:E, 4, :], w2[:, e - 1, :], hg[:, (e - 1) % 2, :],
                                  start=False, stop=(e == NE)).then_inc(s_m2, 1)
                pe.wait_ge(s_yt, c + 1 + SEED)
                pe.wait_ge(s_ya, c + SEED)
                for r in range(TPC):
                    m = pe.matmul(ps[:, 5, r * E:(r + 1) * E], yt[:, r * P:(r + 1) * P], ident[0:E, 0:E],
                                  start=True, stop=True)
                m.then_inc(s_ytp, 1)

        @block.scalar
        def _(act):
            for s in (s_zt, s_ex, s_ot, s_yt):
                act.sem_inc(s, SEED)
            def ln_std(k):
                act.wait_ge(s_var, k + 1)
                act.activation(stat[:, 3, :], stat[:, 2, :], ACT.Sqrt).then_inc(s_std, 1)

            def turned(k):
                for c in range(NCH):
                    act.wait_ge(s_xtp, k * NCH + c + 1)
                    act.activation(xt[0:E, c * BANK:(c + 1) * BANK], ps[0:E, c, :], ACT.Copy).then_inc(s_xt, 1)

            act.wait_ge(s_wm, N_WM)
            act.activation(neg_a[:, :], alog[:, :], ACT.Exp).then_inc(step_s, 1)
            act.wait_ge(step_s, 1)
            act.mul(neg_a[:, :], neg_a[:, :], -1.0).then_inc(step_s, 1)
            act.wait_ge(s_pad, 1)
            act.wait_ge(s_wps, 1)
            for dst, src in (
                (dtwT[:, :], ps[0:RK, 5, P:2 * P]),
                (wconv[:, :, :], ps[:, 4, 0:2 * P].rearrange("p (k n) -> p k n", k=2)),
                (wz[0:E, :], ps[0:E, 4, 2 * P:3 * P]), (wg[0:E, :], ps[0:E, 4, 3 * P:3 * P + E]),
                (wbc[:, :], ps[:, 5, RK:RK + 2 * DS]), (woT[:, :], ps[:, 5, 2 * P:2 * P + E]),
            ):
                last = act.activation(dst, src, ACT.Copy)
            last.then_inc(s_wsb, 1)
            act.wait_ge(s_wdp, 1)
            act.activation(wdelta[:, :], ps[:, 6, 0:DI], ACT.Copy).then_inc(s_wds, 1)
            ln_std(0)
            ln_std(1)
            for c in range(NCH):
                act.wait_ge(s_xtp, c + 1)
                act.activation(x2[0:E, 3 + c * BANK:3 + (c + 1) * BANK], ps[0:E, c, :], ACT.Identity,
                               bias=bet[:, :], scale=gam[:, :])
                act.activation(x2[E:P, 4 + c * BANK:4 + (c + 1) * BANK], ps[0:E, c, :], ACT.Identity,
                               bias=bet[:, :], scale=gam[:, :]).then_inc(s_xt, 1)
            for c in range(NCH):
                cs = slice(c * BANK, (c + 1) * BANK)
                act.wait_ge(s_in, c + 1)
                act.activation(u[:, cs], ps[:, 4, :], ACT.Silu, bias=convb[:, :]).then_inc(s_u, 1)
                act.activation(sz[:, cs], ps[:, 5, :], ACT.Silu)
                act.activation(gsig[:, cs], ps[0:E, 6, :], ACT.Identity, bias=gateb[:, :]).then_inc(s_zg, 1)
            act.wait_ge(s_zg, NCH)
            act.activation(gsig[:, :], gsig[:, :], ACT.Sigmoid).then_inc(s_zg, 1)
            for c in range(NCH):
                act.wait_ge(s_dlp, c + 1)
                if c >= 2:
                    act.wait_ge(s_dl, c - 1)
                b = spl[:, c % 2, :]
                act.activation(b, ps[:, 6 + c % 2, :], ACT.Abs, bias=dtb[:, :]).then_inc(s_abs, 1)
                act.wait_ge(s_abs, c + 1)
                act.activation(b, b, ACT.Exp, scale=-1.0).then_inc(step_s, 1)
                act.wait_ge(step_s, 3 + c)
                act.activation(b, b, ACT.Ln, bias=1.0).then_inc(s_ln1, 1)
            act.wait_ge(s_zf, 4 * 16)
            with act.Fori(0, NCH) as c:
                for s in range(DS):
                    if s == 0:
                        act.wait_ge(s_dcur, c + 1)
                    act.wait_ge(s_scan, (c * DS + s - 1 if s >= 2 else c * DS) + SEED)
                    act.activation(dA[:, s % 2, :], dcur[:, :], ACT.Exp,
                                   scale=neg_a[:, s:s + 1]).then_inc(s_da, 1)

            ln_std(2)
            act.wait_ge(s_w1p, 1)
            act.activation(w1T[0:E, 0:ND], ps[0:E, 7, 0:ND], ACT.Copy).then_inc(s_w1T, 1)
            turned(1)
            for b in range(NT // 2):
                act.wait_ge(s_sc, 2 * b + 2)
                act.activation(sc[:, 2 * b:2 * b + 2, 0:ND],
                               ps[:, (4 + b) % 8, :].rearrange("p (c n) -> p c n", n=NDP)[:, :, 0:ND], ACT.Copy)\
                   .then_inc(s_sce, 1)
            act.wait_ge(s_ls, 1)
            act.activation(ls[:, :, :], ls[:, :, :], ACT.Abs).then_inc(s_pw, 1)
            act.wait_ge(s_pw, 1)
            act.activation(pw[:, :, :], ls[:, :, :], ACT.Gelu).then_inc(s_pw, 1)
            for b in range(8):
                act.wait_ge(s_pmp, b + 1)
                act.activation(pmT[:, b // 4, (b % 4) * BANK:(b % 4 + 1) * BANK], ps[:, b, :], ACT.Copy)\
                   .then_inc(s_pmT, 1)
            act.wait_ge(s_sum, 1)
            with act.Fori(0, TS // 8) as it:
                for v in range(8):
                    act.wait_ge(s_tz, it * 8 + v + 1 + SEED)
                    act.wait_ge(s_blk, (it * 8 + v - 1 if v >= 2 else it * 8) + SEED)
                    act.activation(zt[:, v % 2, :, :].rearrange("p q s -> p (q s)"), ps[:, v % 2, :], ACT.Copy)\
                       .then_inc(s_zt, 1)

            ln_std(3)
            turned(2)
            with act.Fori(0, NP) as p:
                for c in range(NCH):
                    act.wait_ge(s_qkp, p * 2 * NCH + c + 1)
                    act.activation(qa[0:E, 0, c * BANK:(c + 1) * BANK], ps[0:E, c, :], ACT.Copy, scale=float(E) ** -0.5)
                    act.activation(qa[0:E, 1, c * BANK:(c + 1) * BANK], ps[E:P, c, :], ACT.Copy,
                                   scale=float(E) ** -0.5).then_inc(s_qe, 1)
                for n, (h, ic) in enumerate(UNITS):
                    for k in range(4 * (ic + 1)):
                        g = FIRST[n] + k
                        lo = max(0, k - 4 * ic) * P
                        act.wait_ge(s_st, p * NSTEP + g + 1)
                        act.wait_ge(s_av, (p * NSTEP + g - 3 if g >= 4 else p * NSTEP) + SEED)
                        act.activation(pt[:, g % 4, lo:BANK], ps[:, 2 + g % 4, lo:BANK], ACT.Exp).then_inc(s_ex, 1)
                    act.wait_ge(s_av, p * NSTEP + FIRST[n + 1] + SEED)
                    if n >= 1:
                        act.wait_ge(s_pj, p * len(UNITS) + n + SEED)
                    else:
                        act.wait_ge(s_pj, p * len(UNITS) + SEED)
                    act.activation(ot[:, :], ps[0:E + 1, 6, :], ACT.Copy).then_inc(s_ot, 1)

            ln_std(4)
            turned(3)
            act.wait_ge(s_d, 1)
            act.activation(tw[:, 1, :], tw[:, 0, :], ACT.Exp).then_inc(s_e, 1)
            with act.Fori(0, NCH) as c:
                for e in range(NE):
                    act.wait_ge(s_m1, c * NE + e + 1)
                    act.wait_ge(s_hg, (c * NE + e - 1 if e >= 2 else c * NE) + SEED)
                    act.activation(hr[:, e % 2, :], ps[:, e % 2, :], ACT.Relu).then_inc(s_rl, 1)
                act.wait_ge(s_m2, c * NE + NE + SEED)
                act.wait_ge(s_ytp, c + SEED)
                act.activation(yt[:, :], ps[0:E, 4, :], ACT.Copy).then_inc(s_yt, 1)
            ln_std(5)

        @block.vector
        def _(dve):
            st = Steps(dve, step_v)
            for s in (s_dbu, s_hc, s_y, s_h1, s_mxd, s_mx4, s_hd,
                      s_ob, s_hg, s_ya, s_scan, s_mr, s_mo, s_ke):
                dve.sem_inc(s, SEED)

            def wide(col):
                return col.unsqueeze(2).to_broadcast([P, NT, E])

            def layernorm(src, dst, k):
                st.after()
                st.did(dve.tensor_reduce(stat[:, 0, :], src, AX_X, ALU.add))
                st.after()
                st.did(dve.tensor_scalar(stat[:, 0, :], stat[:, 0, :], -1.0 / E, None, ALU.mult))
                st.after()
                st.did(dve.tensor_tensor(cen[:, :, :], src, wide(stat[:, 0, :]), ALU.add))
                st.after()
                st.did(dve.tensor_tensor(sq[:, :, :], cen[:, :, :], cen[:, :, :], ALU.mult))
                st.after()
                st.did(dve.tensor_reduce(stat[:, 1, :], sq[:, :, :], AX_X, ALU.add))
                st.after()
                dve.tensor_scalar(stat[:, 2, :], stat[:, 1, :], 1.0 / E, EPS, ALU.mult, ALU.add).then_inc(s_var, 1)
                dve.wait_ge(s_std, k + 1)
                st.did(dve.reciprocal(stat[:, 4, :], stat[:, 3, :]))
                st.after()
                st.did(dve.tensor_tensor(dst, cen[:, :, :], wide(stat[:, 4, :]), ALU.mult))

            dve.wait_ge(s_ids, 16)
            dve.tensor_copy(idr[:, :], ids[:, :]).then_inc(s_idr, 1)
            dve.wait_ge(s_idt, 1)
            st.did(dve.tensor_copy(idf[:, 0, :], ps[:, 7, 0:NT]))
            st.after()
            st.did(dve.tensor_scalar(idf[:, 1, :], idf[:, 0, :], 0.0, float(V), ALU.is_lt, ALU.mult))
            st.after()
            st.did(dve.tensor_tensor(idf[:, 0, :], idf[:, 0, :], idf[:, 1, :], ALU.add))
            st.after()
            st.did(dve.tensor_scalar(idf[:, 0, :], idf[:, 0, :], 0.0, float(V - 1), ALU.max, ALU.min))
            st.after()
            dve.tensor_scalar(rows[:, :], idf[:, 0, :], float(HID // E), float(LAYER), ALU.mult, ALU.add)\
               .then_inc(s_rows, 1)
            for t in (x2[:, 0:4], wz[E:P, :], wg[E:P, :], hs[:, :, 0:1], xt[E:P, :]):
                st.did(dve.memset(t, 0.0))
            st.after()
            st.did(dve.memset(xt[E:E + 1, :], 1.0))
            st.after()
            dve.sem_inc(s_pad, 1)
            dve.wait_ge(s_wm, N_WM)
            for k in range(KC):
                st.did(dve.tensor_scalar(wtap[:, k, :], win[:, 0, :], convw[:, KC - 1 - k:KC - k], None, ALU.mult))
            st.after()
            dve.sem_inc(s_wtap, 1)

            dve.wait_ge(s_emb, NT * 16)
            layernorm(h0[:, :, :], xn[:, :, :], 0)
            st.after()
            st.did(dve.tensor_tensor(h1[:, :, :], h0[:, :, :], xn[:, :, :], ALU.add))
            layernorm(xn[:, :, :], xn[:, :, :], 1)
            st.after()
            dve.sem_inc(s_xn, 1)
            for c in range(NCH):
                cs = slice(c * BANK, (c + 1) * BANK)
                dve.wait_ge(s_abs, c + 1)
                st.did(dve.tensor_scalar(delta[:, cs], ps[:, 6 + c % 2, :], dtb[:, :], 0.0, ALU.add, ALU.max))
                dve.wait_ge(s_bcp, c + 1)
                st.did(dve.tensor_copy(bc[0:32, cs], ps[0:32, c % 2, :]))
                st.after()
                st.did(dve.tensor_tensor(res1[:, :], ps[0:32, c % 2, :], bc[0:32, cs], ALU.subtract))
                st.after()
                st.did(dve.tensor_copy(mid[:, :], res1[:, :]))
                st.after()
                st.did(dve.tensor_tensor(res2[:, :], res1[:, :], mid[:, :], ALU.subtract))
                st.did(dve.tensor_copy(bc[32:64, cs], mid[:, :]))
                st.after()
                dve.tensor_copy(bc[64:96, cs], res2[:, :]).then_inc(s_bch, 1)
                dve.wait_ge(s_ln1, c + 1)
                st.did(dve.tensor_tensor(delta[:, cs], delta[:, cs], spl[:, c % 2, :], ALU.add))
                st.after()
                dve.wait_ge(s_u, c + 1)
                dve.tensor_tensor(du[:, cs], delta[:, cs], u[:, cs], ALU.mult).then_inc(s_dl, 1)
            dve.wait_ge(s_dl, NCH)
            dve.wait_ge(s_zg, NCH + 1)
            n0 = st.n
            with dve.Fori(0, NCH) as c:
                cd = bass.ds(c * BANK, BANK)
                dve.tensor_copy(dcur[:, :], delta[:, cd]).then_inc(s_dcur, 1)
                for s in range(DS + 1):
                    if s < DS:
                        dve.wait_ge(s_bb, c * DS + s + 1)
                        dve.tensor_tensor(dbu[:, s % 2, :], du[:, cd], ps[:, s % 2, :], ALU.mult).then_inc(s_dbu, 1)
                    if s >= 1:
                        dve.wait_ge(s_cb, c * DS + s)
                        dve.wait_ge(s_scan, c * DS + s + SEED)
                        dve.wait_ge(s_yac, (c * DS + s - 2 if s >= 3 else c * DS) + SEED)
                        dve.tensor_tensor(hc[:, (s - 1) % 2, :], hs[:, s - 1, 1:BANK + 1], ps[:, 2 + (s - 1) % 2, :],
                                          ALU.mult).then_inc(s_hc, 1)
                    if s < DS:
                        dve.wait_ge(s_da, c * DS + s + 1)
                        dve.wait_ge(s_dbu, c * DS + s + 1 + SEED)
                        if s == 0:
                            dve.wait_ge(s_h1, c * 2 + SEED)
                        dve.tensor_tensor_scan(hs[:, s, 1:BANK + 1], dA[:, s % 2, :], dbu[:, s % 2, :],
                                               hs[:, s, 0:1], ALU.mult, ALU.add).then_inc(s_scan, 1)
                dve.wait_ge(s_hc, c * DS + DS + SEED)
                dve.tensor_copy(hs[:, :, 0:1], hs[:, :, BANK:BANK + 1]).then_inc(s_h1, 1)
                dve.wait_ge(s_yac, c * DS + DS + SEED)
                dve.scalar_tensor_tensor(yb[:, 0, :], u[:, cd], dskip[:, :], ps[:, 4, :], ALU.mult, ALU.add)\
                   .then_inc(step_v, 1)
                dve.wait_ge(step_v, n0 + c * 1 + 1)
                dve.wait_ge(s_op, c + SEED)
                dve.tensor_tensor(yb[:, 1, :], yb[:, 0, :], sz[:, cd], ALU.mult).then_inc(s_y, 1)
                dve.wait_ge(s_op, c + 1 + SEED)
                dve.wait_ge(s_mt, c + SEED)
                dve.tensor_tensor(mo[:, :], ps[0:E, 5, :], gsig[:, cd], ALU.mult).then_inc(s_mo, 1)
                dve.wait_ge(s_mt, c + 1 + SEED)
                hv = h1[:, bass.ds(c * TPC, TPC), :]
                dve.tensor_tensor(hv, hv, ps[:, 6, 0:TPC * E].rearrange("p (r e) -> p r e", e=E), ALU.add)\
                   .then_inc(s_h1, 1)
            st.n = n0 + NCH
            dve.wait_ge(s_h1, 2 * NCH + SEED)

            layernorm(h1[:, :, :], xn[:, :, :], 2)
            st.after()
            dve.sem_inc(s_xn, 1)
            st.did(dve.memset(mk[:, :, 0:1], 1.0))
            st.did(dve.memset(mk[:, :, ND:NDP], 0.0))
            dve.wait_ge(s_sce, NT // 2)
            st.did(dve.memset(sc[:, :, ND:NDP], 0.0))
            for i in range(DL - 1):
                lo, n = 2 ** i - 1, 2 ** i
                kids = mk[:, :, 2 * lo + 1:2 * lo + 1 + 2 * n].rearrange("p c (n h) -> p c n h", h=2)
                left, right = kids[:, :, :, 0], kids[:, :, :, 1]
                st.after()
                st.did(dve.scalar_tensor_tensor(right, sc[:, :, lo:lo + n], 0.0, mk[:, :, lo:lo + n],
                                                ALU.is_gt, ALU.mult))
                st.after()
                st.did(dve.tensor_tensor(left, mk[:, :, lo:lo + n], right, ALU.subtract))
            st.after()
            leaf = mk[:, :, NL - 1:ND]
            st.did(dve.tensor_copy(ohb[:, :, :], leaf))
            st.did(dve.tensor_copy(pre[:, 0, :], mk[:, 0, NL - 1:ND]))
            for c in range(1, NT):
                st.after()
                st.did(dve.tensor_tensor(pre[:, c, :], pre[:, c - 1, :], ohb[:, c, :], ALU.add))
            st.after()
            dve.sem_inc(s_oh, 1)
            st.did(dve.tensor_tensor(sc[:, :, :], sc[:, :, :], mk[:, :, :], ALU.mult))
            st.after()
            for i in range(DL):
                lo, n = 2 ** i - 1, 2 ** i
                st.did(dve.tensor_reduce(ls[:, :, DL - 1 - i:DL - i].rearrange("p c o -> p (c o)"), sc[:, :, lo:lo + n],
                                         AX_X, ALU.add))
            st.after()
            dve.sem_inc(s_ls, 1)
            st.did(dve.memset(onesf[:, :], 1.0))
            dve.wait_ge(s_cnt, 1)
            st.did(dve.tensor_scalar(cnt[:, :], ps[:, 6, 0:NL], float(BLK - 1), None, ALU.add))
            st.after()
            st.did(dve.tensor_scalar(cnt[:, :], cnt[:, :], SH, None, ALU.logical_shift_right))
            st.after()
            st.did(dve.tensor_copy(nbf[:, :], cnt[:, :]))
            st.after()
            st.did(dve.tensor_tensor_scan(cumend[:, :], onesf[:, :], nbf[:, :], 0.0, ALU.mult, ALU.add))
            st.after()
            st.did(dve.tensor_tensor(base[:, :], cumend[:, :], nbf[:, :], ALU.subtract))
            st.after()
            st.did(dve.tensor_scalar(base[:, :], base[:, :], float(BLK), None, ALU.mult))
            dve.wait_ge(s_const, 1)
            for k in range(2):
                st.after()
                st.did(dve.tensor_scalar(onesf[:, :], cumend[:, :], iota_b[:, k:k + 1], None, ALU.is_le))
                st.after()
                st.did(dve.tensor_reduce(nbf[:, k:k + 1], onesf[:, :], AX_X, ALU.add))
            st.after()
            dve.tensor_scalar(nbf[:, 0:2], nbf[:, 0:2], float(NL - 1), None, ALU.min).then_inc(s_lc, 1)
            dve.wait_ge(s_rkp, 1)
            for c in range(NCH):
                st.did(dve.tensor_tensor(rank[:, c * TPC:(c + 1) * TPC, :], ps[:, c, :].rearrange("p (r n) -> p r n", n=NL),
                                         base[:, :].unsqueeze(1).to_broadcast([P, TPC, NL]), ALU.add))
            st.after()
            st.did(dve.tensor_tensor(rank[:, :, :], rank[:, :, :], leaf, ALU.mult))
            st.after()
            st.did(dve.tensor_reduce(slot[:, :], rank[:, :, :], AX_X, ALU.add))
            st.after()
            st.did(dve.tensor_copy(slot_i[:, 0, :], slot[:, :]))
            st.after()
            st.did(dve.tensor_scalar(slot_i[:, 1, :], slot_i[:, 0, :], P.bit_length() - 1, None, ALU.logical_shift_right))
            st.did(dve.tensor_scalar(slot_i[:, 2, :], slot_i[:, 0, :], P - 1, None, ALU.bitwise_and))
            st.after()
            st.did(dve.tensor_copy(idf2[:, 0, :], slot_i[:, 1, :]))
            st.did(dve.tensor_copy(idf2[:, 1, :], slot_i[:, 2, :]))
            st.after()
            st.did(dve.scalar_tensor_tensor(slot[:, :], idf2[:, 1, :], float(TS), idf2[:, 0, :], ALU.mult, ALU.add))
            st.after()
            st.did(dve.tensor_copy(rows[:, :], slot[:, :]))
            st.after()
            dve.sem_inc(s_slot, 1)
            dve.wait_ge(s_lr, 1)
            st.did(dve.tensor_copy(cnt_row, ps[0:1, 7, 0:NB]))
            offq = offs[:, :].rearrange("p (b q) -> p b q", q=len(QN))
            for q in range(len(QN)):
                st.after()
                st.did(dve.tensor_scalar(offq[:, :, q], cnt_row, 2 * q, E.bit_length() - 1,
                                         ALU.logical_shift_right, ALU.logical_shift_left))
            st.after()
            dve.sem_inc(s_offs, 1)
            dve.wait_ge(s_pw, 2)
            for i in range(DL):
                lo, n = 2 ** i - 1, 2 ** i
                st.did(dve.tensor_tensor(sc[:, :, lo:lo + n], mk[:, :, lo:lo + n],
                                         pw[:, :, DL - 1 - i:DL - i].to_broadcast([P, NT, n]), ALU.mult))
            st.after()
            dve.sem_inc(s_pm, 1)
            st.did(dve.tensor_copy(pay[:, :, 0:E], xn[:, :, :]))
            st.did(dve.tensor_copy(pay[:, :, E:PL], pw[:, :, :]))
            st.after()
            dve.sem_inc(s_pay, 1)
            dve.wait_ge(s_sum, 1)
            for k in range(2):
                hv = h1[:, 8 * k:8 * k + 8, :]
                st.did(dve.tensor_tensor(hv, hv, ps[:, 4 + k, :].rearrange("p (r e) -> p r e", e=E), ALU.add))
            dve.wait_ge(s_xs, 16)
            with dve.Fori(0, TS // 8) as it:
                for v in range(10):
                    if v < 8:
                        dve.wait_ge(s_tz, (it * 8 + v - 1 if v >= 2 else it * 8) + SEED)
                        xv = xsb[:, bass.ds(it * 8 + v, 1), :]
                        dve.tensor_tensor(zz[:, v % 2, :, :], xv[:, :, 0:E].to_broadcast([P, DL, E]),
                                          xv[:, :, E:PL].rearrange("p o k -> p (o k)").unsqueeze(2).to_broadcast([P, DL, E]),
                                          ALU.mult).then_inc(s_z, 1)
                    if v % 2 == 1 and v >= 3:
                        w = (v - 3) // 2
                        dve.wait_ge(s_blk, it * 8 + 2 * w + 2 + SEED)
                        pv = ps[0:BLK, 2 + w % 2, :].rearrange("p (t b e) -> p t b e", t=2, e=E)
                        for b in range(P // BLK):
                            last = dve.tensor_copy(ob[b * BLK:(b + 1) * BLK, bass.ds(it * 8 + 2 * w, 2), :], pv[:, :, b, :])
                        last.then_inc(s_ob, 1)
            dve.wait_ge(s_res, NT * 16)
            st.did(dve.tensor_tensor(h1[:, :, :], h1[:, :, :], res[:, :, :], ALU.add))
            st.after()
            dve.sem_inc(s_h2, 1)

            layernorm(h1[:, :, :], xn[:, :, :], 3)
            st.after()
            dve.sem_inc(s_xn, 1)
            dve.wait_ge(s_wa, N_WA)
            st.did(dve.tensor_tensor(h3[:, :, :], h1[:, :, :], bub[:, :].unsqueeze(1).to_broadcast([P, NT, E]), ALU.add))
            st.after()

            def take_max(p, n, between=None):
                h, ic = UNITS[n]
                for k in range(4 * (ic + 1)):
                    if k == 4 and between:
                        between()
                    g = FIRST[n] + k
                    r, jc = divmod(k, ic + 1)
                    w = BANK if jc < ic else (r + 1) * P
                    dve.wait_ge(s_sm, p * NSTEP + g + 1)
                    if k == 0:
                        dve.wait_ge(s_mx4, p * len(UNITS) + n + SEED)
                    dve.tensor_reduce(mx[:, n % 2, r, jc:jc + 1], ps[:, g % 2, 0:w], AX_X, ALU.max).then_inc(s_mxd, 1)
                dve.wait_ge(s_mxd, p * NSTEP + FIRST[n + 1] + SEED)
                if ic == 0 and between:
                    between()
                dve.tensor_reduce(mx4[:, n % 2, :], mx[:, n % 2, :, 0:ic + 1], AX_X, ALU.max).then_inc(s_mx4, 1)

            def max_row(p, n):
                h, ic = UNITS[n]
                dve.wait_ge(s_mrp, p * len(UNITS) + n + 1)
                dve.tensor_copy(qa[E:E + 1, h, ic * BANK:(ic + 1) * BANK], ps[0:1, 7, :]).then_inc(s_mr, 1)

            def add_head(p, n, m0):
                h, ic = UNITS[n]
                dve.wait_ge(s_pj, p * len(UNITS) + n + 1 + SEED)
                v = ps[:, 7, 0:TPC * (E + 1)].rearrange("p (r e) -> p r e", e=E + 1)
                m = m0 + p * (2 * len(UNITS) + 2)
                k = 2 * n + (n > 0) + (n > 1)
                dve.reciprocal(rden[:, 0, :], v[:, :, E:E + 1].rearrange("p r o -> p (r o)")).then_inc(step_v, 1)
                k += 1
                dve.wait_ge(step_v, m + k)
                if ic == 0:
                    dve.memset(rden[0:1, 0, 0:1], 0.0).then_inc(step_v, 1)
                    k += 1
                    dve.wait_ge(step_v, m + k)
                dve.tensor_tensor(on[:, :, :], v[:, :, 0:E], rden[:, 0, :].unsqueeze(2).to_broadcast([P, TPC, E]),
                                  ALU.mult).then_inc(step_v, 1)
                k += 1
                dve.wait_ge(step_v, m + k)
                hv = h3[:, ic * TPC:(ic + 1) * TPC, :]
                dve.tensor_tensor(hv, hv, on[:, :, :], ALU.add).then_inc(s_hd, 1)

            n0 = st.n
            with dve.Fori(0, NP) as p:
                for c in range(NCH):
                    dve.wait_ge(s_qkp, p * 2 * NCH + NCH + c + 1)
                    dve.tensor_copy(ka[0:E, 0, c * BANK:(c + 1) * BANK], ps[0:E, 4 + c, :])
                    dve.tensor_copy(ka[0:E, 1, c * BANK:(c + 1) * BANK], ps[E:P, 4 + c, :]).then_inc(s_ke, 1)
                dve.wait_ge(s_apad, 1)
                dve.memset(qa[E:E + 1, :, :], 0.0).then_inc(s_ke, 1)
                for c in range(NCH):
                    dve.wait_ge(s_vp, p * NCH + c + 1)
                    dve.tensor_copy(va[:, c * TPC:(c + 1) * TPC, :, 0:E],
                                    ps[:, c, :].rearrange("p (r h e) -> p r h e", h=2, e=E)).then_inc(s_ke, 1)
                take_max(p, 0)
                for n in range(len(UNITS)):
                    max_row(p, n)
                    add = (lambda: add_head(p, n - 1, n0)) if n >= 1 else None
                    if n + 1 < len(UNITS):
                        take_max(p, n + 1, add)
                    else:
                        add()
                add_head(p, len(UNITS) - 1, n0)
            st.n = n0 + NP * (2 * len(UNITS) + 2)
            dve.wait_ge(s_hd, NP * len(UNITS) + SEED)

            layernorm(h3[:, :, :], xn[:, :, :], 4)
            st.after()
            dve.sem_inc(s_xn, 1)
            dve.wait_ge(s_lg, 1)
            st.did(dve.tensor_copy(lg[:, :, :], ps[:, 4, 0:NT * NE].rearrange("p (c e) -> p c e", e=NE)))
            st.after()
            for c in range(NT):
                st.did(dve.max(out=top[:, c, :], in_=lg[:, c, :]))
            st.after()
            for c in range(NT):
                st.did(dve.max_index(out=topi[:, c, :], in_max=top[:, c, :], in_values=lg[:, c, :]))
            dve.tensor_tensor(tw[:, 0, :], top[:, :, 1:2].rearrange("p c o -> p (c o)"),
                              top[:, :, 0:1].rearrange("p c o -> p (c o)"), ALU.subtract).then_inc(s_d, 1)
            st.after()
            st.did(dve.tensor_copy(topf[:, :, :], topi[:, :, 0:2]))
            dve.wait_ge(s_e, 1)
            st.did(dve.tensor_scalar(tw[:, 2, :], tw[:, 1, :], 1.0, None, ALU.add))
            st.after()
            st.did(dve.reciprocal(tw[:, 0, :], tw[:, 2, :]))
            st.after()
            st.did(dve.tensor_tensor(tw[:, 1, :], tw[:, 1, :], tw[:, 0, :], ALU.mult))
            io = iota_e[:, :].unsqueeze(1).to_broadcast([P, NT, NE])
            dve.wait_ge(s_const, 1)
            for j, dst in ((0, ge), (1, ge2)):
                st.after()
                st.did(dve.tensor_tensor(dst[:, :, :], io, topf[:, :, j:j + 1].to_broadcast([P, NT, NE]), ALU.is_equal))
                st.after()
                st.did(dve.tensor_tensor(dst[:, :, :], dst[:, :, :], tw[:, j, :].unsqueeze(2).to_broadcast([P, NT, NE]),
                                         ALU.mult))
            st.after()
            dve.tensor_tensor(ge[:, :, :], ge[:, :, :], ge2[:, :, :], ALU.add).then_inc(s_g, 1)
            st.did(dve.memset(bc[:, :], 0.0))
            st.did(dve.memset(gT[:, :], 0.0))
            st.after()
            for c in range(NCH):
                cs = slice(c * BANK, (c + 1) * BANK)
                dve.wait_ge(s_gt, c + 1)
                st.did(dve.tensor_copy(gT[0:NE, cs], ps[0:NE, c, :]))
                st.after()
                st.did(dve.tensor_copy(bc[0:NE, cs], gT[0:NE, cs]))
                st.after()
                st.did(dve.tensor_tensor(res1[0:NE, :], gT[0:NE, cs], bc[0:NE, cs], ALU.subtract))
                st.after()
                st.did(dve.tensor_copy(mid[0:NE, :], res1[0:NE, :]))
                st.after()
                st.did(dve.tensor_tensor(res2[0:NE, :], res1[0:NE, :], mid[0:NE, :], ALU.subtract))
                st.did(dve.tensor_copy(bc[32:32 + NE, cs], mid[0:NE, :]))
                st.after()
                dve.tensor_copy(bc[64:64 + NE, cs], res2[0:NE, :]).then_inc(s_gp, 1)
                dve.wait_ge(s_gp, c + 1)
            with dve.Fori(0, NCH) as c:
                for e in range(NE):
                    dve.wait_ge(s_gb, c * NE + e + 1)
                    dve.wait_ge(s_rl, c * NE + e + 1)
                    dve.wait_ge(s_m2, (c * NE + e - 1 if e >= 2 else c * NE) + SEED)
                    dve.tensor_tensor(hg[:, e % 2, :], hr[:, e % 2, :], ps[:, 2 + e % 2, :], ALU.mult).then_inc(s_hg, 1)
                dve.wait_ge(s_ytp, c + 1 + SEED)
                xv = xn[:, bass.ds(c * TPC, TPC), :]
                dve.tensor_tensor(xv, xv, ps[:, 5, 0:TPC * E].rearrange("p (r e) -> p r e", e=E), ALU.add)\
                   .then_inc(s_ya, 1)
            dve.wait_ge(s_ya, NCH + SEED)
            layernorm(xn[:, :, :], xn[:, :, :], 5)
            dve.wait_ge(s_we, N_WE)
            st.after()
            st.did(dve.tensor_tensor(xn[:, :, :], xn[:, :, :], gamb[:, :].unsqueeze(1).to_broadcast([P, NT, E]), ALU.mult))
            st.did(dve.tensor_tensor(h3[:, :, :], h3[:, :, :], betb[:, :].unsqueeze(1).to_broadcast([P, NT, E]), ALU.add))
            st.after()
            dve.tensor_tensor(xn[:, :, :], xn[:, :, :], h3[:, :, :], ALU.add).then_inc(s_fin, 1)


_INS = ['x', 'L0_tok_ple_table', 'L0_attn_ln_gamma', 'L0_attn_ln_beta', 'L0_attn_in_proj_w', 'L0_attn_conv_w',
        'L0_attn_conv_b', 'L0_attn_x_proj_w', 'L0_attn_dt_proj_w', 'L0_attn_dt_proj_b', 'L0_attn_A_log', 'L0_attn_D',
        'L0_attn_out_proj_w', 'L0_attn_gate_w', 'L0_attn_gate_b', 'L0_ffn_w1s', 'L0_ffn_b1s', 'L0_ffn_w2s',
        'L0_ffn_b2s', 'L1_attn_Wq', 'L1_attn_bq', 'L1_attn_Wk', 'L1_attn_bk', 'L1_attn_Wv', 'L1_attn_bv',
        'L1_attn_Wu', 'L1_attn_bu', 'L1_ffn_gate_w', 'L1_ffn_gate_b', 'L1_ffn_w1', 'L1_ffn_b1', 'L1_ffn_w2',
        'L1_ffn_b2', 'L1_ffn_gamma', 'L1_ffn_beta']


def kernel(**inputs):
    import numpy as _np
    import concourse.bacc as _bacc
    from concourse import mybir as _mybir
    from concourse.bass_utils import run_bass_kernel_spmd as _run

    nc = _bacc.Bacc("TRN2", target_bir_lowering=False, num_devices=1)
    arrays, args = {}, {}
    for name in _INS:
        v = _np.ascontiguousarray(inputs[name])
        arrays[f"in_{name}"] = v
        args[name] = nc.dram_tensor(f"in_{name}", v.shape, _mybir.dt.from_np(v.dtype), kind="ExternalInput").ap()
    t = inputs["x"].shape[1]
    d = inputs["L0_attn_gate_w"].shape[0]
    out = nc.dram_tensor("out_h", (1, t, d), _mybir.dt.float32, kind="ExternalOutput").ap()
    tower_kernel(nc, args, out)
    r = _run(nc, [arrays], core_ids=[0])
    return r.results[0]["out_h"]
```

```python
from contextlib import ExitStack

import concourse.bass as bass
from concourse import mybir

F32 = mybir.dt.float32
F32R = mybir.dt.float32r
BF16 = mybir.dt.bfloat16
I32 = mybir.dt.int32
U32 = mybir.dt.uint32
ALU = mybir.AluOpType
ACT = mybir.ActivationFunctionType
AX_X = mybir.AxisListType.X

P = 128
SEED = 1
BANK = 512
NEG = -1.0e30


class Steps:

    def __init__(self, eng, sem):
        self.eng, self.sem, self.n = eng, sem, 0

    def did(self, ins):
        ins.then_inc(self.sem, 1)
        self.n += 1
        return self.n

    def after(self, n=None):
        self.eng.wait_ge(self.sem, self.n if n is None else n)


def tower_kernel(nc, a, out):
    T = a["x"].shape[1]
    V, HID = a["L0_tok_ple_table"].shape
    E = a["L0_attn_gate_w"].shape[0]
    LAYER = 3
    NT = T // P
    NCH = T // BANK
    HT = NT // 2
    HALVES = (slice(0, HT), slice(HT, NT))
    TPC = BANK // P
    DI = a["L0_attn_D"].shape[0]
    DS = a["L0_attn_A_log"].shape[1]
    KC = a["L0_attn_conv_w"].shape[2]
    RK = a["L0_attn_dt_proj_w"].shape[1]
    NH = a["L1_attn_Wq"].shape[1] // E
    NP = NH // 2
    NE = a["L1_ffn_gate_w"].shape[1]
    FF = a["L1_ffn_w1"].shape[2]
    ND = a["L0_ffn_w1s"].shape[0]
    NDP = ND + 1
    DL = NDP.bit_length() - 1
    NL = 2 ** (DL - 1)
    BLK = 32
    UT = 16
    TS = -(-(T // BLK + NL) // (P // BLK * UT)) * UT
    NB = TS * (P // BLK)
    SH = BLK.bit_length() - 1
    QN = [NL >> (2 * q) for q in range(DL // 2)]
    PL = E + DL
    EPS = 1e-5

    with ExitStack() as ctx:
        def sb(name, shape, dt=F32):
            return ctx.enter_context(nc.sbuf_tensor(name, shape, dt))

        def sem(name):
            return ctx.enter_context(nc.semaphore(name))

        ps = ctx.enter_context(nc.psum_tensor("ps", [P, 8, BANK], F32))
        with nc.sbuf_tensor("arena", [P, 26 * 1024 + 64], F32) as arena:
            pass
        qk = sb("qk", [P, 4, 2, T], F32R)
        sb("arena_rest", [P, 26 * 1024 + 64 - 4 * 2 * T])
        taken = {"mamba": 0, "tree": 0, "attention": 0, "moe": 0}

        def part(stage, shape, dt=F32):
            n = 1
            for d in shape[1:]:
                n *= d
            words = n * mybir.dt.size(dt) // 4
            v = arena[0:shape[0], taken[stage]:taken[stage] + words]
            taken[stage] += words
            if dt != F32:
                v = v.bitcast(dt)
            if len(shape) == 2:
                return v
            names = "abcd"[:len(shape) - 1]
            return v.rearrange(f"p ({' '.join(names)}) -> p {' '.join(names)}", **dict(zip(names[1:], shape[2:])))

        ident = sb("ident", [P, P])
        spare = sb("spare", [P, 8])
        nident = sb("nident", [P, P])
        identb = sb("identb", [P, P], BF16)
        mask_q = sb("mask_q", [P, P], BF16)
        mask_k = sb("mask_k", [P, P], BF16)
        sel = sb("sel", [96, 32, P], BF16)
        iota_e = sb("iota_e", [P, NE])
        iota_b = sb("iota_b", [P, 2])
        onesb = sb("onesb", [P, P], BF16)
        before = sb("before", [P, P], BF16)

        h0 = sb("h0", [P, NT, E])
        h1 = sb("h1", [P, NT, E])
        h3 = sb("h3", [P, NT, E])
        cen = sb("cen", [P, NT, E])
        sq = sb("sq", [P, NT, E])
        xn = sb("xn", [P, NT, E])
        stat = sb("stat", [P, 8, NT])
        xt = sb("xt", [P, T])

        ids = sb("ids", [NT, P], I32)
        idr = sb("idr", [NT, P])
        idf = sb("idf", [P, 2, NT])
        rows = sb("rows", [P, NT], U32)

        win = sb("win", [P, 2, E])
        convw = sb("convw", [DI, KC])
        convb = sb("convb", [DI, 1])
        xpw = sb("xpw", [RK + 2 * DS, DI])
        dtw = sb("dtw", [DI, RK])
        dtb = sb("dtb", [DI, 1])
        alog = sb("alog", [DI, DS])
        neg_a = sb("neg_a", [DI, DS])
        dskip = sb("dskip", [DI, 1])
        outw = sb("outw", [E, DI])
        gatew = sb("gatew", [E, E])
        gateb = sb("gateb", [E, 1])
        gam = sb("gam", [E, 1])
        bet = sb("bet", [E, 1])
        wtap = sb("wtap", [DI, KC, E])
        wconv = sb("wconv", [P, 2, DI])
        wz = sb("wz", [P, DI])
        wg = sb("wg", [P, E])
        wbc = sb("wbc", [DI, 2 * DS])
        dtwT = sb("dtwT", [RK, DI])
        wdelta = sb("wdelta", [DI, DI])
        woT = sb("woT", [DI, E])
        x2 = part("mamba", [P, T + 8])
        u = part("mamba", [DI, T])
        sz = part("mamba", [DI, T])
        gsig = part("mamba", [E, T])
        delta = part("mamba", [DI, T])
        du = part("mamba", [DI, T])
        x4 = x2[:, 0:4 * BANK].rearrange("p (k n) -> p k n", k=4)
        spl = x4
        dcur = part("mamba", [DI, BANK])
        mo = part("mamba", [E, 2, BANK])
        bc = sb("bc", [96, T], BF16)
        res1 = sb("res1", [32, BANK])
        mid = sb("mid", [32, BANK], BF16)
        res2 = sb("res2", [32, BANK])
        dA = part("mamba", [DI, 2, BANK])
        dbu = part("mamba", [DI, 2, BANK])
        hs = part("mamba", [DI, DS, BANK + 1])
        hc = x4
        hc_sum = part("mamba", [DI, BANK])
        yb = part("mamba", [DI, 2, BANK])

        step_v = sem("vector_step")
        step_s = sem("scalar_step")
        step_g = sem("gpsimd_step")
        s_ids = sem("ids_loaded")
        s_idr = sem("ids_as_floats")
        s_idt = sem("ids_turned")
        s_ident = sem("identity_ready")
        s_rows = sem("rows_ready")
        s_emb = [sem(f"embeddings_loaded_{h}") for h in range(2)]
        s_const = sem("constants_ready")
        s_wm = sem("mamba_weights_loaded")
        s_wa = sem("attn_weights_loaded")
        s_we = sem("moe_weights_loaded")
        s_wtap = sem("taps_scaled")
        s_wps = sem("mamba_weights_turned")
        s_wsb = sem("mamba_weights_in_sbuf")
        s_wdp = sem("wdelta_product")
        s_wds = sem("wdelta_in_sbuf")
        s_var = sem("ln_variance")
        s_std = sem("ln_std")
        s_xn = sem("normalised_tokens")
        s_xtp = sem("turned_in_psum")
        s_xt = sem("turned_in_sbuf")
        s_wpad = sem("weight_pads_zeroed")
        s_pad = sem("mamba_pads_zeroed")
        s_apad = sem("attn_pads_set")
        s_in = sem("in_projected")
        s_u = sem("u_ready")
        s_zg = sem("z_gate_ready")
        s_bcp = sem("bc_projected")
        s_bch = sem("bc_parts")
        s_dlp = sem("delta_projected")
        s_abs = sem("delta_abs")
        s_ln1 = sem("delta_log")
        s_dl = sem("delta_ready")
        s_bb = sem("b_broadcast")
        s_cb = sem("c_broadcast")
        s_dcur = sem("chunk_delta_ready")
        s_da = sem("decay_ready")
        s_scan = sem("scan_done")
        s_dbu = sem("dbu_done")
        s_hc = sem("hc_ready")
        s_yac = sem("hc_accumulated")
        s_y = sem("y_gated")
        s_op = sem("out_projected")
        s_mo = sem("gated_out")
        s_mt = sem("out_turned")
        s_h1 = sem("h1_ready")

        w1n = part("tree", [P, 2, E])
        w1T = part("tree", [P, NDP])
        b2n = part("tree", [P, 2, E])
        w2q = [part("tree", [P, n * E]) for n in QN]
        ls = part("tree", [P, NT, DL])
        pw = part("tree", [P, NT, DL])
        pay = part("tree", [P, NT, PL])
        offs = part("tree", [1, NB * len(QN)], I32)
        cnt = part("tree", [P, NL], I32)
        nbf, cumend, base, onesf = [sq[:, k * NL // E:(k + 1) * NL // E, :].rearrange("p c e -> p (c e)")
                                    for k in range(4)]
        slot = part("tree", [P, NT])
        idf2 = part("tree", [P, 2, NT])
        cnt_row = part("tree", [1, NB], I32)
        slot_i = part("tree", [P, 3, NT], I32)
        tw0 = taken["tree"]
        sc = part("tree", [P, NT, NDP])
        mk = part("tree", [P, NT, NDP])
        tw1 = taken["tree"]
        pmT = part("tree", [P, 2, T])
        taken["tree"] = tw1
        ohb = part("tree", [P, NT, NL], BF16)
        pre = part("tree", [P, NT, NL], BF16)
        rank = part("tree", [P, NT, NL])
        taken["tree"] = tw0
        ob = part("tree", [P, TS, E])
        taken["tree"] = tw0 + NT * NDP
        xsb = part("tree", [P, TS, PL])
        taken["tree"] = tw1
        zz = part("tree", [P, 2, DL, E])
        zt = part("tree", [P, 2, DL // 2, P])
        res = cen
        slots_x = nc.dram_tensor("slots_x", (P * TS, PL), F32, kind="Internal").ap()
        slots_y = nc.dram_tensor("slots_y", (P * TS, E), F32, kind="Internal").ap()
        s_tpad = sem("tree_pads_zeroed")
        s_wt = sem("tree_weights_loaded")
        s_w2n = sem("tree_w2_loaded")
        s_w1p = sem("tree_w1_turned")
        s_w1T = sem("tree_w1_in_sbuf")
        s_sc = sem("tree_scores")
        s_sce = sem("tree_scores_in_sbuf")
        s_ls = sem("tree_path_scores")
        s_pw = sem("tree_path_weights")
        s_pm = sem("tree_node_weights")
        s_pmp = sem("tree_node_weights_turned")
        s_pmT = sem("tree_node_weights_in_sbuf")
        s_zero = sem("zeros_ready")
        zeros = dA[:, :, :].rearrange("p a b -> p (a b)")[:, 0:TS // 4 * PL]
        s_zf = sem("slots_zeroed")
        s_cnt = sem("leaf_counts")
        s_oh = sem("leaves_marked")
        s_rkp = sem("ranks_in_psum")
        s_slot = sem("slots_ready")
        s_lc = sem("leaf_of_block")
        s_lr = sem("leaf_of_block_turned")
        s_offs = sem("block_offsets_ready")
        s_pay = sem("payload_ready")
        s_scat = sem("payload_scattered")
        s_xs = sem("sorted_tokens_loaded")
        s_z = sem("z_ready")
        s_tz = sem("z_turned")
        s_zt = sem("turned_z_in_sbuf")
        s_blk = sem("tile_of_blocks_done")
        s_ob = sem("results_in_sbuf")
        s_obs = sem("results_stored")
        s_res = [sem(f"results_gathered_{h}") for h in range(2)]
        s_sum = sem("tree_summed")

        wqk = sb("wqk", [P, 2, NH * E])
        wv = sb("wv", [P, NH * E])
        wu = sb("wu", [E + 1, NH, E + 1])
        bub = sb("bub", [P, E])
        wh = sb("wh", [P, 2, 2, E])
        wuh = sb("wuh", [E + 1, 2, E + 1])
        q1 = qk[:, 0]
        k1 = qk[:, 1]
        q2 = qk[:, 2]
        k2 = qk[:, 3]
        taken["attention"] = 4 * 2 * T
        vall = part("attention", [P, NT, NH * E])
        vh = part("attention", [P, 2, NT, E + 1])
        mx = sb("mx", [P, 2, TPC, NCH])
        mx4 = sb("mx4", [P, 2, TPC])
        mhl = sb("mhl", [P, 2, TPC, 2], F32R)
        nident_r = sb("nident_r", [P, P], F32R)
        pt = [t[:, 8 * k:8 * k + 8, :].rearrange("p c e -> p (c e)") for t in (cen, sq) for k in range(2)]
        ot = sb("ot", [E + 1, BANK])
        rden = sb("rden", [P, 2, TPC])
        on = sb("on", [P, TPC, E])
        s_qs = sem("head_weights_copied")
        s_qkp = sem("qk_projected")
        s_vp = sem("v_projected")
        s_va = sem("v_in_sbuf")
        s_nir = sem("nident_r_ready")
        s_vh = sem("head_v_copied")
        s_qh = sem("qk_hi_in_sbuf")
        s_ql = sem("qk_lo_in_sbuf")
        s_qc = sem("qk_hi_copied")
        s_sm = sem("scores_for_max")
        s_mxd = sem("scores_max_taken")
        s_mx4 = sem("row_max_ready")
        s_mrp = sem("row_max_turned")
        s_mh = sem("row_max_step")
        s_mr = sem("row_max_in_q")
        s_st = sem("scores_turned")
        s_ex = sem("exp_done")
        s_av = sem("av_step")
        s_ot = sem("av_in_sbuf")
        s_pj = sem("head_projected")
        s_hd = sem("head_added")

        gw = sb("gw", [P, NE])
        w1 = sb("w1", [P, NE, FF])
        b1 = sb("b1", [NE, FF])
        b1T = sb("b1T", [FF, NE])
        w2 = sb("w2", [FF, NE, E])
        b2 = sb("b2", [P, 2 * E])
        gamb = sb("gamb", [P, E])
        betb = sb("betb", [P, E])
        lg = sb("lg", [P, NT, NE])
        top = sb("top", [P, NT, 8])
        topi = sb("topi", [P, NT, 8], U32)
        topf = sb("topf", [P, NT, 2])
        tw = sb("tw", [P, 3, NT])
        ge = sb("ge", [P, NT, NE])
        ge2 = sb("ge2", [P, NT, NE])
        ident2 = sb("ident2", [P, E])
        x1 = qk[:, 0, 0]
        w2p = qk[:, 0, 1].rearrange("p (n k e) -> p n k e", k=2, e=E)
        w1p = qk[:, 1]
        hp = qk[:, 2:4].rearrange("p k s t -> p k (s t)").rearrange("p k (r n) -> p k r n", n=BANK)
        HR = 8
        taken["moe"] = 4 * 2 * T
        g3 = part("moe", [P, NT, 96], BF16)
        gT = part("moe", [P, T])
        hr = part("moe", [FF, 2, BANK])
        hg = part("moe", [FF, 4, BANK])
        yt = part("moe", [P, BANK])
        s_b1p = sem("b1_turned")
        s_b1T = sem("b1_in_sbuf")
        s_id2 = sem("ident2_ready")
        s_wh = sem("expert_weights_hi")
        s_wl = sem("expert_weights_lo")
        s_xh = sem("x_hi_in_sbuf")
        s_xl = sem("x_lo_in_sbuf")
        s_gTs = sem("gates_turned_in_sbuf")
        s_hh = sem("hidden_hi")
        s_hld = sem("hidden_lo_by_vector")
        s_hlp = sem("hidden_lo_by_gpsimd")
        s_lg = sem("gate_logits")
        s_d = sem("top2_difference")
        s_e = sem("top2_exp")
        s_g = sem("gates_ready")
        s_gt = sem("gates_turned")
        s_gp0 = sem("gate_pads_zeroed")
        s_gp = sem("gate_parts")
        s_m1 = sem("expert_up")
        s_gb = sem("gate_broadcast")
        s_rl = sem("expert_relu")
        s_hg = sem("expert_gated")
        s_m2 = sem("expert_down")
        s_yt = sem("moe_in_sbuf")
        s_ytp = sem("moe_turned")
        s_ya = sem("moe_added")
        s_fin = sem("result_ready")
        s_out = sem("result_stored")

        UNITS = [(h, ic) for h in range(2) for ic in range(NCH)]
        NSTEP = sum(4 * (ic + 1) for _, ic in UNITS)
        FIRST = [sum(4 * (ic + 1) for _, ic in UNITS[:n]) for n in range(len(UNITS) + 1)]

        NU = len(UNITS)
        ns_of = lambda n: 4 * (UNITS[(n + 1) % NU][1] + 1)
        LEAD = 6
        LAG = 5
        VB = (3, 4, 6)
        step_at = lambda n, kk: kk * max(ns_of(n) - LEAD, 4) // ns_of(n)
        turn_at = lambda n: max(step_at(n, ns_of(n) - 1) + 2, 5)
        PREP = {2: {4: 0, 8: 1}, 3: {4: 2, 8: 3}}

        GATE_AT = 2
        inb = lambda c: 0 if c % 2 else 4

        block = ctx.enter_context(nc.Block())

        @block.sync
        def _(sp):
            def load(dst, src, s):
                sp.dma_start(dst, src).then_inc(s, 16)

            load(ids[:, :], a["x"].rearrange("b (c p) -> (b c) p", p=P), s_ids)
            col = lambda ap: ap.rearrange("(p o) -> p o", o=1)
            m = "L0_attn_"
            for dst, src in (
                (win[:, :, :], a[m + "in_proj_w"].rearrange("(k p) d -> p k d", p=P)),
                (convw[:, :], a[m + "conv_w"].rearrange("d o k -> d (o k)")),
                (convb[:, :], col(a[m + "conv_b"])), (xpw[:, :], a[m + "x_proj_w"]),
                (dtw[:, :], a[m + "dt_proj_w"]), (dtb[:, :], col(a[m + "dt_proj_b"])),
                (alog[:, :], a[m + "A_log"]), (dskip[:, :], col(a[m + "D"])),
                (outw[:, :], a[m + "out_proj_w"]), (gatew[:, :], a[m + "gate_w"]),
                (gateb[:, :], col(a[m + "gate_b"])),
                (gam[:, :], col(a[m + "ln_gamma"])), (bet[:, :], col(a[m + "ln_beta"])),
            ):
                load(dst, src, s_wm)
            sp.wait_ge(s_zero, 1)
            for t0 in range(0, TS, TS // 4):
                load(slots_x.rearrange("(p t) d -> p t d", t=TS)[:, t0:t0 + TS // 4, :],
                     zeros[:, :].rearrange("p (t d) -> p t d", d=PL), s_zf)
            sp.wait_ge(s_wpad, 1)
            row = lambda ap: ap.rearrange("(o n) -> o n", o=1)
            m = "L1_attn_"
            for dst, src in (
                (wqk[0:E, 0, :], a[m + "Wq"]), (wqk[0:E, 1, :], a[m + "Wk"]), (wv[0:E, :], a[m + "Wv"]),
                (wqk[E:E + 1, 0, :], row(a[m + "bq"])), (wqk[E:E + 1, 1, :], row(a[m + "bk"])),
                (wv[E:E + 1, :], row(a[m + "bv"])),
                (wu[0:E, :, 0:E], a[m + "Wu"].rearrange("(h e) n -> e h n", e=E)),
                (bub[:, :], a[m + "bu"].partition_broadcast(P)),
            ):
                load(dst, src, s_wa)
            m = "L1_ffn_"
            for dst, src in (
                (gw[0:E, :], a[m + "gate_w"]), (gw[E:E + 1, :], row(a[m + "gate_b"])),
                (w1[0:E, :, :], a[m + "w1"].rearrange("e d f -> d e f")),
                (w1[E:P, :, :], a[m + "w1"].rearrange("e d f -> d e f")), (b1[:, :], a[m + "b1"]),
                (w2[:, :, :], a[m + "w2"].rearrange("e f d -> f e d")), (b2[0:NE, 0:E], a[m + "b2"]),
                (gamb[:, :], a[m + "gamma"].partition_broadcast(P)),
                (betb[:, :], a[m + "beta"].partition_broadcast(P)),
            ):
                load(dst, src, s_we)
            sp.wait_ge(s_tpad, 1)
            m = "L0_ffn_"
            for dst, src in (
                (w1n[:, 0, :], a[m + "w1s"][0:P, :]), (w1n[0:ND - P, 1, :], a[m + "w1s"][P:ND, :]),
                (w1T[E:E + 1, 0:ND], row(a[m + "b1s"])),
                (b2n[:, 0, :], a[m + "b2s"][0:P, :]), (b2n[0:ND - P, 1, :], a[m + "b2s"][P:ND, :]),
            ):
                load(dst, src, s_wt)
            for q, n in enumerate(QN):
                load(w2q[q][0:E, :].rearrange("p (n o) -> p n o", o=E),
                     a[m + "w2s"][n - 1:2 * n - 1].rearrange("n d o -> d n o"), s_w2n)
                for h in range(2):
                    load(w2q[q][E:P, :].rearrange("p (n h o) -> p n h o", h=2, o=E)[:, :, h, :],
                         a[m + "w2s"][n // 2 - 1:n - 1].rearrange("n d o -> d n o"), s_w2n)
            sp.wait_ge(s_scat, NT * 16)
            sp.wait_ge(s_pm, 1)
            load(xsb[:, :, :], slots_x.rearrange("(p t) d -> p t d", t=TS), s_xs)
            sp.wait_ge(s_ob, TS // 2 + SEED)
            load(slots_y.rearrange("(p t) d -> p t d", t=TS), ob[:, :, :], s_obs)
            sp.wait_ge(s_fin, 1)
            sp.dma_start(out.rearrange("b (c p) d -> p (b c) d", p=P), xn[:, :, :]).then_inc(s_out, 16)
            sp.wait_ge(s_out, 16)

        N_WM, N_WA, N_WE, N_WT, N_W2 = 13 * 16, 8 * 16, 9 * 16, 5 * 16, 3 * (DL // 2) * 16

        @block.gpsimd
        def _(pool):
            st = Steps(pool, step_g)
            st.did(pool.memset(ident[:, :], 0.0))
            st.after()
            pool.affine_select(out=ident[:, :], in_=ident[:, :], compare_op=ALU.not_equal, fill=1.0,
                               base=0, pattern=[[-1, P]], channel_multiplier=1).then_inc(s_ident, 1)
            pool.wait_ge(s_ident, 1)
            for t in (wqk[E:P], wv[E:P], gw[E:P], b2[:, :]):
                st.did(pool.memset(t, 0.0))
                st.after()
            st.after()
            st.did(pool.memset(wu[:, :, :], 0.0))
            st.after()
            st.did(pool.memset(wu[E:E + 1, :, E:E + 1], 1.0))
            st.after()
            pool.sem_inc(s_wpad, 1)
            for t in (identb, mask_q, mask_k, nident):
                st.did(pool.memset(t[:, :], 0.0))
            st.did(pool.memset(sel[:, :, :], 0.0))
            st.did(pool.iota(iota_e[:, :], [[1, NE]], base=0, channel_multiplier=0,
                             allow_small_or_imprecise_dtypes=True))
            pool.wait_ge(s_rows, 1)
            st.after()
            for c in range(NT):
                pool.indirect_dma_start(
                    out=h0[:, c, :], out_offset=None,
                    in_=a["L0_tok_ple_table"].rearrange("v (k e) -> (v k) e", e=E),
                    in_offset=bass.IndirectOffsetOnAxis(ap=rows[:, c:c + 1], axis=0),
                ).then_inc(s_emb[c // HT], 16)
            pool.memset(zeros, 0.0).then_inc(s_zero, 1)
            st.did(pool.memset(onesb[:, :], 1.0))
            st.did(pool.iota(iota_b[:, :], [[P, 2]], base=0, channel_multiplier=1,
                             allow_small_or_imprecise_dtypes=True))
            st.did(pool.memset(before[:, :], 1.0))
            st.after()
            st.did(pool.affine_select(out=before[:, :], in_=before[:, :], compare_op=ALU.is_gt, fill=0.0,
                                      base=0, pattern=[[1, P]], channel_multiplier=-1))
            for t, fill in ((identb, 1.0), (nident, -1.0)):
                st.did(pool.affine_select(out=t[:, :], in_=t[:, :], compare_op=ALU.not_equal, fill=fill,
                                          base=0, pattern=[[-1, P]], channel_multiplier=1))
            st.did(pool.affine_select(out=mask_q[:, :], in_=mask_q[:, :], compare_op=ALU.is_gt, fill=NEG,
                                      base=0, pattern=[[-1, P]], channel_multiplier=1))
            st.did(pool.affine_select(out=mask_k[:, :], in_=mask_k[:, :], compare_op=ALU.is_gt, fill=NEG,
                                      base=0, pattern=[[1, P]], channel_multiplier=-1))
            for part in range(3):
                st.after()
                st.did(pool.affine_select(out=sel[:, :, :], in_=sel[:, :, :], compare_op=ALU.not_equal,
                                          fill=1.0, base=-32 * part, pattern=[[-1, 32], [0, P]],
                                          channel_multiplier=1))
            st.after()
            pool.sem_inc(s_const, 1)
            pool.sem_inc(s_yac, SEED)
            for c in range(NCH):
                for s in range(1, DS):
                    pool.wait_ge(s_hc, c * DS + s + 1 + SEED)
                    if s == 1 and c:
                        pool.wait_ge(s_y, c + SEED)
                    if s > 1:
                        pool.wait_ge(s_yac, c * (DS - 1) + s - 1 + SEED)
                    pool.tensor_tensor(hc_sum[:, :], hc[:, 0, :] if s == 1 else hc_sum[:, :], hc[:, s % 4, :], ALU.add)\
                        .then_inc(s_yac, 1)
            pool.wait_ge(s_h1, 2 * NCH + SEED)
            for t in (w1T[:, :], b2n[:, :, :], w1n[:, 1, :]):
                st.did(pool.memset(t, 0.0))
                st.after()
            pool.sem_inc(s_tpad, 1)
            pool.wait_ge(s_zf, 4 * 16)
            pool.wait_ge(s_pay, 1)
            for c in range(NT):
                pool.indirect_dma_start(
                    out=slots_x, out_offset=bass.IndirectOffsetOnAxis(ap=rows[:, c:c + 1], axis=0),
                    in_=pay[:, c, :], in_offset=None).then_inc(s_scat, 16)
            pool.wait_ge(s_obs, 16)
            for c in range(NT):
                pool.indirect_dma_start(
                    out=res[:, c, :], out_offset=None, in_=slots_y,
                    in_offset=bass.IndirectOffsetOnAxis(ap=rows[:, c:c + 1], axis=0)).then_inc(s_res[c // HT], 16)
            pool.wait_ge(s_apad, 1)

            def weights(h, slot):
                pool.tensor_copy(wh[:, slot, :, :], wqk[:, :, h * E:(h + 1) * E]).then_inc(s_qs, 1)
                pool.tensor_copy(wuh[:, slot, :], wu[:, h, :]).then_inc(s_qs, 1)

            def head_values(h, slot):
                pool.tensor_copy(vh[:, slot, :, 0:E], vall[:, :, h * E:(h + 1) * E]).then_inc(s_vh, 1)

            def copies(h, slot):
                for c in range(NCH):
                    cs = slice(c * BANK, (c + 1) * BANK)
                    pool.wait_ge(s_qh, h * NCH + c + 1)
                    if c:
                        pool.wait_ge(s_qc, 2 * (h * NCH + c))
                    elif h:
                        pool.wait_ge(s_vh, h + 1)
                    else:
                        pool.wait_ge(s_qs, 2)
                    pool.tensor_copy(k1[E:P, slot, cs], k1[0:E, slot, cs]).then_inc(s_qc, 1)
                    pool.wait_ge(s_qc, 2 * (h * NCH + c) + 1)
                    pool.tensor_copy(q2[0:E, slot, cs], q1[0:E, slot, cs]).then_inc(s_qc, 1)

            pool.wait_ge(s_wa, N_WA)
            weights(0, 0)
            copies(0, 0)
            pool.wait_ge(s_va, NT)
            pool.wait_ge(s_qc, 2 * NCH)
            head_values(0, 0)
            for h in range(1, NH):
                pool.wait_ge(s_hd, (h - 1) * NCH + SEED)
                weights(h, h % 2)
                head_values(h, h % 2)
                copies(h, h % 2)
            w1f, w2f = w1[:, :, :].rearrange("p n f -> p (n f)"), w2[:, :, :]
            pool.wait_ge(s_wh, 1)
            pool.tensor_tensor(w1p[:, 1, :], w1f, w1p[:, 0, :].bitcast(F32), ALU.subtract).then_inc(s_wl, 1)
            pool.wait_ge(s_wh, 2)
            pool.tensor_tensor(w2p[:, :, 1, :], w2f, w2p[:, :, 0, :].bitcast(F32), ALU.subtract).then_inc(s_wl, 1)
            for g in range(1, NCH * NE, 2):
                pool.wait_ge(s_hh, g + 1 + SEED)
                if g >= HR:
                    pool.wait_ge(s_m2, g - HR + 1 + SEED)
                pool.tensor_tensor(hp[:, 1, g % HR, :], hg[:, g % 4, :], hp[:, 0, g % HR, :].bitcast(F32),
                                   ALU.subtract).then_inc(s_hlp, 1)

        @block.tensor
        def _(pe):
            for s in (s_op, s_mt, s_av, s_pj, s_blk, s_tz, s_m2, s_ytp):
                pe.sem_inc(s, SEED)
            XN = ((1, 2), (3, 3), (4, 5), (6, 6))

            def turn_tokens(k):
                for c in range(NT):
                    if c % HT == 0:
                        pe.wait_ge(s_xn, XN[k][c // HT])
                    last = pe.transpose(ps[0:E, c // TPC, (c % TPC) * P:(c % TPC + 1) * P], xn[:, c, :], ident[:, :])
                    if c % TPC == TPC - 1:
                        last.then_inc(s_xtp, 1)

            pe.wait_ge(s_ident, 1)
            pe.wait_ge(s_idr, 1)
            pe.transpose(ps[:, 7, 0:NT], idr[:, :], ident[0:NT, 0:NT]).then_inc(s_idt, 1)
            pe.wait_ge(s_wm, N_WM)
            pe.wait_ge(s_wtap, 1)
            for k in range(2):
                pe.transpose(ps[:, 4, k * P:(k + 1) * P], wtap[:, 2 * k:2 * k + 2, :], ident[:, :])
            pe.transpose(ps[0:E, 4, 2 * P:3 * P], win[:, 1, :], ident[:, :])
            pe.transpose(ps[0:E, 4, 3 * P:3 * P + E], gatew[:, :], ident[0:E, 0:E])
            pe.transpose(ps[:, 5, 0:RK + 2 * DS], xpw[:, :], ident[0:RK + 2 * DS, 0:RK + 2 * DS])
            pe.transpose(ps[0:RK, 5, P:2 * P], dtw[:, :], ident[:, :])
            pe.transpose(ps[:, 5, 2 * P:2 * P + E], outw[:, :], ident[0:E, 0:E]).then_inc(s_wps, 1)
            pe.wait_ge(s_wsb, 1)
            pe.matmul(ps[:, 6, 0:DI], xpw[0:RK, :], dtwT[:, :], start=True, stop=True).then_inc(s_wdp, 1)

            turn_tokens(0)
            pe.wait_ge(s_wds, 1)
            pe.wait_ge(s_pad, 1)
            for c in range(NCH + 1):
                if c < NCH:
                    pe.wait_ge(s_xt, max(c + 1, 3) if c % 2 else c + 1)
                    if c >= 2:
                        pe.wait_ge(s_zg, c - 1)
                    b = inb(c)
                    for k in range(2):
                        pe.matmul(ps[:, b, :], wconv[:, k, :], x2[:, c * BANK + 3 - 2 * k:c * BANK + 3 - 2 * k + BANK],
                                  start=(k == 0), stop=(k == 1))
                    pe.matmul(ps[:, b + 1, :], wz[:, :], x2[:, c * BANK + 3:c * BANK + 3 + BANK], start=True, stop=True)
                    pe.matmul(ps[0:E, b + 2, :], wg[:, :], x2[:, c * BANK + 3:c * BANK + 3 + BANK],
                              start=True, stop=True).then_inc(s_in, 1)
                if c >= 1:
                    d = c - 1
                    us = u[:, d * BANK:(d + 1) * BANK]
                    pe.wait_ge(s_u, d + 1)
                    if d == 0:
                        pe.wait_ge(s_xt, NCH)
                    else:
                        pe.wait_ge(s_abs, d)
                        pe.wait_ge(s_bch, d)
                    pe.matmul(ps[:, 7, :], wdelta[:, :], us, start=True, stop=True).then_inc(s_dlp, 1)
                    pe.matmul(ps[0:2 * DS, 3, :], wbc[:, :], us, start=True, stop=True).then_inc(s_bcp, 1)

            pe.wait_ge(s_const, 1)
            pe.wait_ge(s_dl, NCH)
            pe.wait_ge(s_bch, NCH)

            def project_out(c):
                pe.wait_ge(s_y, c + 1 + SEED)
                pe.matmul(ps[0:E, bass.ds(4 + c, 1), :].rearrange("p o n -> p (o n)"), woT[:, :], yb[:, 1, :],
                          start=True, stop=True).then_inc(s_op, 1)

            def spread(c, before, first):
                mv = bc[:, bass.ds(c * BANK, BANK)]
                for s in range(DS):
                    if s >= 2 or not first:
                        pe.wait_ge(s_dbu, c * DS + s - 1 + SEED)
                    pe.matmul(ps[:, s % 2, :], sel[:, s, :], mv, start=True, stop=True).then_inc(s_bb, 1)
                    if s >= 2 or not first:
                        pe.wait_ge(s_hc, c * DS + s - 1 + SEED)
                    pe.matmul(ps[:, 2 + s % 2, :], sel[:, DS + s, :], mv, start=True, stop=True).then_inc(s_cb, 1)
                    if s == GATE_AT + 2 and not first:
                        project_out(before)

            spread(0, None, True)
            with pe.Fori(0, NCH - 1) as i:
                spread(i + 1, i, False)
            project_out(NCH - 1)
            for c in range(NCH):
                pe.wait_ge(s_mo, c + 1 + SEED)
                if c >= 2:
                    pe.wait_ge(s_h1, NCH + c - 1 + SEED)
                for r in range(TPC):
                    last = pe.transpose(ps[:, c % 2, r * E:(r + 1) * E], mo[:, c % 2, r * P:(r + 1) * P], ident[0:E, 0:E])
                last.then_inc(s_mt, 1)

            turn_tokens(1)
            pe.wait_ge(s_wt, N_WT)
            for k in range(2):
                m = pe.transpose(ps[0:E, 7, k * P:(k + 1) * P], w1n[:, k, :], ident[:, :])
            m.then_inc(s_w1p, 1)
            pe.wait_ge(s_w1T, 1)
            pe.wait_ge(s_xt, 2 * NCH)
            for c in range(NT):
                pe.matmul(ps[:, (4 + c // 2) % 8, (c % 2) * NDP:(c % 2) * NDP + ND], xt[:, c * P:(c + 1) * P],
                          w1T[:, 0:ND], start=True, stop=True).then_inc(s_sc, 1)
            pe.wait_ge(s_oh, 1)
            pe.wait_ge(s_sce, NT // 2)
            pe.matmul(ps[:, 6, 0:NL], onesb[:, :], pre[:, NT - 1, :], start=True, stop=True).then_inc(s_cnt, 1)
            for c in range(NT):
                dst = ps[:, c // TPC, (c % TPC) * NL:(c % TPC + 1) * NL]
                m = pe.matmul(dst, before[:, :], ohb[:, c, :], start=True, stop=c == 0)
                if c:
                    m = pe.matmul(dst, onesb[:, :], pre[:, c - 1, :], start=False, stop=True)
            m.then_inc(s_rkp, 1)
            pe.wait_ge(s_lc, 1)
            for k in range(2):
                m = pe.matmul(ps[0:1, 7, k * P:(k + 1) * P], nbf[:, k:k + 1], ident[:, :], start=True, stop=True)
            m.then_inc(s_lr, 1)
            pe.wait_ge(s_offs, 1)
            pe.wait_ge(s_slot, 1)
            pe.wait_ge(s_sce, NT // 2)
            pe.wait_ge(s_pm, 1)
            for k in range(2):
                for c in range(NT):
                    m = pe.transpose(ps[:, 4 * k + c // TPC, (c % TPC) * P:(c % TPC + 1) * P],
                                     sc[:, c, k * P:(k + 1) * P], ident[:, :])
                    if c % TPC == TPC - 1:
                        m.then_inc(s_pmp, 1)
            pe.wait_ge(s_pmT, 8)
            for c in range(NT):
                for k in range(2):
                    m = pe.matmul(ps[:, 4 + c // 8, (c % 8) * E:(c % 8 + 1) * E], pmT[:, k, c * P:(c + 1) * P],
                                  b2n[:, k, :], start=(k == 0), stop=(k == 1))
            m.then_inc(s_sum, 1)
            pe.wait_ge(s_w2n, N_W2)
            BT, NQ = P // BLK, len(QN)
            place = [pe.alloc_register(f"place{i}") for i in range(BT * NQ)]
            with pe.Fori(0, TS // UT) as it:
                for v in range(UT + 1):
                    if v < UT:
                        pe.wait_ge(s_zt, (it * UT + v - 1 if v >= 2 else it * UT) + SEED)
                        pe.wait_ge(s_z, it * UT + v + 1)
                        for q in range(NQ):
                            m = pe.matmul(ps[:, v % 2, q * P:(q + 1) * P],
                                          zz[:, v % 2, 2 * q:2 * q + 2, :].rearrange("p k e -> p (k e)"),
                                          ident[:, :], start=True, stop=True)
                        m.then_inc(s_tz, 1)
                    if v >= 1:
                        w = v - 1
                        pe.load(place, offs[0:1, bass.ds(it * (UT * BT * NQ) + w * BT * NQ, BT * NQ)])
                        if w % 2 == 0:
                            pe.wait_ge(s_ob, (it * (UT // 2) + w // 2 - 1 if w >= 4 else it * (UT // 2)) + SEED)
                        pe.wait_ge(s_zt, it * UT + w + 1 + SEED)
                        for b in range(BT):
                            for q in range(NQ):
                                o = pe.snap(place[b * NQ + q], min_val=0, max_val=(QN[q] - 1) * E)
                                m = pe.matmul(ps[0:BLK, 2 + (w // 2) % 2, ((w % 2) * BT + b) * E:((w % 2) * BT + b + 1) * E],
                                              zt[:, w % 2, q, b * BLK:(b + 1) * BLK], w2q[q][:, bass.ds(o, E)],
                                              start=(q == 0), stop=(q == NQ - 1))
                        m.then_inc(s_blk, 1)

            turn_tokens(2)
            pe.wait_ge(s_xt, 3 * NCH)
            pe.wait_ge(s_wa, N_WA)

            def prep(u, slot, c):
                pe.wait_ge(s_ql, u + SEED)
                pe.matmul(ps[:, 5, :], wh[:, slot, :, :].rearrange("p t e -> p (t e)"), xt[:, c * BANK:(c + 1) * BANK],
                          start=True, stop=True).then_inc(s_qkp, 1)

            def scores_max(p, n, k):
                h, ic = UNITS[n % NU]
                g = n // NU * NSTEP + FIRST[n % NU] + k
                r, jc = divmod(k, ic + 1)
                w = BANK if jc < ic else (r + 1) * P
                q0 = ic * BANK + r * P
                if k == 0:
                    pe.wait_ge(s_ql, p * NU + n + 1 + SEED)
                    pe.wait_ge(s_qc, 2 * (p * NU + n + 1))
                if g >= 3:
                    pe.wait_ge(s_mxd, p * NSTEP + g - (1 if g in (4, 5) else 2) + SEED)
                m = pe.matmul(ps[:, g % 3, 0:w], q1[:, h, q0:q0 + P], k1[:, h, jc * BANK:jc * BANK + w],
                              start=True, stop=jc < ic)
                if jc == ic:
                    m = pe.matmul(ps[:, g % 3, r * P:(r + 1) * P], identb[:, :], mask_q[:, :], start=False, stop=True)
                m.then_inc(s_sm, 1)

            def turn_max(p, n):
                pe.wait_ge(s_mx4, p * NU + n + 1 + SEED)
                if n >= 1:
                    pe.wait_ge(s_hd, p * NU + n - 1 + SEED)
                for r in range(TPC):
                    m = pe.matmul(ps[0:2, 7, r * P:(r + 1) * P], mhl[:, n % 2, r, :], nident_r[:, :],
                                  start=True, stop=True)
                m.then_inc(s_mrp, 1)

            def scores_turned(p, n, k):
                h, ic = UNITS[n]
                g = FIRST[n] + k
                lo = max(0, k - 4 * ic) * P
                bank = 3 + g % 2
                pe.wait_ge(s_ex, (p * NSTEP + g - 1 if g >= 2 else p * NSTEP) + SEED)
                qs = slice(ic * BANK + lo, (ic + 1) * BANK)
                pe.matmul(ps[:, bank, lo:BANK], k1[:, h, k * P:(k + 1) * P], q1[:, h, qs], start=True, stop=False)
                m = pe.matmul(ps[:, bank, lo:BANK], k2[:, h, k * P:(k + 1) * P], q2[:, h, qs],
                              start=False, stop=k < 4 * ic)
                if k >= 4 * ic:
                    m = pe.matmul(ps[:, bank, lo:lo + P], identb[:, :], mask_k[:, :], start=False, stop=True)
                m.then_inc(s_st, 1)

            def values(p, n, k):
                h, ic = UNITS[n]
                g = FIRST[n] + k
                lo = max(0, k - 4 * ic) * P
                if k == 0:
                    pe.wait_ge(s_ot, p * NU + n + SEED)
                    if ic == 0:
                        pe.wait_ge(s_vh, p * 2 + h + 1)
                pe.wait_ge(s_ex, p * NSTEP + g + 1 + SEED)
                m = pe.matmul(ps[0:E + 1, 6, lo:BANK], vh[:, h, k, :], pt[g % 4][:, lo:BANK],
                              start=(k == 0), stop=(k == 4 * ic + 3))
                m.then_inc(s_av, 1)

            def project(p, n):
                pe.wait_ge(s_ot, p * NU + n + 1 + SEED)
                pe.wait_ge(s_hd, p * NU + n + SEED)
                for r in range(TPC):
                    m = pe.matmul(ps[:, 7, r * (E + 1):(r + 1) * (E + 1)], ot[:, r * P:(r + 1) * P],
                                  wuh[:, UNITS[n][0], :], start=True, stop=True)
                m.then_inc(s_pj, 1)

            pe.wait_ge(s_apad, 1)
            pe.wait_ge(s_qs, 2)
            for c in range(NCH):
                prep(c, 0, c)
                for t in range(c * TPC, (c + 1) * TPC):
                    if t >= 3:
                        pe.wait_ge(s_va, t - 2)
                    pe.matmul(ps[:, VB[t % 3], :], xt[:, t * P:(t + 1) * P], wv[:, :], start=True, stop=True)\
                      .then_inc(s_vp, 1)
                if c == 0:
                    for k in range(4):
                        scores_max(0, 0, k)
            pe.wait_ge(s_nir, 1)
            turn_max(0, 0)
            pe.wait_ge(s_va, NT)

            def pair(p, last):
                for n, (h, ic) in enumerate(UNITS):
                    more = n + 1 < NU or not last
                    ahead = h == 0 or not last
                    ns = ns_of(n) if more else 0
                    nt = 4 * (ic + 1)
                    pe.wait_ge(s_mr, p * NU + n + 1 + SEED)
                    if ahead and ic == 2:
                        pe.wait_ge(s_qs, 2 * (p * 2 + h + 2))
                    for k in range(nt + 3):
                        for kk in range(ns):
                            if step_at(n, kk) == k:
                                scores_max(p, n + 1, kk)
                        if k == 3 and n >= 1:
                            project(p, n - 1)
                        if k < nt:
                            scores_turned(p, n, k)
                        if k >= 3:
                            values(p, n, k - 3)
                        if ahead and k in PREP.get(ic, {}):
                            c = PREP[ic][k]
                            prep(p * NU + (h + 1) * NCH + c, (h + 1) % 2, c)
                        if more and k == turn_at(n):
                            turn_max(p, n + 1)
                if not last:
                    pe.wait_ge(s_mr, p * NU + NU + 1 + SEED)
                project(p, NU - 1)

            with pe.Fori(0, NP - 1) as p:
                pair(p, False)
            pair(NP - 1, True)

            turn_tokens(3)
            pe.wait_ge(s_xt, 4 * NCH)
            pe.wait_ge(s_we, N_WE)
            for c in range(NT):
                m = pe.matmul(ps[:, 4, c * NE:(c + 1) * NE], xt[:, c * P:(c + 1) * P], gw[:, :], start=True, stop=True)
            m.then_inc(s_lg, 1)
            pe.transpose(ps[:, 5, 0:NE], b1[:, :], ident[0:NE, 0:NE]).then_inc(s_b1p, 1)
            pe.wait_ge(s_g, 1)
            pe.wait_ge(s_b1T, 1)
            pe.wait_ge(s_xl, NCH)
            for c in range(NT):
                ts = slice((c % TPC) * P, (c % TPC + 1) * P)
                pe.matmul(ps[0:96, c // TPC, ts], g3[:, c, :], identb[:, :], start=True, stop=True)
                m = pe.transpose(ps[0:NE, 4 + c // TPC, ts], ge[:, c, :], ident[:, :])
                if c % TPC == TPC - 1:
                    m.then_inc(s_gt, 1)
            pe.wait_ge(s_gp, NCH)
            pe.wait_ge(s_gTs, NCH)
            pe.wait_ge(s_wl, 2)
            pe.wait_ge(s_id2, 1)

            def up(c, e, first):
                g = c * NE + e
                if e >= 2 or not first:
                    pe.wait_ge(s_rl, g - 1 + SEED)
                for k in range(2):
                    m = pe.matmul(ps[:, e % 2, :], w1p[:, k, e * FF:(e + 1) * FF], x1[:, bass.ds(c * BANK, BANK)],
                                  start=(k == 0), stop=(k == 1))
                m.then_inc(s_m1, 1)
                if e >= 2 or not first:
                    pe.wait_ge(s_hg, g - 1 + SEED)
                pe.matmul(ps[:, 2 + e % 2, :], sel[:, e, :], bc[:, bass.ds(c * BANK, BANK)],
                          start=True, stop=True).then_inc(s_gb, 1)

            def down(c, w):
                if w % 2:
                    pe.wait_ge(s_hlp, c * (NE // 2) + w // 2 + 1)
                else:
                    pe.wait_ge(s_hld, c * (NE // 2) + w // 2 + 1)
                for k in range(2):
                    m = pe.matmul(ps[:, 4, :], w2p[:, w, :, :].rearrange("p k e -> p (k e)"), hp[:, k, w % HR, :],
                                  start=False, stop=(w == NE - 1 and k == 1))
                m.then_inc(s_m2, 1)

            def finish(c):
                pe.wait_ge(s_yt, c + 1 + SEED)
                pe.wait_ge(s_ya, c + SEED)
                for r in range(TPC):
                    m = pe.matmul(ps[:, 5, r * E:(r + 1) * E], yt[:, r * P:(r + 1) * P], ident2[:, :],
                                  start=True, stop=True)
                m.then_inc(s_ytp, 1)

            def chunk(c, before, first):
                for e in range(NE):
                    up(c, e, first)
                    if e == LAG:
                        pe.wait_ge(s_yt, c + SEED)
                        pe.matmul(ps[:, 4, :], b2[:, :], gT[:, bass.ds(c * BANK, BANK)], start=True, stop=False)
                    if e >= LAG:
                        down(c, e - LAG)
                    elif not first:
                        down(before, NE - LAG + e)
                    if e == LAG + 1 and not first:
                        finish(before)

            chunk(0, None, True)
            with pe.Fori(0, NCH - 1) as i:
                chunk(i + 1, i, False)
            for w in range(NE - LAG, NE):
                down(NCH - 1, w)
            finish(NCH - 1)

        @block.scalar
        def _(act):
            for s in (s_zt, s_ex, s_ot, s_yt):
                act.sem_inc(s, SEED)
            def table(func, k):
                act.activation(spare[:, k:k + 1], ident[:, 0:1], func)

            def ln_std(n, tiles=slice(0, NT)):
                act.wait_ge(s_var, n + 1)
                act.activation(stat[:, 3, tiles], stat[:, 2, tiles], ACT.Sqrt).then_inc(s_std, 1)

            def turned(k):
                for c in range(NCH):
                    act.wait_ge(s_xtp, k * NCH + c + 1)
                    act.activation(xt[0:E, c * BANK:(c + 1) * BANK], ps[0:E, c, :], ACT.Copy).then_inc(s_xt, 1)

            act.wait_ge(s_ident, 1)
            act.wait_ge(s_wm, N_WM)
            act.activation(neg_a[:, :], alog[:, :], ACT.Exp).then_inc(step_s, 1)
            act.wait_ge(step_s, 1)
            act.mul(neg_a[:, :], neg_a[:, :], -1.0).then_inc(step_s, 1)
            act.wait_ge(s_pad, 1)
            act.wait_ge(s_wps, 1)
            for dst, src in (
                (dtwT[:, :], ps[0:RK, 5, P:2 * P]),
                (wconv[:, :, :], ps[:, 4, 0:2 * P].rearrange("p (k n) -> p k n", k=2)),
                (wz[0:E, :], ps[0:E, 4, 2 * P:3 * P]), (wg[0:E, :], ps[0:E, 4, 3 * P:3 * P + E]),
                (wbc[:, :], ps[:, 5, RK:RK + 2 * DS]), (woT[:, :], ps[:, 5, 2 * P:2 * P + E]),
            ):
                last = act.activation(dst, src, ACT.Copy)
            last.then_inc(s_wsb, 1)
            act.wait_ge(s_wdp, 1)
            act.activation(wdelta[:, :], ps[:, 6, 0:DI], ACT.Copy).then_inc(s_wds, 1)
            table(ACT.Sqrt, 0)
            for h, tiles in enumerate(HALVES):
                ln_std(2 * h, tiles)
                ln_std(2 * h + 1, tiles)
            for c in range(NCH):
                act.wait_ge(s_xtp, c + 1)
                act.activation(x2[0:E, 3 + c * BANK:3 + (c + 1) * BANK], ps[0:E, c, :], ACT.Identity,
                               bias=bet[:, :], scale=gam[:, :])
                act.activation(x2[E:P, 4 + c * BANK:4 + (c + 1) * BANK], ps[0:E, c, :], ACT.Identity,
                               bias=bet[:, :], scale=gam[:, :]).then_inc(s_xt, 1)
            for c in range(NCH + 1):
                if c < NCH:
                    cs = slice(c * BANK, (c + 1) * BANK)
                    b = inb(c)
                    act.wait_ge(s_in, c + 1)
                    act.activation(u[:, cs], ps[:, b, :], ACT.Silu, bias=convb[:, :]).then_inc(s_u, 1)
                    act.activation(sz[:, cs], ps[:, b + 1, :], ACT.Silu)
                    act.activation(gsig[:, cs], ps[0:E, b + 2, :], ACT.Identity, bias=gateb[:, :]).then_inc(s_zg, 1)
                if c >= 1:
                    act.wait_ge(s_dlp, c)
                    act.activation(spl[:, c - 1, :], ps[:, 7, :], ACT.Abs, bias=dtb[:, :]).then_inc(s_abs, 1)
            for c in range(NCH):
                act.wait_ge(s_abs, c + 1)
                act.activation(spl[:, c, :], spl[:, c, :], ACT.Exp, scale=-1.0).then_inc(step_s, 1)
            for c in range(NCH):
                act.wait_ge(step_s, 3 + c)
                act.activation(spl[:, c, :], spl[:, c, :], ACT.Ln, bias=1.0).then_inc(s_ln1, 1)
            act.wait_ge(s_zf, 4 * 16)
            with act.Fori(0, NCH) as c:
                for s in range(DS):
                    if s == 0:
                        act.wait_ge(s_dcur, c + 1)
                    act.wait_ge(s_scan, (c * DS + s - 1 if s >= 2 else c * DS) + SEED)
                    act.activation(dA[:, s % 2, :], dcur[:, :], ACT.Exp,
                                   scale=neg_a[:, s:s + 1]).then_inc(s_da, 1)
            act.wait_ge(s_zg, NCH)
            act.activation(gsig[:, :], gsig[:, :], ACT.Sigmoid).then_inc(s_zg, 1)

            table(ACT.Sqrt, 1)
            ln_std(4)
            act.wait_ge(s_w1p, 1)
            act.activation(w1T[0:E, 0:ND], ps[0:E, 7, 0:ND], ACT.Copy).then_inc(s_w1T, 1)
            turned(1)
            for b in range(NT // 2):
                act.wait_ge(s_sc, 2 * b + 2)
                act.activation(sc[:, 2 * b:2 * b + 2, 0:ND],
                               ps[:, (4 + b) % 8, :].rearrange("p (c n) -> p c n", n=NDP)[:, :, 0:ND], ACT.Copy)\
                   .then_inc(s_sce, 1)
            table(ACT.Gelu, 5)
            act.wait_ge(s_ls, 1)
            act.activation(pw[:, :, :], ls[:, :, :], ACT.Gelu).then_inc(s_pw, 1)
            for b in range(8):
                act.wait_ge(s_pmp, b + 1)
                act.activation(pmT[:, b // 4, (b % 4) * BANK:(b % 4 + 1) * BANK], ps[:, b, :], ACT.Copy)\
                   .then_inc(s_pmT, 1)
            act.wait_ge(s_sum, 1)
            with act.Fori(0, TS // UT) as it:
                for v in range(UT):
                    act.wait_ge(s_tz, it * UT + v + 1 + SEED)
                    act.wait_ge(s_blk, (it * UT + v - 1 if v >= 2 else it * UT) + SEED)
                    act.activation(zt[:, v % 2, :, :].rearrange("p q s -> p (q s)"), ps[:, v % 2, :], ACT.Copy)\
                       .then_inc(s_zt, 1)

            table(ACT.Sqrt, 2)
            for h, tiles in enumerate(HALVES):
                ln_std(5 + h, tiles)
            turned(2)
            table(ACT.Exp, 6)
            def hi_parts(u, slot, c):
                cs = slice(c * BANK, (c + 1) * BANK)
                act.wait_ge(s_qkp, u + 1)
                act.activation(q1[0:E, slot, cs], ps[0:E, 5, :], ACT.Copy, scale=float(E) ** -0.5)
                act.activation(k1[0:E, slot, cs], ps[E:P, 5, :], ACT.Copy).then_inc(s_qh, 1)

            for c in range(NCH):
                hi_parts(c, 0, c)
                for t in range(c * TPC, (c + 1) * TPC):
                    act.wait_ge(s_vp, t + 1)
                    act.activation(vall[:, t, :], ps[:, VB[t % 3], :], ACT.Copy).then_inc(s_va, 1)

            def pair(p, last):
                for n, (h, ic) in enumerate(UNITS):
                    for k in range(4 * (ic + 1)):
                        if (h == 0 or not last) and k in PREP.get(ic, {}):
                            c = PREP[ic][k]
                            hi_parts(p * NU + (h + 1) * NCH + c, (h + 1) % 2, c)
                        g = FIRST[n] + k
                        lo = max(0, k - 4 * ic) * P
                        act.wait_ge(s_st, p * NSTEP + g + 1)
                        act.wait_ge(s_av, (p * NSTEP + g - 3 if g >= 4 else p * NSTEP) + SEED)
                        act.activation(pt[g % 4][:, lo:BANK], ps[:, 3 + g % 2, lo:BANK], ACT.Exp).then_inc(s_ex, 1)
                    act.wait_ge(s_av, p * NSTEP + FIRST[n + 1] + SEED)
                    act.wait_ge(s_pj, p * NU + n + SEED)
                    act.activation(ot[:, :], ps[0:E + 1, 6, :], ACT.Copy).then_inc(s_ot, 1)

            with act.Fori(0, NP - 1) as p:
                pair(p, False)
            pair(NP - 1, True)

            act.wait_ge(s_hd, NP * NU + SEED)
            act.wait_ge(s_we, N_WE)
            act.activation(w1p[:, 0, :], w1[:, :, :].rearrange("p n f -> p (n f)"), ACT.Copy).then_inc(s_wh, 1)
            table(ACT.Sqrt, 3)
            ln_std(7)
            turned(3)
            for c in range(NCH):
                act.activation(x1[0:E, c * BANK:(c + 1) * BANK], ps[0:E, c, :], ACT.Copy).then_inc(s_xh, 1)
            act.activation(w2p[:, :, 0, :], w2[:, :, :], ACT.Copy).then_inc(s_wh, 1)
            act.wait_ge(s_b1p, 1)
            act.activation(b1T[:, :], ps[:, 5, 0:NE], ACT.Copy).then_inc(s_b1T, 1)
            act.wait_ge(s_d, 1)
            act.activation(tw[:, 1, :], tw[:, 0, :], ACT.Exp).then_inc(s_e, 1)
            act.wait_ge(s_gp0, 1)
            for c in range(NCH):
                act.wait_ge(s_gt, c + 1)
                act.activation(gT[0:NE, c * BANK:(c + 1) * BANK], ps[0:NE, 4 + c, :], ACT.Copy).then_inc(s_gTs, 1)
            act.sem_inc(s_rl, SEED)
            act.sem_inc(s_hh, SEED)

            def hidden_hi(c, w, first):
                act.wait_ge(s_hg, c * NE + w + 1 + SEED)
                if w >= HR or not first:
                    act.wait_ge(s_m2, c * NE + w - HR + 1 + SEED)
                act.activation(hp[:, 0, w % HR, :], hg[:, w % 4, :], ACT.Copy).then_inc(s_hh, 1)

            def summed(c):
                act.wait_ge(s_m2, c * NE + NE + SEED)
                act.wait_ge(s_ytp, c + SEED)
                act.activation(yt[:, :], ps[:, 4, :], ACT.Copy).then_inc(s_yt, 1)

            def chunk(c, before, first):
                for e in range(NE):
                    act.wait_ge(s_m1, c * NE + e + 1)
                    if e >= 2 or not first:
                        act.wait_ge(s_hg, c * NE + e - 1 + SEED)
                    act.activation(hr[:, e % 2, :], ps[:, e % 2, :], ACT.Relu, bias=b1T[:, e:e + 1]).then_inc(s_rl, 1)
                    if e >= 1:
                        hidden_hi(c, e - 1, first)
                    elif not first:
                        hidden_hi(before, NE - 1, False)
                    if e == LAG and not first:
                        summed(before)

            chunk(0, None, True)
            with act.Fori(0, NCH - 1) as i:
                chunk(i + 1, i, False)
            hidden_hi(NCH - 1, NE - 1, False)
            summed(NCH - 1)
            table(ACT.Sqrt, 4)
            ln_std(8)

        @block.vector
        def _(dve):
            st = Steps(dve, step_v)
            for s in (s_dbu, s_hc, s_y, s_h1, s_mxd, s_mx4, s_hd,
                      s_ob, s_hg, s_ya, s_scan, s_mr, s_mo, s_ql):
                dve.sem_inc(s, SEED)

            def layernorm(src, dst, n, tiles=slice(0, NT)):
                def wide(k):
                    return stat[:, k, tiles].unsqueeze(2).to_broadcast([P, tiles.stop - tiles.start, E])

                st.after()
                st.did(dve.tensor_reduce(stat[:, 0, tiles], src[:, tiles, :], AX_X, ALU.add))
                st.after()
                st.did(dve.tensor_scalar(stat[:, 0, tiles], stat[:, 0, tiles], -1.0 / E, None, ALU.mult))
                st.after()
                st.did(dve.tensor_tensor(cen[:, tiles, :], src[:, tiles, :], wide(0), ALU.add))
                st.after()
                st.did(dve.tensor_tensor(sq[:, tiles, :], cen[:, tiles, :], cen[:, tiles, :], ALU.mult))
                st.after()
                st.did(dve.tensor_reduce(stat[:, 1, tiles], sq[:, tiles, :], AX_X, ALU.add))
                st.after()
                dve.tensor_scalar(stat[:, 2, tiles], stat[:, 1, tiles], 1.0 / E, EPS, ALU.mult, ALU.add)\
                   .then_inc(s_var, 1)
                dve.wait_ge(s_std, n + 1)
                st.did(dve.reciprocal(stat[:, 4, tiles], stat[:, 3, tiles]))
                st.after()
                st.did(dve.tensor_tensor(dst[:, tiles, :], cen[:, tiles, :], wide(4), ALU.mult))

            dve.wait_ge(s_ids, 16)
            dve.tensor_copy(idr[:, :], ids[:, :]).then_inc(s_idr, 1)
            dve.wait_ge(s_idt, 1)
            st.did(dve.tensor_copy(idf[:, 0, :], ps[:, 7, 0:NT]))
            st.after()
            st.did(dve.tensor_scalar(idf[:, 1, :], idf[:, 0, :], 0.0, float(V), ALU.is_lt, ALU.mult))
            st.after()
            st.did(dve.tensor_tensor(idf[:, 0, :], idf[:, 0, :], idf[:, 1, :], ALU.add))
            st.after()
            st.did(dve.tensor_scalar(idf[:, 0, :], idf[:, 0, :], 0.0, float(V - 1), ALU.max, ALU.min))
            st.after()
            dve.tensor_scalar(rows[:, :], idf[:, 0, :], float(HID // E), float(LAYER), ALU.mult, ALU.add)\
               .then_inc(s_rows, 1)
            for t in (x2[:, 0:4], wz[E:P, :], wg[E:P, :], hs[:, :, 0:1], xt[E:P, :]):
                st.did(dve.memset(t, 0.0))
            st.after()
            st.did(dve.memset(xt[E:E + 1, :], 1.0))
            st.after()
            dve.sem_inc(s_pad, 1)
            dve.wait_ge(s_wm, N_WM)
            for k in range(KC):
                st.did(dve.tensor_scalar(wtap[:, k, :], win[:, 0, :], convw[:, KC - 1 - k:KC - k], None, ALU.mult))
            st.after()
            dve.sem_inc(s_wtap, 1)

            for h, tiles in enumerate(HALVES):
                dve.wait_ge(s_emb[h], HT * 16)
                layernorm(h0, xn, 2 * h, tiles)
                st.after()
                st.did(dve.tensor_tensor(h1[:, tiles, :], h0[:, tiles, :], xn[:, tiles, :], ALU.add))
                layernorm(xn, xn, 2 * h + 1, tiles)
                st.after()
                dve.sem_inc(s_xn, 1)
            for c in range(NCH):
                cs = slice(c * BANK, (c + 1) * BANK)
                dve.wait_ge(s_abs, c + 1)
                st.did(dve.tensor_scalar(delta[:, cs], ps[:, 7, :], dtb[:, :], 0.0, ALU.add, ALU.max))
                dve.wait_ge(s_bcp, c + 1)
                st.did(dve.tensor_copy(bc[0:32, cs], ps[0:32, 3, :]))
                st.after()
                st.did(dve.tensor_tensor(res1[:, :], ps[0:32, 3, :], bc[0:32, cs], ALU.subtract))
                st.after()
                st.did(dve.tensor_copy(mid[:, :], res1[:, :]))
                st.after()
                st.did(dve.tensor_tensor(res2[:, :], res1[:, :], mid[:, :], ALU.subtract))
                st.did(dve.tensor_copy(bc[32:64, cs], mid[:, :]))
                st.after()
                dve.tensor_copy(bc[64:96, cs], res2[:, :]).then_inc(s_bch, 1)
                dve.wait_ge(s_bch, c + 1)
            for c in range(NCH):
                cs = slice(c * BANK, (c + 1) * BANK)
                dve.wait_ge(s_ln1, c + 1)
                st.did(dve.tensor_tensor(delta[:, cs], delta[:, cs], spl[:, c, :], ALU.add))
                st.after()
                dve.wait_ge(s_u, c + 1)
                dve.tensor_tensor(du[:, cs], delta[:, cs], u[:, cs], ALU.mult).then_inc(s_dl, 1)
            dve.wait_ge(s_dl, NCH)
            n0 = st.n

            def gate_sum(c):
                cd = bass.ds(c * BANK, BANK)
                dve.wait_ge(s_yac, (c + 1) * (DS - 1) + SEED)
                dve.scalar_tensor_tensor(yb[:, 0, :], u[:, cd], dskip[:, :], hc_sum[:, :], ALU.mult, ALU.add)\
                   .then_inc(step_v, 1)
                dve.wait_ge(step_v, n0 + c + 1)
                dve.wait_ge(s_op, c + SEED)
                dve.tensor_tensor(yb[:, 1, :], yb[:, 0, :], sz[:, cd], ALU.mult).then_inc(s_y, 1)

            def scan_chunk(c, before, first):
                cd = bass.ds(c * BANK, BANK)
                dve.tensor_copy(dcur[:, :], delta[:, cd]).then_inc(s_dcur, 1)
                for s in range(DS + 1):
                    if s < DS:
                        dve.wait_ge(s_bb, c * DS + s + 1)
                        dve.tensor_tensor(dbu[:, s % 2, :], du[:, cd], ps[:, s % 2, :], ALU.mult).then_inc(s_dbu, 1)
                    if s >= 1:
                        dve.wait_ge(s_cb, c * DS + s)
                        dve.wait_ge(s_scan, c * DS + s + SEED)
                        if s >= 5:
                            dve.wait_ge(s_yac, c * (DS - 1) + max(1, s - 5) + SEED)
                        elif not first:
                            dve.wait_ge(s_yac, c * (DS - 1) - (4 - s) + SEED)
                        dve.tensor_tensor(hc[:, (s - 1) % 4, :], hs[:, s - 1, 1:BANK + 1], ps[:, 2 + (s - 1) % 2, :],
                                          ALU.mult).then_inc(s_hc, 1)
                    if s < DS:
                        dve.wait_ge(s_da, c * DS + s + 1)
                        dve.wait_ge(s_dbu, c * DS + s + 1 + SEED)
                        if s == 0:
                            dve.wait_ge(s_h1, c + SEED)
                        dve.tensor_tensor_scan(hs[:, s, 1:BANK + 1], dA[:, s % 2, :], dbu[:, s % 2, :],
                                               hs[:, s, 0:1], ALU.mult, ALU.add).then_inc(s_scan, 1)
                    if s == GATE_AT and not first:
                        gate_sum(before)
                dve.wait_ge(s_hc, c * DS + DS + SEED)
                dve.tensor_copy(hs[:, :, 0:1], hs[:, :, BANK:BANK + 1]).then_inc(s_h1, 1)

            scan_chunk(0, None, True)
            with dve.Fori(0, NCH - 1) as i:
                scan_chunk(i + 1, i, False)
            gate_sum(NCH - 1)
            st.n = n0 + NCH
            dve.wait_ge(s_zg, NCH + 1)
            for c in range(NCH + 1):
                if c < NCH:
                    dve.wait_ge(s_op, c + 1 + SEED)
                    if c >= 2:
                        dve.wait_ge(s_mt, c - 1 + SEED)
                    dve.tensor_tensor(mo[:, c % 2, :], ps[0:E, 4 + c, :], gsig[:, c * BANK:(c + 1) * BANK], ALU.mult)\
                       .then_inc(s_mo, 1)
                if c >= 1:
                    dve.wait_ge(s_mt, c + SEED)
                    hv = h1[:, (c - 1) * TPC:c * TPC, :]
                    dve.tensor_tensor(hv, hv, ps[:, (c - 1) % 2, 0:TPC * E].rearrange("p (r e) -> p r e", e=E), ALU.add)\
                       .then_inc(s_h1, 1)
            dve.wait_ge(s_h1, 2 * NCH + SEED)

            layernorm(h1, xn, 4)
            st.after()
            dve.sem_inc(s_xn, 1)
            st.did(dve.tensor_copy(pay[:, :, 0:E], xn[:, :, :]))
            st.did(dve.memset(mk[:, :, 0:1], 1.0))
            st.did(dve.memset(mk[:, :, ND:NDP], 0.0))
            for h, tiles in enumerate(HALVES):
                dve.wait_ge(s_sce, (h + 1) * (HT // 2))
                st.did(dve.memset(sc[:, tiles, ND:NDP], 0.0))
                for i in range(DL - 1):
                    lo, n = 2 ** i - 1, 2 ** i
                    kids = mk[:, tiles, 2 * lo + 1:2 * lo + 1 + 2 * n].rearrange("p c (n h) -> p c n h", h=2)
                    left, right = kids[:, :, :, 0], kids[:, :, :, 1]
                    st.after()
                    st.did(dve.scalar_tensor_tensor(right, sc[:, tiles, lo:lo + n], 0.0, mk[:, tiles, lo:lo + n],
                                                    ALU.is_gt, ALU.mult))
                    st.after()
                    st.did(dve.tensor_tensor(left, mk[:, tiles, lo:lo + n], right, ALU.subtract))
                st.after()
            leaf = mk[:, :, NL - 1:ND]
            st.did(dve.tensor_copy(ohb[:, :, :], leaf))
            st.did(dve.tensor_copy(pre[:, 0, :], mk[:, 0, NL - 1:ND]))
            for c in range(1, NT):
                st.after()
                st.did(dve.tensor_tensor(pre[:, c, :], pre[:, c - 1, :], ohb[:, c, :], ALU.add))
            st.after()
            dve.sem_inc(s_oh, 1)
            st.did(dve.tensor_tensor(sc[:, :, :], sc[:, :, :], mk[:, :, :], ALU.mult))
            st.after()
            for i in range(DL):
                lo, n = 2 ** i - 1, 2 ** i
                st.did(dve.tensor_reduce(ls[:, :, DL - 1 - i:DL - i].rearrange("p c o -> p (c o)"), sc[:, :, lo:lo + n],
                                         AX_X, ALU.add))
            st.after()
            st.did(dve.scalar_tensor_tensor(ls[:, :, :], ls[:, :, :], -1.0, ls[:, :, :], ALU.mult, ALU.max))
            st.after()
            dve.sem_inc(s_ls, 1)
            st.did(dve.memset(onesf[:, :], 1.0))
            dve.wait_ge(s_cnt, 1)
            st.did(dve.tensor_scalar(cnt[:, :], ps[:, 6, 0:NL], float(BLK - 1), None, ALU.add))
            st.after()
            st.did(dve.tensor_scalar(cnt[:, :], cnt[:, :], SH, None, ALU.logical_shift_right))
            st.after()
            st.did(dve.tensor_copy(nbf[:, :], cnt[:, :]))
            st.after()
            st.did(dve.tensor_tensor_scan(cumend[:, :], onesf[:, :], nbf[:, :], 0.0, ALU.mult, ALU.add))
            st.after()
            st.did(dve.tensor_tensor(base[:, :], cumend[:, :], nbf[:, :], ALU.subtract))
            st.after()
            st.did(dve.tensor_scalar(base[:, :], base[:, :], float(BLK), None, ALU.mult))
            dve.wait_ge(s_rkp, 1)
            st.after()
            for c in range(NCH):
                st.did(dve.tensor_tensor(rank[:, c * TPC:(c + 1) * TPC, :], ps[:, c, :].rearrange("p (r n) -> p r n", n=NL),
                                         base[:, :].unsqueeze(1).to_broadcast([P, TPC, NL]), ALU.add))
            st.after()
            st.did(dve.tensor_tensor(rank[:, :, :], rank[:, :, :], leaf, ALU.mult))
            st.after()
            st.did(dve.tensor_reduce(slot[:, :], rank[:, :, :], AX_X, ALU.add))
            st.after()
            st.did(dve.tensor_copy(slot_i[:, 0, :], slot[:, :]))
            st.after()
            st.did(dve.tensor_scalar(slot_i[:, 1, :], slot_i[:, 0, :], P.bit_length() - 1, None, ALU.logical_shift_right))
            st.did(dve.tensor_scalar(slot_i[:, 2, :], slot_i[:, 0, :], P - 1, None, ALU.bitwise_and))
            st.after()
            st.did(dve.tensor_copy(idf2[:, 0, :], slot_i[:, 1, :]))
            st.did(dve.tensor_copy(idf2[:, 1, :], slot_i[:, 2, :]))
            st.after()
            st.did(dve.scalar_tensor_tensor(slot[:, :], idf2[:, 1, :], float(TS), idf2[:, 0, :], ALU.mult, ALU.add))
            st.after()
            st.did(dve.tensor_copy(rows[:, :], slot[:, :]))
            st.after()
            dve.sem_inc(s_slot, 1)
            dve.wait_ge(s_pw, 1)
            st.did(dve.tensor_copy(pay[:, :, E:PL], pw[:, :, :]))
            st.after()
            dve.sem_inc(s_pay, 1)
            dve.wait_ge(s_const, 1)
            for k in range(2):
                st.after()
                st.did(dve.tensor_scalar(onesf[:, :], cumend[:, :], iota_b[:, k:k + 1], None, ALU.is_le))
                st.after()
                st.did(dve.tensor_reduce(nbf[:, k:k + 1], onesf[:, :], AX_X, ALU.add))
            st.after()
            dve.tensor_scalar(nbf[:, 0:2], nbf[:, 0:2], float(NL - 1), None, ALU.min).then_inc(s_lc, 1)
            dve.wait_ge(s_lr, 1)
            st.did(dve.tensor_copy(cnt_row, ps[0:1, 7, 0:NB]))
            offq = offs[:, :].rearrange("p (b q) -> p b q", q=len(QN))
            for q in range(len(QN)):
                st.after()
                st.did(dve.tensor_scalar(offq[:, :, q], cnt_row, 2 * q, E.bit_length() - 1,
                                         ALU.logical_shift_right, ALU.logical_shift_left))
            st.after()
            dve.sem_inc(s_offs, 1)
            for i in range(DL):
                lo, n = 2 ** i - 1, 2 ** i
                st.did(dve.tensor_tensor(sc[:, :, lo:lo + n], mk[:, :, lo:lo + n],
                                         pw[:, :, DL - 1 - i:DL - i].to_broadcast([P, NT, n]), ALU.mult))
            st.after()
            dve.sem_inc(s_pm, 1)
            dve.wait_ge(s_sum, 1)
            for k in range(2):
                hv = h1[:, 8 * k:8 * k + 8, :]
                st.did(dve.tensor_tensor(hv, hv, ps[:, 4 + k, :].rearrange("p (r e) -> p r e", e=E), ALU.add))
            dve.wait_ge(s_xs, 16)
            with dve.Fori(0, TS // UT) as it:
                for v in range(UT + 2):
                    if v < UT:
                        dve.wait_ge(s_tz, (it * UT + v - 1 if v >= 2 else it * UT) + SEED)
                        xv = xsb[:, bass.ds(it * UT + v, 1), :]
                        dve.tensor_tensor(zz[:, v % 2, :, :], xv[:, :, 0:E].to_broadcast([P, DL, E]),
                                          xv[:, :, E:PL].rearrange("p o k -> p (o k)").unsqueeze(2).to_broadcast([P, DL, E]),
                                          ALU.mult).then_inc(s_z, 1)
                    if v % 2 == 1 and v >= 3:
                        w = (v - 3) // 2
                        dve.wait_ge(s_blk, it * UT + 2 * w + 2 + SEED)
                        pv = ps[0:BLK, 2 + w % 2, :].rearrange("p (t b e) -> p t b e", t=2, e=E)
                        for b in range(P // BLK):
                            last = dve.tensor_copy(ob[b * BLK:(b + 1) * BLK, bass.ds(it * UT + 2 * w, 2), :], pv[:, :, b, :])
                        last.then_inc(s_ob, 1)
            dve.wait_ge(s_obs, 16)
            dve.wait_ge(s_blk, TS + SEED)
            st.did(dve.memset(q2[E:P, :, :].bitcast(F32), 0.0))
            st.did(dve.memset(k2[E:P, :, :].bitcast(F32), 0.0))
            st.did(dve.memset(vh[:, :, :, E:E + 1], 1.0))
            st.after()
            st.did(dve.memset(k2[E:E + 2, :, :].bitcast(F32), 1.0))
            st.after()
            dve.sem_inc(s_apad, 1)
            for h, tiles in enumerate(HALVES):
                dve.wait_ge(s_res[h], HT * 16)
                st.did(dve.tensor_tensor(h1[:, tiles, :], h1[:, tiles, :], res[:, tiles, :], ALU.add))
                layernorm(h1, xn, 5 + h, tiles)
                st.after()
                dve.sem_inc(s_xn, 1)
            dve.wait_ge(s_wa, N_WA)
            st.did(dve.tensor_tensor(h3[:, :, :], h1[:, :, :], bub[:, :].unsqueeze(1).to_broadcast([P, NT, E]), ALU.add))
            st.after()

            def lo_parts(u, slot, c):
                cs = slice(c * BANK, (c + 1) * BANK)
                dve.wait_ge(s_qh, u + 1)
                dve.scalar_tensor_tensor(q1[E:P, slot, cs], ps[0:E, 5, :], float(E) ** -0.5,
                                         q1[0:E, slot, cs].bitcast(F32), ALU.mult, ALU.subtract)
                dve.tensor_tensor(k2[0:E, slot, cs], ps[E:P, 5, :], k1[0:E, slot, cs].bitcast(F32), ALU.subtract)\
                   .then_inc(s_ql, 1)

            def take_max(p, n, at=None):
                h, ic = UNITS[n % NU]
                ns = 4 * (ic + 1)
                for k in range(ns):
                    if at and k in at:
                        at[k]()
                    g = n // NU * NSTEP + FIRST[n % NU] + k
                    r, jc = divmod(k, ic + 1)
                    w = BANK if jc < ic else (r + 1) * P
                    dve.wait_ge(s_sm, p * NSTEP + g + 1)
                    dve.tensor_reduce(mx[:, n % 2, r, jc:jc + 1], ps[:, g % 3, 0:w], AX_X, ALU.max).then_inc(s_mxd, 1)
                dve.wait_ge(s_mxd, p * NSTEP + n // NU * NSTEP + FIRST[n % NU] + ns + SEED)
                u = p * NU + n
                dve.tensor_reduce(mx4[:, n % 2, :], mx[:, n % 2, :, 0:ic + 1], AX_X, ALU.max).then_inc(s_mh, 1)
                dve.wait_ge(s_mh, 2 * u + 1)
                dve.tensor_copy(mhl[:, n % 2, :, 0], mx4[:, n % 2, :]).then_inc(s_mh, 1)
                dve.wait_ge(s_mh, 2 * u + 2)
                dve.tensor_tensor(mhl[:, n % 2, :, 1], mx4[:, n % 2, :], mhl[:, n % 2, :, 0].bitcast(F32),
                                  ALU.subtract).then_inc(s_mx4, 1)

            def max_row(p, n):
                h, ic = UNITS[n % NU]
                cs = slice(ic * BANK, (ic + 1) * BANK)
                dve.wait_ge(s_mrp, p * NU + n + 1)
                dve.tensor_copy(q2[E:E + 2, h, cs], ps[0:2, 7, :]).then_inc(s_mr, 1)

            def add_head(p, n, m0):
                h, ic = UNITS[n]
                dve.wait_ge(s_pj, p * NU + n + 1 + SEED)
                v = ps[:, 7, 0:TPC * (E + 1)].rearrange("p (r e) -> p r e", e=E + 1)
                m = m0 + p * (2 * NU + 2)
                k = 2 * n + (n > 0) + (n > NCH)
                dve.reciprocal(rden[:, 0, :], v[:, :, E:E + 1].rearrange("p r o -> p (r o)")).then_inc(step_v, 1)
                k += 1
                dve.wait_ge(step_v, m + k)
                if ic == 0:
                    dve.memset(rden[0:1, 0, 0:1], 0.0).then_inc(step_v, 1)
                    k += 1
                    dve.wait_ge(step_v, m + k)
                dve.tensor_tensor(on[:, :, :], v[:, :, 0:E], rden[:, 0, :].unsqueeze(2).to_broadcast([P, TPC, E]),
                                  ALU.mult).then_inc(step_v, 1)
                k += 1
                dve.wait_ge(step_v, m + k)
                hv = h3[:, ic * TPC:(ic + 1) * TPC, :]
                dve.tensor_tensor(hv, hv, on[:, :, :], ALU.add).then_inc(s_hd, 1)

            dve.wait_ge(s_apad, 1)
            st.did(dve.tensor_copy(nident_r[:, :], nident[:, :]))
            st.after()
            dve.sem_inc(s_nir, 1)
            n0 = st.n
            for c in range(NCH):
                lo_parts(c, 0, c)
                if c == 0:
                    take_max(0, 0)
            max_row(0, 0)

            def pair(p, last):
                for n, (h, ic) in enumerate(UNITS):
                    more = n + 1 < NU or not last
                    ahead = h == 0 or not last
                    ns = ns_of(n) if more else 0
                    add = [lambda: add_head(p, n - 1, n0)] if n >= 1 else []
                    pre = [lambda c=c: lo_parts(p * NU + (h + 1) * NCH + c, (h + 1) % 2, c)
                           for c in PREP.get(ic, {}).values()] if ahead else []
                    at = {}
                    if ns > 8 and add:
                        at[8] = add.pop()
                    if ns > 8 and pre:
                        at[10] = pre.pop(0)
                    if more:
                        take_max(p, n + 1, at)
                    for f in add + pre[:1]:
                        f()
                    if more:
                        max_row(p, n + 1)
                    for f in pre[1:]:
                        f()
                add_head(p, NU - 1, n0)

            with dve.Fori(0, NP - 1) as p:
                pair(p, False)
            pair(NP - 1, True)
            st.n = n0 + NP * (2 * NU + 2)
            dve.wait_ge(s_hd, NP * NU + SEED)

            st.did(dve.memset(g3[:, :, :], 0.0))
            st.did(dve.memset(gT[:, :], 0.0))
            st.did(dve.tensor_tensor(ident2[:, :], ident[:, 0:E], ident[:, E:P], ALU.add))
            st.after()
            dve.sem_inc(s_id2, 1)
            dve.sem_inc(s_gp0, 1)
            layernorm(h3, xn, 7)
            st.after()
            dve.sem_inc(s_xn, 1)
            dve.wait_ge(s_lg, 1)
            st.did(dve.tensor_copy(lg[:, :, :], ps[:, 4, 0:NT * NE].rearrange("p (c e) -> p c e", e=NE)))
            st.after()
            for c in range(NT):
                st.did(dve.max(out=top[:, c, :], in_=lg[:, c, :]))
            st.after()
            for c in range(NT):
                st.did(dve.max_index(out=topi[:, c, :], in_max=top[:, c, :], in_values=lg[:, c, :]))
            dve.tensor_tensor(tw[:, 0, :], top[:, :, 1:2].rearrange("p c o -> p (c o)"),
                              top[:, :, 0:1].rearrange("p c o -> p (c o)"), ALU.subtract).then_inc(s_d, 1)
            st.after()
            st.did(dve.tensor_copy(topf[:, :, :], topi[:, :, 0:2]))
            dve.wait_ge(s_e, 1)
            st.did(dve.tensor_scalar(tw[:, 2, :], tw[:, 1, :], 1.0, None, ALU.add))
            st.after()
            st.did(dve.reciprocal(tw[:, 0, :], tw[:, 2, :]))
            st.after()
            st.did(dve.tensor_tensor(tw[:, 1, :], tw[:, 1, :], tw[:, 0, :], ALU.mult))
            io = iota_e[:, :].unsqueeze(1).to_broadcast([P, NT, NE])
            dve.wait_ge(s_const, 1)
            for j, dst in ((0, ge), (1, ge2)):
                st.after()
                st.did(dve.tensor_tensor(dst[:, :, :], io, topf[:, :, j:j + 1].to_broadcast([P, NT, NE]), ALU.is_equal))
                st.after()
                st.did(dve.tensor_tensor(dst[:, :, :], dst[:, :, :], tw[:, j, :].unsqueeze(2).to_broadcast([P, NT, NE]),
                                         ALU.mult))
            st.after()
            st.did(dve.tensor_tensor(ge[:, :, :], ge[:, :, :], ge2[:, :, :], ALU.add))
            st.after()
            rest = ge
            for k in range(3):
                gk = g3[:, :, 32 * k:32 * k + NE]
                st.did(dve.tensor_copy(gk, rest[:, :, :]))
                st.after()
                if k < 2:
                    st.did(dve.tensor_tensor(ge2[:, :, :], rest[:, :, :], gk, ALU.subtract))
                    st.after()
                rest = ge2
            dve.sem_inc(s_g, 1)
            for c in range(NCH):
                dve.wait_ge(s_xh, c + 1)
                dve.tensor_tensor(x1[E:P, c * BANK:(c + 1) * BANK], ps[0:E, c, :],
                                  x1[0:E, c * BANK:(c + 1) * BANK].bitcast(F32), ALU.subtract).then_inc(s_xl, 1)
            for c in range(NCH):
                dve.wait_ge(s_gt, c + 1)
                dve.tensor_copy(bc[:, c * BANK:(c + 1) * BANK], ps[0:96, c, :]).then_inc(s_gp, 1)

            def hidden_lo(c, w, first):
                dve.wait_ge(s_hh, c * NE + w + 1 + SEED)
                if w >= HR or not first:
                    dve.wait_ge(s_m2, c * NE + w - HR + 1 + SEED)
                dve.tensor_tensor(hp[:, 1, w % HR, :], hg[:, w % 4, :], hp[:, 0, w % HR, :].bitcast(F32),
                                  ALU.subtract).then_inc(s_hld, 1)

            def add_chunk(c):
                dve.wait_ge(s_ytp, c + 1 + SEED)
                xv = xn[:, bass.ds(c * TPC, TPC), :]
                dve.tensor_tensor(xv, xv, ps[:, 5, 0:TPC * E].rearrange("p (r e) -> p r e", e=E), ALU.add)\
                   .then_inc(s_ya, 1)

            def chunk(c, before, first):
                for e in range(NE):
                    dve.wait_ge(s_gb, c * NE + e + 1)
                    dve.wait_ge(s_rl, c * NE + e + 1 + SEED)
                    if e >= 4 or not first:
                        dve.wait_ge(s_hh, c * NE + e - 3 + SEED)
                        dve.wait_ge(s_hlp if e % 2 else s_hld, c * (NE // 2) + (e - 4) // 2 + 1)
                    dve.tensor_tensor(hg[:, e % 4, :], hr[:, e % 2, :], ps[:, 2 + e % 2, :], ALU.mult).then_inc(s_hg, 1)
                    if e % 2 == 0 and e:
                        hidden_lo(c, e - 2, first)
                    elif e == 0 and not first:
                        hidden_lo(before, NE - 2, False)
                    if e == LAG + 2 and not first:
                        add_chunk(before)

            chunk(0, None, True)
            with dve.Fori(0, NCH - 1) as i:
                chunk(i + 1, i, False)
            hidden_lo(NCH - 1, NE - 2, False)
            add_chunk(NCH - 1)
            dve.wait_ge(s_ya, NCH + SEED)
            layernorm(xn, xn, 8)
            dve.wait_ge(s_we, N_WE)
            st.after()
            st.did(dve.tensor_tensor(xn[:, :, :], xn[:, :, :], gamb[:, :].unsqueeze(1).to_broadcast([P, NT, E]), ALU.mult))
            st.did(dve.tensor_tensor(h3[:, :, :], h3[:, :, :], betb[:, :].unsqueeze(1).to_broadcast([P, NT, E]), ALU.add))
            st.after()
            dve.tensor_tensor(xn[:, :, :], xn[:, :, :], h3[:, :, :], ALU.add).then_inc(s_fin, 1)


_INS = ['x', 'L0_tok_ple_table', 'L0_attn_ln_gamma', 'L0_attn_ln_beta', 'L0_attn_in_proj_w', 'L0_attn_conv_w',
        'L0_attn_conv_b', 'L0_attn_x_proj_w', 'L0_attn_dt_proj_w', 'L0_attn_dt_proj_b', 'L0_attn_A_log', 'L0_attn_D',
        'L0_attn_out_proj_w', 'L0_attn_gate_w', 'L0_attn_gate_b', 'L0_ffn_w1s', 'L0_ffn_b1s', 'L0_ffn_w2s',
        'L0_ffn_b2s', 'L1_attn_Wq', 'L1_attn_bq', 'L1_attn_Wk', 'L1_attn_bk', 'L1_attn_Wv', 'L1_attn_bv',
        'L1_attn_Wu', 'L1_attn_bu', 'L1_ffn_gate_w', 'L1_ffn_gate_b', 'L1_ffn_w1', 'L1_ffn_b1', 'L1_ffn_w2',
        'L1_ffn_b2', 'L1_ffn_gamma', 'L1_ffn_beta']


def kernel(**inputs):
    import numpy as _np
    import concourse.bacc as _bacc
    from concourse import mybir as _mybir
    from concourse.bass_utils import run_bass_kernel_spmd as _run

    nc = _bacc.Bacc("TRN2", target_bir_lowering=False, num_devices=1)
    arrays, args = {}, {}
    for name in _INS:
        v = _np.ascontiguousarray(inputs[name])
        arrays[f"in_{name}"] = v
        args[name] = nc.dram_tensor(f"in_{name}", v.shape, _mybir.dt.from_np(v.dtype), kind="ExternalInput").ap()
    t = inputs["x"].shape[1]
    d = inputs["L0_attn_gate_w"].shape[0]
    out = nc.dram_tensor("out_h", (1, t, d), _mybir.dt.float32, kind="ExternalOutput").ap()
    tower_kernel(nc, args, out)
    r = _run(nc, [arrays], core_ids=[0])
    return r.results[0]["out_h"]
```
